# Optimizing a Trainium2 kernel written in Bass

```python
import numpy as np
import jax
import jax.numpy as jnp

def _softmax(x, axis=-1):
    return jax.nn.softmax(x, axis=axis)

def _gelu(x):
    return jax.nn.gelu(x, approximate=True)

def _silu(x):
    return jax.nn.silu(x)

def _sigmoid(x):
    return jax.nn.sigmoid(x)

def _layernorm(x, axis=-1, eps=1e-05):
    m = jnp.mean(x, axis=axis, keepdims=True)
    v = jnp.var(x, axis=axis, keepdims=True)
    return (x - m) / jnp.sqrt(v + eps)

def _scatter_add(tgt, idx, src, axis=0):
    return tgt.at[idx].add(src)

def _segment_sum(src, seg, n):
    return jax.ops.segment_sum(src, seg, n)
kernel_name = 'mk_flamingo_gated_d4_seqx_r4_9761d4'

def setup_inputs(seed: int=0):
    np.random.seed(seed)
    _w = jnp.asarray

    def _rec_inputs():
        import jax
        import jax.numpy as jnp
        _rk = jax.random.key(seed)
        x = 7.22e-05 + 1 * jax.random.normal(jax.random.fold_in(_rk, 1), (4, 512, 256), jnp.float32)
        _lenS = 512 - jax.random.randint(jax.random.fold_in(_rk, 7), (4,), 0, max(1, 512 // 4) + 1, jnp.int32)
        _lenS2 = 512 - jax.random.randint(jax.random.fold_in(_rk, 8), (4,), 0, max(1, 512 // 4) + 1, jnp.int32)
        _ctx_1024P = jax.random.normal(jax.random.fold_in(_rk, 11), (4, 16, 256), jnp.float32)
        _ctx_1024c = jax.random.dirichlet(jax.random.fold_in(_rk, 511), 0.3 * jnp.ones((16,), jnp.float32), (4, 512))
        _ctx_1024t = jnp.einsum('bsk,bkd->bsd', _ctx_1024c, _ctx_1024P)
        _ctx_1024t = _ctx_1024t * jax.lax.rsqrt(jnp.mean(jnp.square(_ctx_1024t)) + 1e-12) * 0.953939
        ctx_1024 = 4.13588e-05 + 0.999923 * (_ctx_1024t + 0.3 * jax.random.normal(jax.random.fold_in(_rk, 611), (4, 512, 256), jnp.float32))
        _validS = jnp.arange(512)[None, :] < _lenS[:, None]
        _validS2 = jnp.arange(512)[None, :] < _lenS2[:, None]
        _causal = jnp.tril(jnp.ones((512, 512), dtype=bool))
        mask_SxS2_bk1 = jnp.broadcast_to(_validS2[0:1, :], (512, 512))
        mask_Bx1xSxS2_ik1 = jnp.where(jnp.broadcast_to(_validS2[:, None, None, :], (4, 1, 512, 512)), 1, 0).astype(jnp.int32)
        _g = jax.random.normal(jax.random.fold_in(_rk, 9001), (2, 4), jnp.float32)
        _g = jnp.sign(_g) * jnp.maximum(jnp.abs(_g), 1.0) + (_g == 0) * 1.0
        g_xattn = _g[0]
        g_ffn = _g[1]
        return (x, ctx_1024, mask_SxS2_bk1, mask_Bx1xSxS2_ik1, g_xattn, g_ffn)
    x, ctx_1024, mask_SxS2_bk1, mask_Bx1xSxS2_ik1, g_xattn, g_ffn = _rec_inputs()

    def _L0_xattn_setup():
        import jax, jax.numpy as jnp
        import numpy as np
        D = 256
        H = 16
        HD = D // H
        SCALE = 1.0 / np.sqrt(HD)

        def _split_heads(x):
            B, S, _ = x.shape
            return x.reshape(B, S, H, HD).transpose(0, 2, 1, 3)
        key = jax.random.key(seed)
        ks = jax.random.split(key, 12)
        B, S = (4, 512)
        inp = {'queries': jax.random.normal(ks[0], (B, S, D), jnp.float32), 'keys': jax.random.normal(ks[1], (B, S, D), jnp.float32), 'values': jax.random.normal(ks[2], (B, S, D), jnp.float32), 'mask': jax.random.randint(ks[3], (S, S), 0, 2).astype(bool), 'Wq': jax.random.normal(ks[4], (D, D), jnp.float32) * 0.02, 'bq': jax.random.normal(ks[5], (D,), jnp.float32) * 0.02, 'Wk': jax.random.normal(ks[6], (D, D), jnp.float32) * 0.02, 'bk': jax.random.normal(ks[7], (D,), jnp.float32) * 0.02, 'Wv': jax.random.normal(ks[8], (D, D), jnp.float32) * 0.02, 'bv': jax.random.normal(ks[9], (D,), jnp.float32) * 0.02, 'Wo': jax.random.normal(ks[10], (D, D), jnp.float32) * 0.02, 'bo': jax.random.normal(ks[11], (D,), jnp.float32) * 0.02}
        return inp
    _L0_xattn_all = _L0_xattn_setup()
    _L0_xattn_in = {k: v for k, v in _L0_xattn_all.items() if k in ('Wq', 'bq', 'Wk', 'bk', 'Wv', 'bv', 'Wo', 'bo')}
    del _L0_xattn_all

    def _L0_ffn_setup():
        import jax, jax.numpy as jnp
        import numpy as np
        HIDDEN = 256
        NUM_EXPERTS = 16
        TOP_K = 6
        EPS = 1e-10
        key = jax.random.key(seed)
        k1, k2, k3, k4 = jax.random.split(key, 4)
        tokens = jax.random.normal(k1, (4, 512, HIDDEN), dtype=jnp.float32)
        bound = 1.0 / np.sqrt(HIDDEN)
        router_w = jax.random.uniform(k2, (NUM_EXPERTS, HIDDEN), jnp.float32, -bound, bound)
        router_b = jax.random.uniform(k3, (NUM_EXPERTS,), jnp.float32, -bound, bound)
        expert_w = jax.random.normal(k4, (NUM_EXPERTS, HIDDEN, HIDDEN), dtype=jnp.float32) / np.sqrt(HIDDEN)
        return {'tokens': tokens, 'router_w': router_w, 'router_b': router_b, 'expert_w': expert_w}
    _L0_ffn_all = _L0_ffn_setup()
    _L0_ffn_in = {k: v for k, v in _L0_ffn_all.items() if k in ('router_w', 'router_b', 'expert_w')}
    del _L0_ffn_all

    def _L1_xattn_setup():
        import jax, jax.numpy as jnp
        import numpy as np
        N, L, D_EMBED, H = (2, 512, 256, 16)
        DH = D_EMBED // H
        key = jax.random.key(seed)
        ks = jax.random.split(key, 9)
        s = 1.0 / np.sqrt(DH)
        return {'values': jax.random.normal(ks[0], (N, L, D_EMBED), jnp.float32), 'keys': jax.random.normal(ks[1], (N, L, D_EMBED), jnp.float32), 'query': jax.random.normal(ks[2], (N, L, D_EMBED), jnp.float32), 'mask': jax.random.randint(ks[3], (N, 1, L, L), 0, 2, jnp.int32), 'Wv': jax.random.normal(ks[4], (DH, DH), jnp.float32) * s, 'Wk': jax.random.normal(ks[5], (DH, DH), jnp.float32) * s, 'Wq': jax.random.normal(ks[6], (DH, DH), jnp.float32) * s, 'Wo': jax.random.normal(ks[7], (D_EMBED, D_EMBED), jnp.float32) * (1.0 / np.sqrt(D_EMBED)), 'bo': jax.random.normal(ks[8], (D_EMBED,), jnp.float32) * 0.01}
    _L1_xattn_all = _L1_xattn_setup()
    _L1_xattn_in = {k: v for k, v in _L1_xattn_all.items() if k in ('Wv', 'Wk', 'Wq', 'Wo', 'bo')}
    del _L1_xattn_all

    def _L1_ffn_setup():
        import jax, jax.numpy as jnp
        import numpy as np
        NH, NKV, E, K = (16, 4, 8, 2)
        CAP_FACTOR = 1.25
        LN_EPS = 1e-05

        def _layer_norm(x, w, b):
            mu = jnp.mean(x, axis=-1, keepdims=True)
            var = jnp.mean(jnp.square(x - mu), axis=-1, keepdims=True)
            return (x - mu) * jax.lax.rsqrt(var + LN_EPS) * w + b
        key = jax.random.key(seed)
        ks = jax.random.split(key, 6)
        S, B, H, F = (512, 1, 256, 512)
        HD = H // NH
        qkv_out = NKV * (NH // NKV + 2) * HD
        f32 = jnp.float32
        return {'hidden_states': jax.random.normal(ks[0], (S, B, H), f32), 'ln1_weight': jnp.ones((H,), f32), 'ln1_bias': jnp.zeros((H,), f32), 'ln2_weight': jnp.ones((H,), f32), 'ln2_bias': jnp.zeros((H,), f32), 'qkv_weight': jax.random.normal(ks[1], (qkv_out, H), f32) * 0.02, 'proj_weight': jax.random.normal(ks[2], (H, H), f32) * 0.02, 'router_weight': jax.random.normal(ks[3], (H, E), f32) * 0.02, 'moe_w1': jax.random.normal(ks[4], (E, H, F), f32) * 0.02, 'moe_w2': jax.random.normal(ks[5], (F and E, F, H), f32)[:E] * 0.02 if False else jax.random.normal(ks[5], (E, F, H), f32) * 0.02}
    _L1_ffn_all = _L1_ffn_setup()
    _L1_ffn_in = {k: v for k, v in _L1_ffn_all.items() if k in ('ln1_weight', 'ln1_bias', 'ln2_weight', 'ln2_bias', 'qkv_weight', 'proj_weight', 'router_weight', 'moe_w1', 'moe_w2')}
    del _L1_ffn_all

    def _L2_xattn_setup():
        import jax, jax.numpy as jnp
        import numpy as np
        import math
        B, SQ, SK, DQ, DK = (16, 512, 512, 256, 256)
        key = jax.random.key(seed)
        ks = jax.random.split(key, 6)
        return {'bert_feature': jax.random.normal(ks[0], (B, SQ, DQ), dtype=jnp.float32), 'knowledge_feature': jax.random.normal(ks[1], (B, SK, DK), dtype=jnp.float32), 'w1_w': jax.random.normal(ks[2], (DK, DQ), dtype=jnp.float32) * 0.02, 'w1_b': jax.random.normal(ks[3], (DK,), dtype=jnp.float32) * 0.02, 'w2_w': jax.random.normal(ks[4], (DQ, DQ + DK), dtype=jnp.float32) * 0.02, 'w2_b': jax.random.normal(ks[5], (DQ,), dtype=jnp.float32) * 0.02}
    _L2_xattn_all = _L2_xattn_setup()
    _L2_xattn_in = {k: v for k, v in _L2_xattn_all.items() if k in ('w1_w', 'w1_b', 'w2_w', 'w2_b')}
    del _L2_xattn_all

    def _L2_ffn_setup():
        import jax, jax.numpy as jnp
        import numpy as np
        DIM = 256
        HIDDEN = 1024
        N_EXPERTS = 8
        K = 2
        TEMP = 1.0

        def _expert_ffn(xf, wa, ba, wb, bb):
            h = xf @ wa.T + ba
            h1, h2 = jnp.split(h, 2, axis=-1)
            h = jax.nn.silu(h1) * h2
            return h @ wb.T + bb
        key = jax.random.key(seed)
        ks = jax.random.split(key, 7)
        s = 0.02
        x = jax.random.normal(ks[0], (4, 512, DIM), dtype=jnp.float32)
        router_w = jax.random.normal(ks[1], (N_EXPERTS, DIM), dtype=jnp.float32) * s
        router_b = jnp.zeros((N_EXPERTS,), dtype=jnp.float32)
        w1 = jax.random.normal(ks[2], (N_EXPERTS, 2 * HIDDEN, DIM), dtype=jnp.float32) * s
        b1 = jnp.zeros((N_EXPERTS, 2 * HIDDEN), dtype=jnp.float32)
        w2 = jax.random.normal(ks[3], (N_EXPERTS, DIM, HIDDEN), dtype=jnp.float32) * s
        b2 = jnp.zeros((N_EXPERTS, DIM), dtype=jnp.float32)
        return {'x': x, 'router_w': router_w, 'router_b': router_b, 'w1': w1, 'b1': b1, 'w2': w2, 'b2': b2}
    _L2_ffn_all = _L2_ffn_setup()
    _L2_ffn_in = {k: v for k, v in _L2_ffn_all.items() if k in ('router_w', 'router_b', 'w1', 'b1', 'w2', 'b2')}
    del _L2_ffn_all

    def _L3_xattn_setup():
        import jax, jax.numpy as jnp
        import numpy as np
        EMBED_DIM = 256
        NUM_HEADS = 16
        PROJ_DIM = EMBED_DIM // NUM_HEADS

        def _split_heads(x, B):
            return x.reshape(B, -1, NUM_HEADS, PROJ_DIM).transpose(0, 2, 1, 3)
        key = jax.random.key(seed)
        ks = jax.random.split(key, 11)
        B, S, D = (2, 512, EMBED_DIM)
        scale = 1.0 / np.sqrt(D)
        inp = {'q': jax.random.normal(ks[0], (B, S, D), jnp.float32), 'k': jax.random.normal(ks[1], (B, S, D), jnp.float32), 'v': jax.random.normal(ks[2], (B, S, D), jnp.float32), 'Wq': jax.random.normal(ks[3], (D, D), jnp.float32) * scale, 'bq': jnp.zeros((D,), jnp.float32), 'Wk': jax.random.normal(ks[4], (D, D), jnp.float32) * scale, 'bk': jnp.zeros((D,), jnp.float32), 'Wv': jax.random.normal(ks[5], (D, D), jnp.float32) * scale, 'bv': jnp.zeros((D,), jnp.float32), 'Wo': jax.random.normal(ks[6], (D, D), jnp.float32) * scale, 'bo': jnp.zeros((D,), jnp.float32), 'use_causal_mask': 1}
        return inp
    _L3_xattn_all = _L3_xattn_setup()
    _L3_xattn_in = {k: v for k, v in _L3_xattn_all.items() if k in ('Wq', 'bq', 'Wk', 'bk', 'Wv', 'bv', 'Wo', 'bo')}
    del _L3_xattn_all

    def _L3_ffn_setup():
        import jax, jax.numpy as jnp
        import numpy as np
        LATENT = 256
        LEAF_W = 64
        DEPTH = 4
        N_LEAVES = 2 ** DEPTH
        N_NODES = 2 ** DEPTH - 1
        B, S = (4, 512)

        def _fff_params(key, prefix):
            ks = jax.random.split(key, 4)
            d, h, l, n = (LATENT, LEAF_W, N_LEAVES, N_NODES)
            s_in = 1.0 / np.sqrt(d).astype(np.float32)
            s_h = 1.0 / np.sqrt(h).astype(np.float32)
            return {f'{prefix}_node_w': jax.random.normal(ks[0], (n, d), jnp.float32) * s_in, f'{prefix}_node_b': jax.random.normal(ks[1], (n,), jnp.float32) * s_in, f'{prefix}_w1': jax.random.normal(ks[2], (l, d, h), jnp.float32) * s_in, f'{prefix}_b1': jnp.zeros((l, h), jnp.float32), f'{prefix}_w2': jax.random.normal(ks[3], (l, h, d), jnp.float32) * s_h, f'{prefix}_b2': jnp.zeros((l, d), jnp.float32)}

        def _fff(x, node_w, node_b, w1, b1, w2, b2):
            Bx, Sx, D = x.shape
            xf = x.reshape(-1, D)
            N = xf.shape[0]
            cur = jnp.zeros((N,), jnp.int32)
            for _ in range(DEPTH):
                pw = node_w[cur]
                score = jnp.einsum('nd,nd->n', xf, pw) + node_b[cur]
                cur = 2 * cur + 1 + (score >= 0).astype(jnp.int32)
            leaf = cur - N_NODES
            sel = jax.nn.one_hot(leaf, N_LEAVES, dtype=xf.dtype)
            hidden_all = jax.nn.relu(jnp.einsum('nd,ldh->lnh', xf, w1) + b1[:, None, :])
            hidden = hidden_all * sel.T[:, :, None]
            out = jnp.einsum('lnh,lho->no', hidden, w2) + sel @ b2
            return out.reshape(Bx, Sx, D)
        key = jax.random.key(seed)
        kx, kq, kk, kv = jax.random.split(key, 4)
        inp = {'x': jax.random.normal(kx, (B, S, LATENT), jnp.float32)}
        inp.update(_fff_params(kq, 'q'))
        inp.update(_fff_params(kk, 'k'))
        inp.update(_fff_params(kv, 'v'))
        return inp
    _L3_ffn_all = _L3_ffn_setup()
    _L3_ffn_in = {k: v for k, v in _L3_ffn_all.items() if k in ('q_node_w', 'q_node_b', 'q_w1', 'q_b1', 'q_w2', 'q_b2', 'k_node_w', 'k_node_b', 'k_w1', 'k_b1', 'k_w2', 'k_b2', 'v_node_w', 'v_node_b', 'v_w1', 'v_b1', 'v_w2', 'v_b2')}
    del _L3_ffn_all
    return {'x': x, 'ctx_1024': ctx_1024, 'mask_SxS2_bk1': mask_SxS2_bk1, 'mask_Bx1xSxS2_ik1': mask_Bx1xSxS2_ik1, 'g_xattn': g_xattn, 'g_ffn': g_ffn, 'L0_xattn_Wq': _L0_xattn_in['Wq'], 'L0_xattn_bq': _L0_xattn_in['bq'], 'L0_xattn_Wk': _L0_xattn_in['Wk'], 'L0_xattn_bk': _L0_xattn_in['bk'], 'L0_xattn_Wv': _L0_xattn_in['Wv'], 'L0_xattn_bv': _L0_xattn_in['bv'], 'L0_xattn_Wo': _L0_xattn_in['Wo'], 'L0_xattn_bo': _L0_xattn_in['bo'], 'L0_ffn_router_w': _L0_ffn_in['router_w'], 'L0_ffn_router_b': _L0_ffn_in['router_b'], 'L0_ffn_expert_w': _L0_ffn_in['expert_w'], 'L1_xattn_Wv': _L1_xattn_in['Wv'], 'L1_xattn_Wk': _L1_xattn_in['Wk'], 'L1_xattn_Wq': _L1_xattn_in['Wq'], 'L1_xattn_Wo': _L1_xattn_in['Wo'], 'L1_xattn_bo': _L1_xattn_in['bo'], 'L1_ffn_ln1_weight': _L1_ffn_in['ln1_weight'], 'L1_ffn_ln1_bias': _L1_ffn_in['ln1_bias'], 'L1_ffn_ln2_weight': _L1_ffn_in['ln2_weight'], 'L1_ffn_ln2_bias': _L1_ffn_in['ln2_bias'], 'L1_ffn_qkv_weight': _L1_ffn_in['qkv_weight'], 'L1_ffn_proj_weight': _L1_ffn_in['proj_weight'], 'L1_ffn_router_weight': _L1_ffn_in['router_weight'], 'L1_ffn_moe_w1': _L1_ffn_in['moe_w1'], 'L1_ffn_moe_w2': _L1_ffn_in['moe_w2'], 'L2_xattn_w1_w': _L2_xattn_in['w1_w'], 'L2_xattn_w1_b': _L2_xattn_in['w1_b'], 'L2_xattn_w2_w': _L2_xattn_in['w2_w'], 'L2_xattn_w2_b': _L2_xattn_in['w2_b'], 'L2_ffn_router_w': _L2_ffn_in['router_w'], 'L2_ffn_router_b': _L2_ffn_in['router_b'], 'L2_ffn_w1': _L2_ffn_in['w1'], 'L2_ffn_b1': _L2_ffn_in['b1'], 'L2_ffn_w2': _L2_ffn_in['w2'], 'L2_ffn_b2': _L2_ffn_in['b2'], 'L3_xattn_Wq': _L3_xattn_in['Wq'], 'L3_xattn_bq': _L3_xattn_in['bq'], 'L3_xattn_Wk': _L3_xattn_in['Wk'], 'L3_xattn_bk': _L3_xattn_in['bk'], 'L3_xattn_Wv': _L3_xattn_in['Wv'], 'L3_xattn_bv': _L3_xattn_in['bv'], 'L3_xattn_Wo': _L3_xattn_in['Wo'], 'L3_xattn_bo': _L3_xattn_in['bo'], 'L3_ffn_q_node_w': _L3_ffn_in['q_node_w'], 'L3_ffn_q_node_b': _L3_ffn_in['q_node_b'], 'L3_ffn_q_w1': _L3_ffn_in['q_w1'], 'L3_ffn_q_b1': _L3_ffn_in['q_b1'], 'L3_ffn_q_w2': _L3_ffn_in['q_w2'], 'L3_ffn_q_b2': _L3_ffn_in['q_b2'], 'L3_ffn_k_node_w': _L3_ffn_in['k_node_w'], 'L3_ffn_k_node_b': _L3_ffn_in['k_node_b'], 'L3_ffn_k_w1': _L3_ffn_in['k_w1'], 'L3_ffn_k_b1': _L3_ffn_in['k_b1'], 'L3_ffn_k_w2': _L3_ffn_in['k_w2'], 'L3_ffn_k_b2': _L3_ffn_in['k_b2'], 'L3_ffn_v_node_w': _L3_ffn_in['v_node_w'], 'L3_ffn_v_node_b': _L3_ffn_in['v_node_b'], 'L3_ffn_v_w1': _L3_ffn_in['v_w1'], 'L3_ffn_v_b1': _L3_ffn_in['v_b1'], 'L3_ffn_v_w2': _L3_ffn_in['v_w2'], 'L3_ffn_v_b2': _L3_ffn_in['v_b2']}

def reference(x, ctx_1024, mask_SxS2_bk1, mask_Bx1xSxS2_ik1, g_xattn, g_ffn, L0_xattn_Wq, L0_xattn_bq, L0_xattn_Wk, L0_xattn_bk, L0_xattn_Wv, L0_xattn_bv, L0_xattn_Wo, L0_xattn_bo, L0_ffn_router_w, L0_ffn_router_b, L0_ffn_expert_w, L1_xattn_Wv, L1_xattn_Wk, L1_xattn_Wq, L1_xattn_Wo, L1_xattn_bo, L1_ffn_ln1_weight, L1_ffn_ln1_bias, L1_ffn_ln2_weight, L1_ffn_ln2_bias, L1_ffn_qkv_weight, L1_ffn_proj_weight, L1_ffn_router_weight, L1_ffn_moe_w1, L1_ffn_moe_w2, L2_xattn_w1_w, L2_xattn_w1_b, L2_xattn_w2_w, L2_xattn_w2_b, L2_ffn_router_w, L2_ffn_router_b, L2_ffn_w1, L2_ffn_b1, L2_ffn_w2, L2_ffn_b2, L3_xattn_Wq, L3_xattn_bq, L3_xattn_Wk, L3_xattn_bk, L3_xattn_Wv, L3_xattn_bv, L3_xattn_Wo, L3_xattn_bo, L3_ffn_q_node_w, L3_ffn_q_node_b, L3_ffn_q_w1, L3_ffn_q_b1, L3_ffn_q_w2, L3_ffn_q_b2, L3_ffn_k_node_w, L3_ffn_k_node_b, L3_ffn_k_w1, L3_ffn_k_b1, L3_ffn_k_w2, L3_ffn_k_b2, L3_ffn_v_node_w, L3_ffn_v_node_b, L3_ffn_v_w1, L3_ffn_v_b1, L3_ffn_v_w2, L3_ffn_v_b2):
    import jax
    import jax.numpy as jnp

    def _L0_xattn_ref(queries, keys, values, mask, Wq, bq, Wk, bk, Wv, bv, Wo, bo):
        import jax, jax.numpy as jnp
        import numpy as np
        D = 256
        H = 16
        HD = D // H
        SCALE = 1.0 / np.sqrt(HD)

        def _split_heads(x):
            B, S, _ = x.shape
            return x.reshape(B, S, H, HD).transpose(0, 2, 1, 3)
        q = _split_heads(queries @ Wq + bq)
        k = _split_heads(keys @ Wk + bk)
        v = _split_heads(values @ Wv + bv)
        scores = jnp.einsum('bhqd,bhkd->bhqk', q, k) * SCALE
        neg = jnp.finfo(scores.dtype).min
        scores = jnp.where(mask[None, None, :, :], scores, neg)
        probs = jax.nn.softmax(scores, axis=-1)
        ctx = jnp.einsum('bhqk,bhkd->bhqd', probs, v)
        B, _, Sq, _ = ctx.shape
        combined = ctx.transpose(0, 2, 1, 3).reshape(B, Sq, D)
        return combined @ Wo + bo

    def _L0_ffn_ref(tokens, router_w, router_b, expert_w):
        import jax, jax.numpy as jnp
        import numpy as np
        HIDDEN = 256
        NUM_EXPERTS = 16
        TOP_K = 6
        EPS = 1e-10
        B, S, H = tokens.shape
        E = expert_w.shape[0]
        T = B * S
        logits = jnp.einsum('bsh,eh->bse', tokens, router_w) + router_b
        probs = jax.nn.softmax(logits, axis=-1)
        top_p, top_i = jax.lax.top_k(probs, TOP_K)
        top_p = top_p / (jnp.sum(top_p, axis=-1, keepdims=True) + EPS)
        x = tokens.reshape(T, H)
        flat_i = top_i.reshape(T, TOP_K)
        flat_p = top_p.reshape(T, TOP_K)
        gate = jnp.zeros((T, E), dtype=flat_p.dtype)
        gate = gate.at[jnp.arange(T)[:, None], flat_i].add(flat_p)
        acc = jnp.maximum(jnp.sum(gate, axis=-1), EPS)
        out = jnp.zeros_like(x)
        for e in range(E):
            out = out + x @ expert_w[e] * gate[:, e:e + 1]
        out = (out / acc[:, None]).reshape(B, S, H)
        out = out + EPS * jnp.sum(top_p, axis=-1, keepdims=True)
        return out

    def _L1_xattn_ref(values, keys, query, mask, Wv, Wk, Wq, Wo, bo):
        import jax, jax.numpy as jnp
        import numpy as np
        N, L, D_EMBED, H = (2, 512, 256, 16)
        DH = D_EMBED // H
        n, lq, d_embed = query.shape
        dh = Wv.shape[0]
        h = d_embed // dh
        v = values.reshape(n, -1, h, dh)
        k = keys.reshape(n, -1, h, dh)
        q = query.reshape(n, lq, h, dh)
        v = jnp.einsum('nlhd,ed->nlhe', v, Wv)
        k = jnp.einsum('nlhd,ed->nlhe', k, Wk)
        q = jnp.einsum('nlhd,ed->nlhe', q, Wq)
        energy = jnp.einsum('nqhd,nkhd->nhqk', q, k)
        energy = jnp.where(mask == 0, jnp.asarray(-1e+20, energy.dtype), energy)
        attn = jax.nn.softmax(energy / jnp.sqrt(jnp.asarray(d_embed, energy.dtype)), axis=3)
        out = jnp.einsum('nhqk,nkhd->nqhd', attn, v).reshape(n, lq, h * dh)
        return out @ Wo.T + bo

    def _L1_ffn_ref(hidden_states, ln1_weight, ln1_bias, ln2_weight, ln2_bias, qkv_weight, proj_weight, router_weight, moe_w1, moe_w2):
        import jax, jax.numpy as jnp
        import numpy as np
        NH, NKV, E, K = (16, 4, 8, 2)
        CAP_FACTOR = 1.25
        LN_EPS = 1e-05

        def _layer_norm(x, w, b):
            mu = jnp.mean(x, axis=-1, keepdims=True)
            var = jnp.mean(jnp.square(x - mu), axis=-1, keepdims=True)
            return (x - mu) * jax.lax.rsqrt(var + LN_EPS) * w + b
        S, B, H = hidden_states.shape
        HD = H // NH
        q_per_kv = NH // NKV
        ln1 = _layer_norm(hidden_states, ln1_weight, ln1_bias)
        qkv = jnp.einsum('sbh,oh->sbo', ln1, qkv_weight)
        qkv = qkv.reshape(S, B, NKV, (q_per_kv + 2) * HD)
        q = qkv[..., :q_per_kv * HD].reshape(S, B, NH, HD)
        k = qkv[..., q_per_kv * HD:(q_per_kv + 1) * HD]
        v = qkv[..., (q_per_kv + 1) * HD:]
        qb = jnp.transpose(q, (1, 2, 0, 3)).reshape(B, NKV, q_per_kv, S, HD)
        kb = jnp.transpose(k, (1, 2, 0, 3))
        vb = jnp.transpose(v, (1, 2, 0, 3))
        scale = 1.0 / np.sqrt(HD).astype(np.float32)
        scores = jnp.einsum('bgqsd,bgtd->bgqst', qb, kb) * scale
        causal = jnp.tril(jnp.ones((S, S), bool))
        scores = jnp.where(causal, scores, jnp.finfo(scores.dtype).min)
        attn = jax.nn.softmax(scores, axis=-1)
        ao = jnp.einsum('bgqst,bgtd->bgqsd', attn, vb)
        ao = ao.reshape(B, NH, S, HD)
        ao = jnp.transpose(ao, (2, 0, 1, 3)).reshape(S, B, H)
        proj = jnp.einsum('sbh,oh->sbo', ao, proj_weight)
        h1 = hidden_states + proj
        ln2 = _layer_norm(h1, ln2_weight, ln2_bias)
        x = ln2.reshape(-1, H)
        N = x.shape[0]
        logits = x @ router_weight
        probs = jax.nn.softmax(logits, axis=-1)
        top_p, top_i = jax.lax.top_k(probs, K)
        top_p = top_p / jnp.sum(top_p, axis=-1, keepdims=True)
        exp_idx = top_i.reshape(-1)
        exp_p = top_p.reshape(-1)
        order = jnp.argsort(exp_idx, stable=True)
        sorted_exp = exp_idx[order]
        counts = jnp.bincount(exp_idx, length=E)
        offsets = jnp.concatenate([jnp.zeros((1,), counts.dtype), jnp.cumsum(counts)[:-1]])
        within = jnp.arange(N * K) - offsets[sorted_exp]
        cap = int(np.ceil(N * K / E * CAP_FACTOR))
        T = E * cap
        valid = within < cap
        dst = jnp.where(valid, sorted_exp * cap + within, T)
        padded_tokens = jnp.zeros((T, H), x.dtype).at[dst].set(x[order // K], mode='drop')
        padded_probs = jnp.zeros((T,), exp_p.dtype).at[dst].set(exp_p[order], mode='drop')
        padded_tid = jnp.zeros((T,), jnp.int32).at[dst].set((order // K).astype(jnp.int32), mode='drop')
        xt = padded_tokens.reshape(E, cap, H)
        fc1 = jax.nn.gelu(jnp.einsum('ech,ehf->ecf', xt, moe_w1))
        fc2 = jnp.einsum('ecf,efh->ech', fc1, moe_w2).reshape(T, H)
        weighted = fc2 * padded_probs[:, None]
        moe_out = jnp.zeros((N, H), hidden_states.dtype).at[padded_tid].add(weighted)
        return h1 + moe_out.reshape(S, B, H)

    def _L2_xattn_ref(bert_feature, knowledge_feature, w1_w, w1_b, w2_w, w2_b):
        import jax, jax.numpy as jnp
        import numpy as np
        import math
        B, SQ, SK, DQ, DK = (16, 512, 512, 256, 256)
        d_k = knowledge_feature.shape[-1]
        bf = jnp.einsum('bqd,kd->bqk', bert_feature, w1_w) + w1_b
        scores = jnp.einsum('bqd,bkd->bqk', bf, knowledge_feature) / math.sqrt(d_k)
        attn = jax.nn.softmax(scores, axis=-1)
        output = jnp.einsum('bqk,bkd->bqd', attn, knowledge_feature)
        fused = jnp.concatenate([bert_feature, output], axis=-1)
        return jnp.einsum('bqf,of->bqo', fused, w2_w) + w2_b

    def _L2_ffn_ref(x, router_w, router_b, w1, b1, w2, b2):
        import jax, jax.numpy as jnp
        import numpy as np
        DIM = 256
        HIDDEN = 1024
        N_EXPERTS = 8
        K = 2
        TEMP = 1.0

        def _expert_ffn(xf, wa, ba, wb, bb):
            h = xf @ wa.T + ba
            h1, h2 = jnp.split(h, 2, axis=-1)
            h = jax.nn.silu(h1) * h2
            return h @ wb.T + bb
        b, t, d = x.shape
        logits = (x @ router_w.T + router_b) / TEMP
        topk_val, topk_idx = jax.lax.top_k(logits, K)
        weights = jax.nn.softmax(topk_val, axis=-1)
        xf = x.reshape(-1, d)
        outs = jax.vmap(_expert_ffn, in_axes=(None, 0, 0, 0, 0))(xf, w1, b1, w2, b2)
        outs = jnp.transpose(outs, (1, 0, 2))
        idx = topk_idx.reshape(-1, K)
        gathered = jnp.take_along_axis(outs, idx[:, :, None], axis=1)
        combined = (gathered * weights.reshape(-1, K, 1)).sum(axis=1)
        return combined.reshape(b, t, d)

    def _L3_xattn_ref(q, k, v, Wq, bq, Wk, bk, Wv, bv, Wo, bo, use_causal_mask):
        import jax, jax.numpy as jnp
        import numpy as np
        EMBED_DIM = 256
        NUM_HEADS = 16
        PROJ_DIM = EMBED_DIM // NUM_HEADS

        def _split_heads(x, B):
            return x.reshape(B, -1, NUM_HEADS, PROJ_DIM).transpose(0, 2, 1, 3)
        B, S, D = q.shape
        qh = _split_heads(q @ Wq + bq, B)
        kh = _split_heads(k @ Wk + bk, B)
        vh = _split_heads(v @ Wv + bv, B)
        logits = jnp.einsum('bhqd,bhkd->bhqk', qh, kh) / jnp.sqrt(jnp.asarray(PROJ_DIM, jnp.float32))
        if use_causal_mask:
            tril = jnp.tril(jnp.ones((S, S), dtype=logits.dtype))
            logits = logits + jnp.log(tril * 1e-09 + 1e-09)
        attn = jax.nn.softmax(logits, axis=-1)
        out = jnp.einsum('bhqk,bhkd->bhqd', attn, vh)
        out = out.transpose(0, 2, 1, 3).reshape(B, S, D)
        return out @ Wo + bo

    def _L3_ffn_ref(x, q_node_w, q_node_b, q_w1, q_b1, q_w2, q_b2, k_node_w, k_node_b, k_w1, k_b1, k_w2, k_b2, v_node_w, v_node_b, v_w1, v_b1, v_w2, v_b2):
        import jax, jax.numpy as jnp
        import numpy as np
        LATENT = 256
        LEAF_W = 64
        DEPTH = 4
        N_LEAVES = 2 ** DEPTH
        N_NODES = 2 ** DEPTH - 1
        B, S = (4, 512)

        def _fff_params(key, prefix):
            ks = jax.random.split(key, 4)
            d, h, l, n = (LATENT, LEAF_W, N_LEAVES, N_NODES)
            s_in = 1.0 / np.sqrt(d).astype(np.float32)
            s_h = 1.0 / np.sqrt(h).astype(np.float32)
            return {f'{prefix}_node_w': jax.random.normal(ks[0], (n, d), jnp.float32) * s_in, f'{prefix}_node_b': jax.random.normal(ks[1], (n,), jnp.float32) * s_in, f'{prefix}_w1': jax.random.normal(ks[2], (l, d, h), jnp.float32) * s_in, f'{prefix}_b1': jnp.zeros((l, h), jnp.float32), f'{prefix}_w2': jax.random.normal(ks[3], (l, h, d), jnp.float32) * s_h, f'{prefix}_b2': jnp.zeros((l, d), jnp.float32)}

        def _fff(x, node_w, node_b, w1, b1, w2, b2):
            Bx, Sx, D = x.shape
            xf = x.reshape(-1, D)
            N = xf.shape[0]
            cur = jnp.zeros((N,), jnp.int32)
            for _ in range(DEPTH):
                pw = node_w[cur]
                score = jnp.einsum('nd,nd->n', xf, pw) + node_b[cur]
                cur = 2 * cur + 1 + (score >= 0).astype(jnp.int32)
            leaf = cur - N_NODES
            sel = jax.nn.one_hot(leaf, N_LEAVES, dtype=xf.dtype)
            hidden_all = jax.nn.relu(jnp.einsum('nd,ldh->lnh', xf, w1) + b1[:, None, :])
            hidden = hidden_all * sel.T[:, :, None]
            out = jnp.einsum('lnh,lho->no', hidden, w2) + sel @ b2
            return out.reshape(Bx, Sx, D)
        q = _fff(x, q_node_w, q_node_b, q_w1, q_b1, q_w2, q_b2)
        k = _fff(x, k_node_w, k_node_b, k_w1, k_b1, k_w2, k_b2)
        v = _fff(x, v_node_w, v_node_b, v_w1, v_b1, v_w2, v_b2)
        scale = 1.0 / np.sqrt(LATENT).astype(np.float32)
        attn = jax.nn.softmax(jnp.einsum('bqd,bkd->bqk', q, k) * scale, axis=-1)
        return jnp.einsum('bqk,bkd->bqd', attn, v)
    x = x + jnp.tanh(g_xattn[0]) * _L0_xattn_ref(_layernorm(x, axis=-1), ctx_1024, ctx_1024, mask_SxS2_bk1, L0_xattn_Wq, L0_xattn_bq, L0_xattn_Wk, L0_xattn_bk, L0_xattn_Wv, L0_xattn_bv, L0_xattn_Wo, L0_xattn_bo)
    x = x + jnp.tanh(g_ffn[0]) * _L0_ffn_ref(_layernorm(x, axis=-1), L0_ffn_router_w, L0_ffn_router_b, L0_ffn_expert_w)
    x = x + jnp.tanh(g_xattn[1]) * _L1_xattn_ref(ctx_1024, ctx_1024, _layernorm(x, axis=-1), mask_Bx1xSxS2_ik1, L1_xattn_Wv, L1_xattn_Wk, L1_xattn_Wq, L1_xattn_Wo, L1_xattn_bo)
    x = x + jnp.tanh(g_ffn[1]) * _L1_ffn_ref(_layernorm(x, axis=-1), L1_ffn_ln1_weight, L1_ffn_ln1_bias, L1_ffn_ln2_weight, L1_ffn_ln2_bias, L1_ffn_qkv_weight, L1_ffn_proj_weight, L1_ffn_router_weight, L1_ffn_moe_w1, L1_ffn_moe_w2)
    x = x + jnp.tanh(g_xattn[2]) * _L2_xattn_ref(_layernorm(x, axis=-1), ctx_1024, L2_xattn_w1_w, L2_xattn_w1_b, L2_xattn_w2_w, L2_xattn_w2_b)
    x = x + jnp.tanh(g_ffn[2]) * _L2_ffn_ref(_layernorm(x, axis=-1), L2_ffn_router_w, L2_ffn_router_b, L2_ffn_w1, L2_ffn_b1, L2_ffn_w2, L2_ffn_b2)
    x = x + jnp.tanh(g_xattn[3]) * _L3_xattn_ref(_layernorm(x, axis=-1), ctx_1024, ctx_1024, L3_xattn_Wq, L3_xattn_bq, L3_xattn_Wk, L3_xattn_bk, L3_xattn_Wv, L3_xattn_bv, L3_xattn_Wo, L3_xattn_bo, 1)
    x = x + jnp.tanh(g_ffn[3]) * _L3_ffn_ref(_layernorm(x, axis=-1), L3_ffn_q_node_w, L3_ffn_q_node_b, L3_ffn_q_w1, L3_ffn_q_b1, L3_ffn_q_w2, L3_ffn_q_b2, L3_ffn_k_node_w, L3_ffn_k_node_b, L3_ffn_k_w1, L3_ffn_k_b1, L3_ffn_k_w2, L3_ffn_k_b2, L3_ffn_v_node_w, L3_ffn_v_node_b, L3_ffn_v_w1, L3_ffn_v_b1, L3_ffn_v_w2, L3_ffn_v_b2)
    return x

_drawn_inputs = setup_inputs


def setup_inputs(seed=0):
    import zlib

    import numpy as np

    out = dict(_drawn_inputs(seed))
    spreads = {'L1_ffn_ln1_weight': (1.0, 0.6),
     'L1_ffn_ln1_bias': (0.0, 0.8),
     'L1_ffn_ln2_weight': (1.0, 0.6),
     'L1_ffn_ln2_bias': (0.0, 0.8),
     'L2_ffn_router_b': (0.0, 0.626),
     'L2_ffn_b1': (0.0, 0.8),
     'L2_ffn_b2': (0.0, 0.302),
     'L3_xattn_bq': (0.0, 0.8),
     'L3_xattn_bk': (0.0, 2.0),
     'L3_xattn_bv': (0.0, 0.1),
     'L3_xattn_bo': (0.0, 0.1),
     'L3_ffn_q_b1': (0.0, 0.8),
     'L3_ffn_q_b2': (0.0, 0.8),
     'L3_ffn_k_b1': (0.0, 0.8),
     'L3_ffn_k_b2': (0.0, 2.0),
     'L3_ffn_v_b1': (0.0, 0.8),
     'L3_ffn_v_b2': (0.0, 0.597)}
    factors = {'g_ffn': 25.896,
     'L0_xattn_Wq': 8.0,
     'L0_xattn_bq': 8.0,
     'L0_xattn_Wk': 8.0,
     'L0_xattn_bk': 64.0,
     'L0_xattn_bv': 4.508,
     'L1_xattn_bo': 6.664,
     'L2_xattn_w1_w': 8.0,
     'L2_xattn_w1_b': 8.0,
     'L2_xattn_w2_b': 7.011,
     'L2_ffn_w1': 5.791,
     'L2_ffn_w2': 5.748,
     'L3_ffn_q_node_w': 8.0,
     'L3_ffn_q_node_b': 8.0,
     'L3_ffn_q_w1': 8.0,
     'L3_ffn_q_w2': 8.0,
     'L3_ffn_k_node_w': 8.0,
     'L3_ffn_k_node_b': 8.0,
     'L3_ffn_k_w1': 8.0,
     'L3_ffn_k_w2': 8.0,
     'L3_ffn_v_node_b': 7.278}
    for name, (base, spread) in spreads.items():
        noise = np.random.default_rng([zlib.crc32(name.encode()), seed]).standard_normal(out[name].shape)
        drawn = base * np.exp(spread * noise) if base else spread * noise
        out[name] = jnp.asarray(drawn.astype(out[name].dtype))
    for name, factor in factors.items():
        out[name] = (out[name] * factor).astype(out[name].dtype)
    return out
```

```python
from contextlib import ExitStack

import concourse.bass as bass
from concourse import mybir

F32 = mybir.dt.float32
BF16 = mybir.dt.bfloat16
ALU = mybir.AluOpType
ACT = mybir.ActivationFunctionType
AX = mybir.AxisListType

P = 128
B, S, D = 4, 512, 256
TILES = B * S // P
TPB = S // P
DC = D // P
H, HD = 16, 16
GH = 4
GROUPS = H // GH
STRIP = 32
LN_EPS = 1e-5
MASKED = -(2.0 ** 100)
Q_PART = (0, 0, 1, 1, 0, 2)
K_PART = (0, 1, 0, 1, 2, 0)
PAIRS = len(Q_PART)
STACK = PAIRS * HD
MROWS = 2
DMA = 16


class Stage:

    def __init__(self, nc, name):
        self.nc, self.name, self.ctx, self.sems = nc, name, ExitStack(), []

    def __enter__(self):
        return self

    def __exit__(self, *exc):
        if exc[0] is None:
            self.nc.clear_and_free_semaphores(self.sems)
            self.nc.all_engine_barrier()
        self.ctx.close()

    def sb(self, name, shape, dt=F32):
        return self.ctx.enter_context(self.nc.sbuf_tensor(f"{self.name}_{name}", shape, dt))

    def ps(self, name, shape, dt=F32):
        return self.ctx.enter_context(self.nc.psum_tensor(f"{self.name}_{name}", shape, dt))

    def sem(self, name):
        s = self.nc.alloc_semaphore(f"{self.name}_{name}")
        self.sems.append(s)
        return s


class Held:
    pass


def load_stage(nc, k, a):
    with Stage(nc, "load") as st:
        loaded, tanh_done, cast_done = st.sem("loaded"), st.sem("tanh_done"), st.sem("cast_done")
        graw = st.sb("graw", [P, 8])
        with nc.Block() as block:
            @block.sync
            def _(sp):
                sp.dma_start(k.X[:], a["x"].rearrange("(t p) d -> p t d", p=P)).then_inc(loaded, DMA)
                sp.dma_start(graw[:], a["gates"]).then_inc(loaded, DMA)
                sp.dma_start(k.ident[:], a["ident"]).then_inc(loaded, DMA)
                sp.wait_ge(loaded, 3 * DMA)

            @block.scalar
            def _(act):
                act.wait_ge(loaded, 3 * DMA)
                act.activation(k.tg[:], graw[:], ACT.Tanh).then_inc(tanh_done, 1)
                act.wait_ge(tanh_done, 1)

            @block.vector
            def _(dve):
                dve.wait_ge(loaded, 3 * DMA)
                dve.tensor_copy(k.ident_bf[:], k.ident[:]).then_inc(cast_done, 1)
                dve.wait_ge(cast_done, 1)


def layernorm_stage(nc, k, name, src, dst, dst_T, affine=None):
    with Stage(nc, name) as st:
        stats = st.sb("stats", [P, TILES, 6])
        mv = st.sb("mv", [P, TILES, 2])
        std = st.sb("std", [P, TILES])
        rstd = st.sb("rstd", [P, TILES])
        shift = st.sb("shift", [P, TILES])
        eps = st.sb("eps", [P, 1])
        wb = st.sb("wb", [P, 2, D]) if affine else None
        tp = st.ps("tp", [P, 4, 512])
        stat_step, aggr_done, std_done = st.sem("stat_step"), st.sem("aggr_done"), st.sem("std_done")
        scale_step, norm_done, tp_full = st.sem("scale_step"), st.sem("norm_done"), st.sem("tp_full")
        act_evac, dve_evac, wb_loaded = st.sem("act_evac"), st.sem("dve_evac"), st.sem("wb_loaded")
        norm_per_tile = 3 if affine else 1
        with nc.Block() as block:
            if affine:
                @block.sync
                def _(sp):
                    for j in range(2):
                        sp.dma_start(wb[:, j, :], affine[j]).then_inc(wb_loaded, DMA)

            @block.vector
            def _(dve):
                dve.memset(eps[:], LN_EPS).then_inc(stat_step, 1)
                for t in range(TILES):
                    dve.bn_stats(stats[:, t, :], src[:, t, :]).then_inc(stat_step, 1)
                for t in range(TILES):
                    dve.wait_ge(stat_step, t + 2)
                    dve.bn_aggr(mv[:, t, :], stats[:, t, :]).then_inc(aggr_done, 1)
                dve.wait_ge(std_done, 1)
                dve.reciprocal(rstd[:], std[:]).then_inc(scale_step, 1)
                dve.wait_ge(scale_step, 1)
                dve.scalar_tensor_tensor(out=shift[:], in0=mv[:, :, 0], scalar=-1.0, in1=rstd[:],
                                         op0=ALU.mult, op1=ALU.mult).then_inc(scale_step, 1)
                dve.wait_ge(scale_step, 2)
                if affine:
                    dve.wait_ge(wb_loaded, 2 * DMA)
                for t in range(TILES):
                    dve.tensor_scalar(dst[:, t, :], src[:, t, :], rstd[:, t:t + 1], shift[:, t:t + 1],
                                      ALU.mult, ALU.add).then_inc(norm_done, 1)
                    if affine:
                        dve.wait_ge(norm_done, 3 * t + 1)
                        dve.tensor_tensor(dst[:, t, :], dst[:, t, :], wb[:, 0, :], ALU.mult).then_inc(norm_done, 1)
                        dve.wait_ge(norm_done, 3 * t + 2)
                        dve.tensor_tensor(dst[:, t, :], dst[:, t, :], wb[:, 1, :], ALU.add).then_inc(norm_done, 1)
                for n in range(1, DC * B, 2):
                    dve.wait_ge(tp_full, n + 1)
                    dve.tensor_copy(dst_T[:, n % DC, (n // DC) * S:(n // DC + 1) * S], tp[:, n % 4, :]).then_inc(dve_evac, 1)

            @block.scalar
            def _(act):
                act.wait_ge(aggr_done, TILES)
                act.activation(std[:], mv[:, :, 1], ACT.Sqrt, bias=eps[:, 0:1]).then_inc(std_done, 1)
                for n in range(0, DC * B, 2):
                    act.wait_ge(tp_full, n + 1)
                    act.copy(dst_T[:, n % DC, (n // DC) * S:(n // DC + 1) * S], tp[:, n % 4, :]).then_inc(act_evac, 1)

            @block.tensor
            def _(pe):
                for n in range(DC * B):
                    b, c = n // DC, n % DC
                    pe.wait_ge(norm_done, norm_per_tile * TPB * (b + 1))
                    if n >= 4:
                        pe.wait_ge(act_evac if n % 2 == 0 else dve_evac, (n - 4) // 2 + 1)
                    for j in range(TPB):
                        mm = pe.transpose(tp[:, n % 4, j * P:(j + 1) * P],
                                          dst[:, TPB * b + j, c * P:(c + 1) * P], k.ident[:])
                    mm.then_inc(tp_full, 1)


def attention_project(nc, k, name, a, vp, qk_dram, wq, wk, wv, bq, bk, bv, scr=None):
    with Stage(nc, name) as st:
        w = st.sb("w", [P, 3, DC, D])
        ctxb = st.sb("ctxb", [P, DC, S])
        qkb = st.sb("qkb", [P, 2, DC])
        bvb = st.sb("bvb", [P, D])
        parts = st.sb("parts", [P, 4, 3, S], BF16)
        rest = st.sb("rest", [P, 4, S])
        pj = st.ps("pj", [P, 4, S])
        pv = st.ps("pv", [P, 4, S])
        w_loaded, ctx_loaded, v_full, v_evac = (st.sem(n) for n in ("w_loaded", "ctx_loaded", "v_full", "v_evac"))
        proj_full, hi_done, rest_done, mid_done, lo_done, stored = (
            st.sem(n) for n in ("proj_full", "hi_done", "rest_done", "mid_done", "lo_done", "stored"))
        vp_zero = st.sem("vp_zero")
        pool_tick = st.sem("pool_tick")
        ORDER = [(1, 0), (1, 1), (0, 0), (0, 1)]
        with nc.Block() as block:
            @block.sync
            def _(sp):
                for j, ww in enumerate((wq, wk, wv)):
                    sp.dma_start(w[:, j], ww.rearrange("(c p) n -> p c n", p=P)).then_inc(w_loaded, DMA)
                sp.dma_start(qkb[:, 0, :], bq).then_inc(w_loaded, DMA)
                sp.dma_start(qkb[:, 1, :], bk).then_inc(w_loaded, DMA)
                sp.dma_start(bvb[:], bv).then_inc(w_loaded, DMA)
                with sp.Fori(0, B) as b:
                    sp.wait_ge(v_full, TPB * b)
                    sp.dma_start(ctxb[:], a["ctxT"].rearrange("(c p) n -> p c n", p=P)[:, :, bass.ds(b * S, S)]).then_inc(ctx_loaded, DMA)

            @block.tensor
            def _(pe):
                pe.wait_ge(w_loaded, 6 * DMA)
                with pe.Fori(0, B) as b:
                    def project(o):
                        which, m = ORDER[o]
                        pe.wait_ge(rest_done, 4 * b)
                        for c in range(DC):
                            rhs = ctxb[:, c, :] if which else k.XNT[:, c, bass.ds(b * S, S)]
                            mm = pe.matmul(pj[:, o, :], w[:, which, c, m * P:(m + 1) * P], rhs,
                                           start=c == 0, stop=c == DC - 1)
                        mm.then_inc(proj_full, 1)
                    pe.wait_ge(ctx_loaded, DMA * b + DMA)
                    project(0)
                    project(1)
                    pe.wait_ge(v_evac, TPB * b)
                    for t in range(TPB):
                        for c in range(DC):
                            mm = pe.matmul(pv[:, t, 0:D], ctxb[:, c, t * P:(t + 1) * P], w[:, 2, c, :],
                                           start=c == 0, stop=c == DC - 1)
                        mm.then_inc(v_full, 1)
                    project(2)
                    project(3)

            @block.scalar
            def _(act):
                act.wait_ge(w_loaded, 6 * DMA)
                with act.Fori(0, B) as b:
                    for o, (which, m) in enumerate(ORDER):
                        act.wait_ge(proj_full, 4 * b + o + 1)
                        act.wait_ge(stored, 4 * DMA * b)
                        act.activation(parts[:, o, 0, :], pj[:, o, :], ACT.Identity,
                                       bias=qkb[:, which, m:m + 1]).then_inc(hi_done, 1)

            @block.vector
            def _(dve):
                dve.wait_ge(vp_zero, 2)
                dve.wait_ge(w_loaded, 6 * DMA)
                with dve.Fori(0, B) as b:
                    def first_rest(o):
                        which, m = ORDER[o]
                        dve.wait_ge(hi_done, 4 * b + o + 1)
                        dve.wait_ge(lo_done, 4 * b)
                        dve.scalar_tensor_tensor(out=rest[:, o, :], in0=pj[:, o, :], scalar=qkb[:, which, m:m + 1],
                                                 in1=parts[:, o, 0, :], op0=ALU.add, op1=ALU.subtract).then_inc(rest_done, 1)
                    first_rest(0)
                    first_rest(1)
                    for t in range(TPB):
                        dve.wait_ge(v_full, TPB * b + t + 1)
                        dve.tensor_tensor(vp[:, bass.ds(GROUPS * b, GROUPS), t, :, 0:HD],
                                          pv[:, t, 0:D].rearrange("p (g i d) -> p g i d", g=GROUPS, i=GH),
                                          bvb[:].rearrange("p (g i d) -> p g i d", g=GROUPS, i=GH), ALU.add).then_inc(v_evac, 1)
                    first_rest(2)
                    first_rest(3)
                    for o in range(4):
                        dve.wait_ge(mid_done, 4 * b + o + 1)
                        dve.tensor_tensor(parts[:, o, 2, :], rest[:, o, :], parts[:, o, 1, :],
                                          ALU.subtract).then_inc(lo_done, 1)

            @block.gpsimd
            def _(pool):
                pool.memset(vp[:, :, :, :, HD:STRIP], 0.0).then_inc(vp_zero, 1)
                pool.wait_ge(vp_zero, 1)
                pool.memset(vp[:, :, :, :, HD:HD + 1], 1.0).then_inc(vp_zero, 1)
                with pool.Fori(0, B) as b:
                    for o in range(4):
                        pool.wait_ge(rest_done, 4 * b + o + 1)
                        pool.sem_inc(pool_tick, 1)
                        pool.tensor_copy(parts[:, o, 1, :], rest[:, o, :]).then_inc(mid_done, 1)
                    for o, (which, m) in enumerate(ORDER):
                        pool.wait_ge(lo_done, 4 * b + o + 1)
                        dst = qk_dram[which, :, bass.ds(GROUPS * b + 2 * m, 2)].rearrange("r g i d t -> (g i d) r t")
                        pool.dma_start(dst, parts[:, o, :, :]).then_inc(stored, DMA)
                pool.wait_ge(stored, 4 * DMA * B)


def attention_core(nc, k, name, vp, atn, qk_dram, scale, selsum, bo, gate, mask=None, tril2=None):
    AV_CREDIT, EXP_CREDIT, S_CREDIT = 4, 2, 2
    with Stage(nc, name) as st:
        rows = B if mask and mask[2] else 1
        qs = [st.sb(f"qs{u}", [P, GH, S], BF16) for u in range(2)]
        ks = [st.sb(f"ks{u}", [P, GH, S], BF16) for u in range(2)]
        vg = [st.sb(f"vg{u}", [P, TPB, GH, STRIP]) for u in range(2)]
        vg2 = [st.sb(f"vgd{u}", [P, TPB, GH, STRIP]) for u in range(2)] if tril2 is not None else None
        prob_wide = [st.sb(f"prob{u}", [P, TPB * (S + P) if tril2 is not None else TPB * S]) for u in range(2)]
        prob = [w[:, 0:TPB * S].rearrange("p (k q) -> p k q", k=TPB) for w in prob_wide]
        avs = [st.sb(f"avs{u}", [P, S]) for u in range(2)]
        rsum = st.sb("rsum", [P, S])
        sel = st.sb("sel", [P, P])
        negm = st.sb("negm", [P, TPB])
        nmp = st.sb("nmp", [P, TPB, MROWS], BF16)
        bob = st.sb("bob", [P, D])
        if mask:
            mraw = st.sb("mraw", [P, TPB, S], mask[0].dtype)
            mb = st.sb("mb", [P, rows * TPB, S], BF16)
            mbT = st.sb("mbT", [P, rows * TPB, S], BF16)
        if tril2 is not None:
            tril = st.sb("tril", [P, P])
        ps_s = st.ps("s", [P, 2, S])
        ps_st = st.ps("st", [P, 4, S])
        ps_av = st.ps("av", [P, S])
        ps_m = st.ps("m", [P, S])
        (qk_loaded, const_loaded, vg_ready, s_full, s_free, split_step, negmax_ready, mt_full, mrow_ready,
         st_full, exp_done, av_done, av_evac, bc_full, recip_done, atn_done, ones_done, mask_loaded,
         mask_ready, diag_done, bias_step) = (st.sem(n) for n in (
             "qk_loaded", "const_loaded", "vg_ready", "s_full", "s_free", "split_step", "negmax_ready", "mt_full",
             "mrow_ready", "st_full", "exp_done", "av_done", "av_evac", "bc_full", "recip_done", "atn_done",
             "ones_done", "mask_loaded", "mask_ready", "diag_done", "bias_step"))
        qk_loaded1 = st.sem("qk_loaded1")
        pool_tick = st.sem("pool_tick")
        loaded = (qk_loaded, qk_loaded1)
        NIT = B * GROUPS // 2
        PER_LOAD = 2 * PAIRS * DMA
        NCONST = 2 + (tril2 is not None)

        def load_stack(sp, u, G):
            for which, part_of, dst in ((0, Q_PART, qs[u]), (1, K_PART, ks[u])):
                for r in range(PAIRS):
                    src = qk_dram[which, part_of[r], bass.ds(G, 1) if not isinstance(G, int) else slice(G, G + 1)]
                    sp.dma_start(dst[r * HD:(r + 1) * HD, :, :], src.rearrange("g i d t -> d (g i) t")).then_inc(loaded[u], DMA)

        with nc.Block() as block:
            @block.sync
            def _(sp):
                sp.dma_start(sel[:], selsum).then_inc(const_loaded, DMA)
                sp.dma_start(bob[:], bo).then_inc(const_loaded, DMA)
                if tril2 is not None:
                    sp.dma_start(tril[:], tril2).then_inc(const_loaded, DMA)
                load_stack(sp, 0, 0)
                load_stack(sp, 1, 1)
                if mask:
                    for n in range(2 * rows):
                        if n:
                            sp.wait_ge(mask_ready, n)
                        m = mask[n % 2]
                        sp.dma_start(mraw[:], m[(n // 2) * S:(n // 2 + 1) * S].rearrange("(t p) c -> p t c", p=P)).then_inc(mask_loaded, DMA)
                with sp.Fori(0, NIT - 1) as it:
                    for u in range(2):
                        sp.wait_ge(st_full, 16 * it + 8 * u + 8)
                        load_stack(sp, u, 2 * it + (2 + u))

            @block.gpsimd
            def _(pool):
                if tril2 is not None:
                    pool.wait_ge(const_loaded, NCONST * DMA)
                for u in range(2):
                    pool.memset(ks[u][STACK:STACK + MROWS, :, :], 1.0).then_inc(ones_done, 1)
                pool.wait_ge(ones_done, 2)
                with pool.Fori(0, NIT) as it:
                    for u in range(2):
                        pool.wait_ge(av_done, 8 * it + 4 * u)
                        pool.sem_inc(pool_tick, 1)
                        pool.tensor_copy(vg[u][:], vp[:, bass.ds(2 * it + u, 1)].rearrange("p g t i c -> p (g t) i c")).then_inc(vg_ready, 1)
                        if vg2 is not None:
                            pool.wait_ge(vg_ready, 4 * it + 2 * u + 1)
                            pool.tensor_tensor(vg2[u][:], vg[u][:], vg[u][:], ALU.add).then_inc(vg_ready, 1)
                    if tril2 is not None:
                        for j in range(2 * GH):
                            pool.wait_ge(exp_done, 16 * it + 2 * j + 2 + EXP_CREDIT)
                            diag = prob_wide[j % 2][:].rearrange("p (k q) -> p k q", k=TPB)[:, :, 0:P]
                            pool.tensor_tensor(diag, diag, tril[:].unsqueeze(1).broadcast_to([P, TPB, P]), ALU.mult).then_inc(diag_done, 1)

            @block.tensor
            def _(pe):
                pe.sem_inc(av_done, AV_CREDIT)
                pe.wait_ge(ones_done, 2)
                pe.wait_ge(const_loaded, NCONST * DMA)
                if mask:
                    pe.wait_ge(mask_ready, 2 * rows)
                with pe.Fori(0, B) as b:
                    with pe.Fori(0, GROUPS // 2) as gp:
                        it = 2 * b + gp

                        def scores(j, qt):
                            u, i = divmod(j, GH)
                            if qt == 0 and i == 0:
                                pe.wait_ge(loaded[u], PER_LOAD * it + PER_LOAD)
                            T = 4 * j + qt
                            pe.wait_ge(s_free, 32 * it + T + 1)
                            if mask:
                                pe.matmul(ps_s[:, T % 2, :], qs[u][0:STACK, i, qt * P:(qt + 1) * P], ks[u][0:STACK, i, :],
                                          start=True, stop=False)
                                mm = pe.matmul(ps_s[:, T % 2, :], k.ident_bf[:],
                                               mb[:, bass.ds(TPB * b + qt, 1), :] if rows > 1 else mb[:, qt, :],
                                               start=False, stop=True)
                            else:
                                mm = pe.matmul(ps_s[:, T % 2, :], qs[u][0:STACK, i, qt * P:(qt + 1) * P], ks[u][0:STACK, i, :],
                                               start=True, stop=True)
                            mm.then_inc(s_full, 1)

                        def max_rows(j):
                            pe.wait_ge(negmax_ready, 8 * it + j + 1)
                            pe.wait_ge(mrow_ready, 8 * it + j)
                            pe.wait_ge(recip_done, 2 * it + (1 if j > GH else 0))
                            for qt in range(TPB):
                                mm = pe.matmul(ps_m[STACK:STACK + MROWS, qt * P:(qt + 1) * P], nmp[:, qt, :], k.ident_bf[:],
                                               start=True, stop=True)
                            mm.then_inc(mt_full, 1)

                        def scores_T(j, hb):
                            u, i = divmod(j, GH)
                            if hb == 0:
                                pe.wait_ge(mrow_ready, 8 * it + j + 1)
                            pe.wait_ge(exp_done, 16 * it + 2 * j + hb + 1)
                            for kt in (2 * hb, 2 * hb + 1):
                                mm = pe.matmul(ps_st[:, kt, :], ks[u][0:STACK + MROWS, i, kt * P:(kt + 1) * P],
                                               qs[u][0:STACK + MROWS, i, :], start=True, stop=not mask)
                                if mask:
                                    mm = pe.matmul(ps_st[:, kt, :], k.ident_bf[:],
                                                   mbT[:, bass.ds(TPB * b + kt, 1), :] if rows > 1 else mbT[:, kt, :],
                                                   start=False, stop=True)
                            mm.then_inc(st_full, 1)

                        def values(j):
                            u, i = divmod(j, GH)
                            out = slice(STRIP * i, STRIP * (i + 1))
                            if i == 0:
                                pe.wait_ge(vg_ready, (2 * it + u + 1) * (2 if vg2 is not None else 1))
                                pe.wait_ge(av_evac, 2 * it + u)
                            pe.wait_ge(exp_done, 16 * it + 2 * j + 2 + EXP_CREDIT)
                            if tril2 is not None:
                                pe.wait_ge(diag_done, 8 * it + j + 1)
                            for kt in range(TPB):
                                cut = (kt + 1) * P if tril2 is not None else S
                                mm = pe.matmul(ps_av[out, 0:cut], vg[u][:, kt, i, :], prob[j % 2][:, kt, 0:cut],
                                               start=kt == 0, stop=kt == TPB - 1, skip_group_check=True)
                                if cut < S:
                                    mm = pe.matmul(ps_av[out, cut:S], vg2[u][:, kt, i, :], prob[j % 2][:, kt, cut:S],
                                                   start=False, stop=False, skip_group_check=True)
                            mm.then_inc(av_done, 1)

                        def sums(u):
                            pe.wait_ge(av_evac, 2 * it + u + 1)
                            pe.wait_ge(mrow_ready, 8 * it + 4 * u + 4 + (1 if u == 0 else 0))
                            pe.matmul(ps_m[:, :], sel[:], avs[u][:], start=True, stop=True).then_inc(bc_full, 1)

                        for qt in range(TPB):
                            scores(0, qt)
                        for j in range(2 * GH):
                            nxt = j + 1 < 2 * GH
                            max_rows(j)
                            if nxt:
                                scores(j + 1, 0)
                                scores(j + 1, 1)
                            scores_T(j, 0)
                            if nxt:
                                scores(j + 1, 2)
                            scores_T(j, 1)
                            if nxt:
                                scores(j + 1, 3)
                            if j == GH:
                                sums(0)
                            values(j)
                        sums(1)

            @block.scalar
            def _(act):
                act.sem_inc(exp_done, EXP_CREDIT)
                act.wait_ge(ones_done, 2)
                with act.Fori(0, NIT) as it:
                    for j in range(2 * GH):
                        u, i = divmod(j, GH)
                        act.wait_ge(mt_full, 8 * it + j + 1)
                        act.copy(qs[u][STACK:STACK + MROWS, i, :], ps_m[STACK:STACK + MROWS, :]).then_inc(mrow_ready, 1)
                        for hb in range(2):
                            act.wait_ge(st_full, 16 * it + 2 * j + hb + 1)
                            act.wait_ge(av_done, 8 * it + j + AV_CREDIT - 1)
                            act.activation(prob[j % 2][:, 2 * hb:2 * hb + 2, :], ps_st[:, 2 * hb:2 * hb + 2, :], ACT.Exp,
                                           scale=scale).then_inc(exp_done, 1)
                        if i == GH - 1:
                            act.wait_ge(av_done, 8 * it + j + 1 + AV_CREDIT)
                            act.wait_ge(atn_done, 2 * it + u + 1)
                            act.copy(avs[u][:], ps_av[:]).then_inc(av_evac, 1)

            @block.vector
            def _(dve):
                dve.sem_inc(s_free, S_CREDIT)
                dve.sem_inc(atn_done, 2)
                if mask:
                    for n in range(2 * rows):
                        dve.wait_ge(mask_loaded, DMA * (n + 1))
                        dst = mb if n % 2 == 0 else mbT
                        dve.tensor_scalar(dst[:, TPB * (n // 2):TPB * (n // 2 + 1), :], mraw[:], 0, MASKED,
                                          ALU.is_equal, ALU.mult).then_inc(mask_ready, 1)
                dve.wait_ge(const_loaded, NCONST * DMA)
                dve.tensor_scalar(bob[:], bob[:], k.tg[:, gate:gate + 1], None, ALU.mult).then_inc(bias_step, 1)
                dve.wait_ge(bias_step, 1)
                dve.tensor_tensor(k.X[:], k.X[:], bob[:].unsqueeze(1).broadcast_to([P, TILES, D]), ALU.add).then_inc(bias_step, 1)
                dve.wait_ge(bias_step, 2)
                with dve.Fori(0, NIT) as it:
                    def divide(u):
                        dve.wait_ge(bc_full, 2 * it + u + 1)
                        dve.wait_ge(atn_done, 2 * it + u + 2)
                        dve.reciprocal(rsum[:], ps_m[:]).then_inc(recip_done, 1)
                        dve.wait_ge(recip_done, 2 * it + u + 1)
                        dve.tensor_tensor(atn[:, bass.ds(2 * it + u, 1), :], avs[u][:], rsum[:], ALU.mult).then_inc(atn_done, 1)

                    for j in range(2 * GH):
                        dve.wait_ge(negmax_ready, 8 * it + j)
                        for qt in range(TPB):
                            T = 4 * j + qt
                            dve.wait_ge(s_full, 32 * it + T + 1)
                            dve.tensor_reduce(negm[:, qt:qt + 1], ps_s[:, T % 2, :], AX.X, ALU.max, negate=True).then_inc(s_free, 1)
                        dve.wait_ge(s_free, 32 * it + 4 * j + 4 + S_CREDIT)
                        dve.tensor_copy(nmp[:, :, 0], negm[:]).then_inc(split_step, 1)
                        dve.wait_ge(split_step, 8 * it + j + 1)
                        dve.tensor_tensor(nmp[:, :, 1], negm[:], nmp[:, :, 0], ALU.subtract).then_inc(negmax_ready, 1)
                        if j == GH + 1:
                            divide(0)
                    divide(1)

def attention_out(nc, k, name, atn, wo, gate):
    with Stage(nc, name) as st:
        w = st.sb("w", [P, GROUPS, D])
        po = st.ps("po", [P, 8, 512])
        w_loaded, out_full, out_evac = st.sem("w_loaded"), st.sem("out_full"), st.sem("out_evac")
        with nc.Block() as block:
            @block.sync
            def _(sp):
                sp.dma_start(w[:], wo).then_inc(w_loaded, DMA)

            @block.tensor
            def _(pe):
                pe.wait_ge(w_loaded, DMA)
                for t in range(TILES):
                    if t >= 8:
                        pe.wait_ge(out_evac, t - 7)
                    for g in range(GROUPS):
                        mm = pe.matmul(po[:, t % 8, 0:D], atn[:, GROUPS * (t // TPB) + g, (t % TPB) * P:(t % TPB + 1) * P],
                                       w[:, g, :], start=g == 0, stop=g == GROUPS - 1)
                    mm.then_inc(out_full, 1)

            @block.vector
            def _(dve):
                for t in range(TILES):
                    dve.wait_ge(out_full, t + 1)
                    dve.scalar_tensor_tensor(out=k.X[:, t, :], in0=po[:, t % 8, 0:D], scalar=k.tg[:, gate:gate + 1],
                                             in1=k.X[:, t, :], op0=ALU.mult, op1=ALU.add).then_inc(out_evac, 1)


def attention_layer(nc, k, name, a, wq, wk, wv, bq, bk, bv, wo, bo, scale, gate, mask=None, tril2=None):
    layernorm_stage(nc, k, name + "_ln", k.X, k.XN, k.XNT)
    with ExitStack() as ctx:
        vp = ctx.enter_context(nc.sbuf_tensor(name + "_vp", [P, B * GROUPS, TPB, GH, STRIP], F32))
        attention_project(nc, k, name + "_p", a, vp, k.qk_dram, wq, wk, wv, bq, bk, bv)
        attention_core(nc, k, name + "_a", vp, k.ATN, k.qk_dram, scale, a["selsum"], bo, gate, mask, tril2)
    attention_out(nc, k, name + "_o", k.ATN, wo, gate)


class Chain:

    def __init__(self, eng, sem, base=0):
        self.eng, self.sem, self.base, self.n = eng, sem, base, 0

    def __call__(self, ins):
        self.n += 1
        ins.then_inc(self.sem, 1)
        self.eng.wait_ge(self.sem, self.base + self.n)


def over(x, n):
    return x.unsqueeze(2).broadcast_to([x.shape[0], x.shape[1], n])


def transpose_stage(nc, k, name, src, dst_T):
    with Stage(nc, name) as st:
        tp = st.ps("tp", [P, 4, 512])
        tp_full, act_evac, dve_evac = st.sem("tp_full"), st.sem("act_evac"), st.sem("dve_evac")

        def bank(n):
            return dst_T[:, n % DC, (n // DC) * S:(n // DC + 1) * S], tp[:, n % 4, :]

        with nc.Block() as block:
            @block.tensor
            def _(pe):
                for n in range(DC * B):
                    if n >= 4:
                        pe.wait_ge(act_evac if n % 2 == 0 else dve_evac, (n - 4) // 2 + 1)
                    for j in range(TPB):
                        mm = pe.transpose(tp[:, n % 4, j * P:(j + 1) * P],
                                          src[:, TPB * (n // DC) + j, (n % DC) * P:(n % DC + 1) * P], k.ident[:])
                    mm.then_inc(tp_full, 1)

            @block.scalar
            def _(act):
                for n in range(0, DC * B, 2):
                    act.wait_ge(tp_full, n + 1)
                    act.copy(*bank(n)).then_inc(act_evac, 1)

            @block.vector
            def _(dve):
                for n in range(1, DC * B, 2):
                    dve.wait_ge(tp_full, n + 1)
                    dve.tensor_copy(*bank(n)).then_inc(dve_evac, 1)


def router_stage(nc, k, name, a, src_T, rw, rb, E, K, kind, gate_col, gates, capacity=None):
    EPS = 1e-10
    with Stage(nc, name) as st:
        w = st.sb("w", [P, DC, E])
        rbb = st.sb("rbb", [P, E])
        ranks = st.sb("ranks", [P, E])
        lg, pr, work, sel, one, tmp = (st.sb(n, [P, TILES, E]) for n in ("lg", "pr", "work", "sel", "one", "tmp"))
        m, s, r = (st.sb(n, [P, TILES]) for n in ("m", "s", "r"))
        ps = st.ps("ps_lg", [P, TILES, E])
        loaded, lg_full, step, shifted, exp_done = (st.sem(n) for n in ("loaded", "lg_full", "step", "shifted", "exp_done"))
        if capacity:
            before = st.sb("before", [P, P])
            ones = st.sb("ones", [P, P])
            cum = st.sb("cum", [P, TILES, E])
            ps_rank = st.ps("ps_rank", [P, TILES, E])
            sel_done, rank_full = st.sem("sel_done"), st.sem("rank_full")
        n_loads = 3 + (1 if capacity else 0)
        with nc.Block() as block:
            @block.sync
            def _(sp):
                sp.dma_start(w[:], rw.rearrange("(c p) e -> p c e", p=P)).then_inc(loaded, DMA)
                sp.dma_start(rbb[:], rb).then_inc(loaded, DMA)
                sp.dma_start(ranks[:], a[f"ranks{E}"]).then_inc(loaded, DMA)
                if capacity:
                    sp.dma_start(before[:], a["before"]).then_inc(loaded, DMA)

            @block.tensor
            def _(pe):
                pe.wait_ge(loaded, n_loads * DMA)
                for t in range(TILES):
                    for c in range(DC):
                        mm = pe.matmul(ps[:, t, :], src_T[:, c, t * P:(t + 1) * P], w[:, c, :], start=c == 0, stop=c == DC - 1)
                mm.then_inc(lg_full, 1)
                if capacity:
                    pe.wait_ge(sel_done, 1)
                    pe.matmul(ps_rank[:], before[:], sel[:], start=True, stop=False)
                    pe.matmul(ps_rank[:], ones[:], cum[:], start=False, stop=True).then_inc(rank_full, 1)

            @block.scalar
            def _(act):
                act.wait_ge(shifted, 1)
                act.activation(pr[:], lg[:], ACT.Exp).then_inc(exp_done, 1)

            @block.vector
            def _(dve):
                do = Chain(dve, step)

                def row_sum(out, x):
                    do(dve.tensor_reduce(out, x, AX.X, ALU.add))

                dve.wait_ge(loaded, n_loads * DMA)
                dve.wait_ge(lg_full, 1)
                do(dve.tensor_tensor(lg[:], ps[:], rbb[:].unsqueeze(1).broadcast_to([P, TILES, E]), ALU.add))
                do(dve.tensor_reduce(m[:], lg[:], AX.X, ALU.max))
                dve.tensor_tensor(lg[:], lg[:], over(m[:], E), ALU.subtract).then_inc(shifted, 1)
                dve.wait_ge(exp_done, 1)
                if kind == "probs":
                    row_sum(s[:], pr[:])
                    do(dve.reciprocal(r[:], s[:]))
                    do(dve.tensor_tensor(pr[:], pr[:], over(r[:], E), ALU.mult))
                do(dve.tensor_copy(work[:], pr[:] if kind == "probs" else lg[:]))
                do(dve.memset(sel[:], 0.0))
                for _i in range(K):
                    do(dve.tensor_reduce(m[:], work[:], AX.X, ALU.max))
                    do(dve.tensor_tensor(one[:], work[:], over(m[:], E), ALU.is_equal))
                    do(dve.tensor_tensor(one[:], one[:], ranks[:].unsqueeze(1).broadcast_to([P, TILES, E]), ALU.mult))
                    do(dve.tensor_reduce(m[:], one[:], AX.X, ALU.max))
                    do(dve.tensor_tensor(one[:], one[:], over(m[:], E), ALU.is_equal))
                    do(dve.tensor_tensor(sel[:], sel[:], one[:], ALU.add))
                    do(dve.scalar_tensor_tensor(out=work[:], in0=one[:], scalar=MASKED, in1=work[:], op0=ALU.mult, op1=ALU.add))
                do(dve.tensor_tensor(tmp[:], pr[:], sel[:], ALU.mult))
                row_sum(s[:], tmp[:])
                if kind == "probs" and not capacity:
                    do(dve.tensor_scalar(s[:], s[:], EPS, None, ALU.add))
                do(dve.reciprocal(r[:], s[:]))
                do(dve.tensor_tensor(tmp[:], tmp[:], over(r[:], E), ALU.mult))
                if kind == "probs" and not capacity:
                    row_sum(s[:], tmp[:])
                    do(dve.tensor_scalar(r[:], s[:], EPS, None, ALU.max))
                    do(dve.reciprocal(m[:], r[:]))
                    do(dve.tensor_tensor(tmp[:], tmp[:], over(m[:], E), ALU.mult))
                    do(dve.tensor_scalar(s[:], s[:], EPS, k.tg[:, gate_col:gate_col + 1], ALU.mult, ALU.mult))
                    do(dve.tensor_tensor(k.X[:], k.X[:], over(s[:], D), ALU.add))
                if capacity:
                    do(dve.memset(ones[:], 1.0))
                    do(dve.memset(cum[:, 0, :], 0.0))
                    for t in range(1, TILES):
                        do(dve.tensor_tensor(cum[:, t, :], cum[:, t - 1, :], sel[:, t - 1, :], ALU.add))
                    dve.sem_inc(sel_done, 1)
                    dve.wait_ge(rank_full, 1)
                    do(dve.tensor_scalar(one[:], ps_rank[:], float(capacity), None, ALU.is_lt))
                    do(dve.tensor_tensor(tmp[:], tmp[:], one[:], ALU.mult))
                do(dve.tensor_scalar(gates[:], tmp[:], k.tg[:, gate_col:gate_col + 1], None, ALU.mult))


def linear_experts_stage(nc, k, name, expert_w, gates, E):
    BANKS = 8
    with Stage(nc, name) as st:
        w = st.sb("w", [P, DC, E, D])
        po = st.ps("po", [P, BANKS, 512])
        w_loaded, full, evac, x_step = (st.sem(n) for n in ("w_loaded", "full", "evac", "x_step"))
        with nc.Block() as block:
            @block.sync
            def _(sp):
                for c in range(DC):
                    sp.dma_start(w[:, c], expert_w[:, c * P:(c + 1) * P, :].rearrange("e p n -> p e n")).then_inc(w_loaded, DMA)

            @block.tensor
            def _(pe):
                pe.wait_ge(w_loaded, DC * DMA)
                with pe.Fori(0, E // 2) as pair:
                    for t in range(TILES):
                        pe.wait_ge(evac, TILES * pair + t + 1)
                        for c in range(DC):
                            mm = pe.matmul(po[:, t % BANKS, :], k.XNT[:, c, t * P:(t + 1) * P],
                                           w[:, c, bass.ds(2 * pair, 2), :], start=c == 0, stop=c == DC - 1)
                        mm.then_inc(full, 1)

            @block.vector
            def _(dve):
                dve.sem_inc(evac, BANKS)
                with dve.Fori(0, E // 2) as pair:
                    for t in range(TILES):
                        dve.wait_ge(full, TILES * pair + t + 1)
                        dve.scalar_tensor_tensor(out=k.X[:, t, :], in0=po[:, t % BANKS, 0:D], scalar=gates[:, t, bass.ds(2 * pair, 1)],
                                                 in1=k.X[:, t, :], op0=ALU.mult, op1=ALU.add).then_inc(x_step, 1)
                        dve.wait_ge(x_step, TILES * pair + t + 1)
                        dve.scalar_tensor_tensor(out=k.X[:, t, :], in0=po[:, t % BANKS, D:2 * D], scalar=gates[:, t, bass.ds(2 * pair + 1, 1)],
                                                 in1=k.X[:, t, :], op0=ALU.mult, op1=ALU.add).then_inc(evac, 1)


def moe_stage(nc, k, name, src_T, w1, w2, b1, gates, E, FC, gated):
    OB, HB = 4, 2
    NW = 2 if gated else 1
    F = NW * FC * P
    with Stage(nc, name) as st:
        w1s = [st.sb(f"w1_{u}", [P, DC, F]) for u in range(2)]
        w2s = [st.sb(f"w2_{u}", [P, FC, D]) for u in range(2)]
        b1s = st.sb("b1", [P, E, NW * FC]) if gated else None
        ht = st.sb("ht", [P, FC, S])
        sg = st.sb("sg", [P, 2, S]) if gated else None
        ph = [st.ps(f"ph{n}", [P, HB, S]) for n in range(NW)]
        po = st.ps("po", [P, OB, 512])
        w_loaded = [st.sem(f"w_loaded{u}") for u in range(2)]
        b_loaded, h_full, act_done, h_ready, o_full, o_evac = (
            st.sem(n) for n in ("b_loaded", "h_full", "act_done", "h_ready", "o_full", "o_evac"))
        hidden_ready = h_ready if gated else act_done

        def load(sp, u, e):
            one = bass.ds(e, 1) if not isinstance(e, int) else slice(e, e + 1)
            sp.dma_start(w1s[u][:], w1[one].rearrange("e (c p) f -> p (e c) f", p=P)).then_inc(w_loaded[u], DMA)
            sp.dma_start(w2s[u][:], w2[one].rearrange("e (j p) n -> p (e j) n", p=P)).then_inc(w_loaded[u], DMA)

        with nc.Block() as block:
            @block.sync
            def _(sp):
                if gated:
                    sp.dma_start(b1s[:], b1).then_inc(b_loaded, DMA)
                load(sp, 0, 0)
                load(sp, 1, 1)
                with sp.Fori(0, E // 2 - 1) as ep:
                    for u in range(2):
                        sp.wait_ge(o_full, 2 * TILES * ep + TILES * u + TILES)
                        load(sp, u, 2 * ep + (2 + u))

            @block.tensor
            def _(pe):
                with pe.Fori(0, E // 2) as ep:
                    for u in range(2):
                        with pe.Fori(0, B) as b:
                            pe.wait_ge(w_loaded[u], 2 * DMA * ep + 2 * DMA)
                            chunk = 2 * B * ep + B * u + b
                            for j in range(FC):
                                pe.wait_ge(hidden_ready, FC * chunk + j + 1)
                                for n in range(NW):
                                    for c in range(DC):
                                        mm = pe.matmul(ph[n][:, j % HB, :], w1s[u][:, c, (n * FC + j) * P:(n * FC + j + 1) * P],
                                                       src_T[:, c, bass.ds(S * b, S)], start=c == 0, stop=c == DC - 1)
                                mm.then_inc(h_full, 1)
                            for t in range(TPB):
                                pe.wait_ge(hidden_ready, FC * chunk + FC + HB)
                                pe.wait_ge(o_evac, TPB * chunk + t + 1)
                                for j in range(FC):
                                    mm = pe.matmul(po[:, t % OB, 0:D], ht[:, j, t * P:(t + 1) * P], w2s[u][:, j, :],
                                                   start=j == 0, stop=j == FC - 1)
                                mm.then_inc(o_full, 1)

            @block.scalar
            def _(act):
                act.sem_inc(act_done, HB)
                if gated:
                    act.wait_ge(b_loaded, DMA)
                with act.Fori(0, E) as e:
                    with act.Fori(0, B) as b:
                        chunk = B * e + b
                        for j in range(FC):
                            act.wait_ge(h_full, FC * chunk + j + 1)
                            if gated:
                                act.wait_ge(h_ready, FC * chunk + j + 1)
                                act.activation(sg[:, j % 2, :], ph[0][:, j % HB, :], ACT.Silu,
                                               bias=b1s[:, bass.ds(e, 1), j:j + 1].rearrange("p e j -> p (e j)")).then_inc(act_done, 1)
                            else:
                                act.activation(ht[:, j, :], ph[0][:, j % HB, :], ACT.Gelu_apprx_tanh).then_inc(act_done, 1)

            @block.vector
            def _(dve):
                dve.sem_inc(o_evac, OB)
                if gated:
                    dve.sem_inc(h_ready, HB)
                    dve.wait_ge(b_loaded, DMA)
                with dve.Fori(0, E) as e:
                    with dve.Fori(0, B) as b:
                        chunk = B * e + b
                        if gated:
                            for j in range(FC):
                                dve.wait_ge(act_done, FC * chunk + j + 1 + HB)
                                dve.scalar_tensor_tensor(out=ht[:, j, :], in0=ph[1][:, j % HB, :],
                                                         scalar=b1s[:, bass.ds(e, 1), FC + j:FC + j + 1].rearrange("p e j -> p (e j)"),
                                                         in1=sg[:, j % 2, :], op0=ALU.add, op1=ALU.mult).then_inc(h_ready, 1)
                        for t in range(TPB):
                            dve.wait_ge(o_full, TPB * chunk + t + 1)
                            x = k.X[:, bass.ds(TPB * b + t, 1), :].rearrange("p t d -> p (t d)")
                            dve.scalar_tensor_tensor(out=x, in0=po[:, t % OB, 0:D],
                                                     scalar=gates[:, bass.ds(TPB * b + t, 1), bass.ds(e, 1)].rearrange("p t e -> p (t e)"),
                                                     in1=x, op0=ALU.mult, op1=ALU.add).then_inc(o_evac, 1)


def gated_bias_stage(nc, k, name, gates, b2, E):
    with Stage(nc, name) as st:
        b2s = st.sb("b2", [E, D])
        gT = st.sb("gT", [E, TILES, P])
        tp = st.ps("tp", [E, TILES, P])
        po = st.ps("po", [P, 4, 512])
        loaded, t_full, t_evac, o_full, o_evac = (st.sem(n) for n in ("loaded", "t_full", "t_evac", "o_full", "o_evac"))
        with nc.Block() as block:
            @block.sync
            def _(sp):
                sp.dma_start(b2s[:], b2).then_inc(loaded, DMA)

            @block.tensor
            def _(pe):
                for t in range(TILES):
                    mm = pe.transpose(tp[:, t, :], gates[:, t, :], k.ident[:])
                mm.then_inc(t_full, 1)
                pe.wait_ge(loaded, DMA)
                pe.wait_ge(t_evac, 1)
                for t in range(TILES):
                    if t >= 4:
                        pe.wait_ge(o_evac, t - 3)
                    pe.matmul(po[:, t % 4, 0:D], gT[:, t, :], b2s[:], start=True, stop=True).then_inc(o_full, 1)

            @block.vector
            def _(dve):
                dve.wait_ge(t_full, 1)
                dve.tensor_copy(gT[:], tp[:]).then_inc(t_evac, 1)
                for t in range(TILES):
                    dve.wait_ge(o_full, t + 1)
                    dve.tensor_tensor(k.X[:, t, :], po[:, t % 4, 0:D], k.X[:, t, :], ALU.add).then_inc(o_evac, 1)


def expert_layer_0(nc, k, a):
    layernorm_stage(nc, k, "l0f_ln", k.X, k.XN, k.XNT)
    with ExitStack() as ctx:
        gates = ctx.enter_context(nc.sbuf_tensor("l0f_gates", [P, TILES, 16], F32))
        router_stage(nc, k, "l0f_r", a, k.XNT, a["r0w"], a["r0b"], 16, 6, "probs", 4, gates)
        linear_experts_stage(nc, k, "l0f_e", a["e0w"], gates, 16)


def expert_layer_2(nc, k, a):
    layernorm_stage(nc, k, "l2f_ln", k.X, k.XN, k.XNT)
    with ExitStack() as ctx:
        gates = ctx.enter_context(nc.sbuf_tensor("l2f_gates", [P, TILES, 8], F32))
        router_stage(nc, k, "l2f_r", a, k.XNT, a["r2w"], a["r2b"], 8, 2, "logits", 6, gates)
        gated_bias_stage(nc, k, "l2f_b", gates, a["e2b2"], 8)
        moe_stage(nc, k, "l2f_e", k.XNT, a["e2w1"], a["e2w2"], a["e2b1"], gates, 8, 8, True)


def qkv_stage(nc, k, name, w_dram, qkv, width):
    with Stage(nc, name) as st:
        w = st.sb("w", [P, DC, width])
        po = st.ps("po", [P, 4, 512])
        loaded, full, evac = st.sem("loaded"), st.sem("full"), st.sem("evac")
        with nc.Block() as block:
            @block.sync
            def _(sp):
                sp.dma_start(w[:], w_dram.rearrange("(c p) n -> p c n", p=P)).then_inc(loaded, DMA)

            @block.tensor
            def _(pe):
                pe.wait_ge(loaded, DMA)
                for t in range(TILES):
                    if t >= 4:
                        pe.wait_ge(evac, t - 3)
                    for c in range(DC):
                        mm = pe.matmul(po[:, t % 4, 0:width], k.XNT[:, c, t * P:(t + 1) * P], w[:, c, :], start=c == 0, stop=c == DC - 1)
                    mm.then_inc(full, 1)

            @block.scalar
            def _(act):
                for t in range(TILES):
                    act.wait_ge(full, t + 1)
                    act.copy(qkv[:, t, :], po[:, t % 4, 0:width]).then_inc(evac, 1)


def short_attention_stage(nc, k, name, qkv, ao):
    KV, QH = 4, 4
    W = (QH + 2) * HD
    NEG = -3.4028234663852886e38
    PAIRS_CAUSAL = [(s, t) for s in range(B) for t in range(s + 1)]
    with Stage(nc, name) as st:
        prod = st.sb("prod", [P, 2, KV, QH, HD])
        sc = st.sb("sc", [P, TPB, B, B, H])
        m, s, r = (st.sb(n, [P, TPB * B, H]) for n in ("m", "s", "r"))
        step, prod_full, prod_used, shifted, exp_done, p_ready, ao_step = (
            st.sem(n) for n in ("step", "prod_full", "prod_used", "shifted", "exp_done", "p_ready", "ao_step"))
        q5 = qkv[:].rearrange("p (s a) (g f) -> p s a g f", s=B, f=W)
        ao5 = ao.rearrange("p (s a) (g h d) -> p s a g h d", s=B, g=KV, h=QH)
        sc3 = sc[:].rearrange("p a s t h -> p (a s) t h")

        def heads(x):
            return x.unsqueeze(2).broadcast_to([P, KV, QH, HD])

        NP_ = len(PAIRS_CAUSAL)
        with nc.Block() as block:
            @block.gpsimd
            def _(pool):
                pool.sem_inc(prod_used, 2)
                with pool.Fori(0, TPB) as a:
                    for n, (sq, t) in enumerate(PAIRS_CAUSAL):
                        pool.wait_ge(prod_used, NP_ * a + n + 1)
                        pool.sem_inc(ao_step, 1)
                        q = q5[:, sq, bass.ds(a, 1), :, 0:QH * HD].rearrange("p a g (h d) -> p (a g) h d", h=QH)
                        key = q5[:, t, bass.ds(a, 1), :, QH * HD:(QH + 1) * HD].rearrange("p a g d -> p (a g) d")
                        pool.tensor_tensor(prod[:, n % 2], q, heads(key), ALU.mult).then_inc(prod_full, 1)
                pool.wait_ge(p_ready, 1)
                with pool.Fori(0, TPB) as a:
                    for n, (sq, t) in enumerate(PAIRS_CAUSAL):
                        pool.wait_ge(prod_used, NP_ * a + NP_ * TPB + n + 1)
                        pool.sem_inc(ao_step, 1)
                        v = q5[:, t, bass.ds(a, 1), :, (QH + 1) * HD:W].rearrange("p a g d -> p (a g) d")
                        prob = sc[:, bass.ds(a, 1), sq, t, :].rearrange("p a (g h) -> p (a g) h", g=KV)
                        pool.tensor_tensor(prod[:, n % 2], heads(v), prob.unsqueeze(3).broadcast_to([P, KV, QH, HD]),
                                           ALU.mult).then_inc(prod_full, 1)

            @block.scalar
            def _(act):
                act.wait_ge(shifted, 1)
                act.activation(sc3, sc3, ACT.Exp, scale=HD ** -0.5).then_inc(exp_done, 1)

            @block.vector
            def _(dve):
                dve.memset(sc[:], NEG).then_inc(step, 1)
                dve.wait_ge(step, 1)
                with dve.Fori(0, TPB) as a:
                    for n, (sq, t) in enumerate(PAIRS_CAUSAL):
                        dve.wait_ge(prod_full, NP_ * a + n + 1)
                        dve.tensor_reduce(sc[:, bass.ds(a, 1), sq, t, :].rearrange("p a (g h) -> p (a g) h", g=KV),
                                          prod[:, n % 2], AX.X, ALU.add).then_inc(prod_used, 1)
                dve.wait_ge(prod_used, NP_ * TPB + 2)
                do = Chain(dve, step, 1)
                by_head = sc3.rearrange("p n t h -> p n h t")

                def over_keys(x):
                    return x.unsqueeze(2).broadcast_to([P, TPB * B, B, H])

                do(dve.tensor_reduce(m[:], by_head, AX.X, ALU.max))
                dve.tensor_tensor(sc3, sc3, over_keys(m[:]), ALU.subtract).then_inc(shifted, 1)
                dve.wait_ge(exp_done, 1)
                do(dve.tensor_reduce(s[:], by_head, AX.X, ALU.add))
                do(dve.reciprocal(r[:], s[:]))
                dve.tensor_tensor(sc3, sc3, over_keys(r[:]), ALU.mult).then_inc(p_ready, 1)
                with dve.Fori(0, TPB) as a:
                    for n, (sq, t) in enumerate(PAIRS_CAUSAL):
                        dve.wait_ge(prod_full, NP_ * a + NP_ * TPB + n + 1)
                        out = ao5[:, sq, bass.ds(a, 1)].rearrange("p a g h d -> p (a g h d)")
                        src = prod[:, n % 2].rearrange("p g h d -> p (g h d)")
                        if t == 0:
                            dve.tensor_scalar(out, src, 1.0, None, ALU.mult).then_inc(prod_used, 1)
                        else:
                            dve.wait_ge(prod_used, NP_ * a + NP_ * TPB + n + 2)
                            dve.tensor_tensor(out, out, src, ALU.add).then_inc(prod_used, 1)


def expert_layer_1(nc, k, a):
    E, CAP = 8, 640
    GATE = 5
    with ExitStack() as ctx:
        y = ctx.enter_context(nc.sbuf_tensor("l1f_y", [P, TILES, D], F32))
        layernorm_stage(nc, k, "l1f_ln", k.X, k.XN, k.XNT)
        layernorm_stage(nc, k, "l1f_ln1", k.XN, y, k.XNT, affine=(a["ln1w"], a["ln1b"]))
        with ExitStack() as inner:
            qkv = inner.enter_context(nc.sbuf_tensor("l1f_qkv", [P, TILES, 384], F32))
            qkv_stage(nc, k, "l1f_qkv_s", a["qkvw"], qkv, 384)
            short_attention_stage(nc, k, "l1f_sa", qkv, y[:])
        transpose_stage(nc, k, "l1f_t", y, k.XNT)
        project_add_stage(nc, k, "l1f_pr", a["projw"], k.XN)
        layernorm_stage(nc, k, "l1f_ln2", k.XN, y, k.XNT, affine=(a["ln2w"], a["ln2b"]))
        gates = ctx.enter_context(nc.sbuf_tensor("l1f_gates", [P, TILES, E], F32))
        router_stage(nc, k, "l1f_r", a, k.XNT, a["r1w"], a["zero_rows"][:, 0:E], E, 2, "probs", GATE, gates, capacity=CAP)
        add_scaled_stage(nc, k, "l1f_x", k.XN, GATE)
        moe_stage(nc, k, "l1f_e", k.XNT, a["e1w1"], a["e1w2"], None, gates, E, 4, False)


def project_add_stage(nc, k, name, w_dram, acc):
    with Stage(nc, name) as st:
        w = st.sb("w", [P, DC, D])
        po = st.ps("po", [P, 4, 512])
        loaded, full, evac = st.sem("loaded"), st.sem("full"), st.sem("evac")
        with nc.Block() as block:
            @block.sync
            def _(sp):
                sp.dma_start(w[:], w_dram.rearrange("(c p) n -> p c n", p=P)).then_inc(loaded, DMA)

            @block.tensor
            def _(pe):
                pe.wait_ge(loaded, DMA)
                for t in range(TILES):
                    if t >= 4:
                        pe.wait_ge(evac, t - 3)
                    for c in range(DC):
                        mm = pe.matmul(po[:, t % 4, 0:D], k.XNT[:, c, t * P:(t + 1) * P], w[:, c, :], start=c == 0, stop=c == DC - 1)
                    mm.then_inc(full, 1)

            @block.vector
            def _(dve):
                for t in range(TILES):
                    dve.wait_ge(full, t + 1)
                    dve.tensor_tensor(acc[:, t, :], po[:, t % 4, 0:D], acc[:, t, :], ALU.add).then_inc(evac, 1)


def add_scaled_stage(nc, k, name, src, gate):
    with Stage(nc, name) as st:
        done = st.sem("done")
        with nc.Block() as block:
            @block.vector
            def _(dve):
                dve.scalar_tensor_tensor(out=k.X[:].rearrange("p t d -> p (t d)"), in0=src.rearrange("p t d -> p (t d)"),
                                         scalar=k.tg[:, gate:gate + 1], in1=k.X[:].rearrange("p t d -> p (t d)"),
                                         op0=ALU.mult, op1=ALU.add).then_inc(done, 1)
                dve.wait_ge(done, 1)


def single_head_stage(nc, k, name, qT, kT, v, scale, out, gate=None):
    with Stage(nc, name) as st:
        qb = [st.sb(f"qb{u}", [P, DC, S]) for u in range(2)]
        prob = st.sb("prob", [P, 2, S])
        pT = st.sb("pT", [P, 2, TPB, P])
        negm = st.sb("negm", [P, 2])
        nbias = st.sb("nbias", [P, 2])
        psum_row = st.sb("sum", [P, 2])
        rinv = st.sb("rinv", [P, 2])
        ps_s = st.ps("ps_s", [P, 2, S])
        ps_t = st.ps("ps_t", [P, 2, TPB, P])
        ps_o = st.ps("ps_o", [P, 2, 512])
        (qb_ready, s_full, negm_done, nbias_done, exp_done, t_full, t_evac, o_full, o_evac, r_step, tick) = (
            st.sem(n) for n in ("qb_ready", "s_full", "negm_done", "nbias_done", "exp_done", "t_full", "t_evac",
                                "o_full", "o_evac", "r_step", "tick"))
        PER = 2 * TPB
        with nc.Block() as block:
            @block.gpsimd
            def _(pool):
                with pool.Fori(0, B // 2) as it:
                    for u in range(2):
                        pool.wait_ge(s_full, PER * it)
                        pool.sem_inc(tick, 1)
                        pool.tensor_copy(qb[u][:], qT[:, :, bass.ds((2 * it + u) * S, S)]).then_inc(qb_ready, 1)

            @block.tensor
            def _(pe):
                with pe.Fori(0, B // 2) as it:
                    def scores(n):
                        u, qt = divmod(n, TPB)
                        if qt == 0:
                            pe.wait_ge(qb_ready, 2 * it + u + 1)
                        pe.wait_ge(exp_done, PER * it + n + 1)
                        for c in range(DC):
                            mm = pe.matmul(ps_s[:, n % 2, :], qb[u][:, c, qt * P:(qt + 1) * P],
                                           kT[:, c, bass.ds((2 * it + u) * S, S)], start=c == 0, stop=c == DC - 1)
                        mm.then_inc(s_full, 1)

                    scores(0)
                    for n in range(PER):
                        if n + 1 < PER:
                            scores(n + 1)
                        pe.wait_ge(exp_done, PER * it + n + 1 + 2)
                        pe.wait_ge(t_evac, PER * it + n + 1)
                        for kt in range(TPB):
                            mm = pe.transpose(ps_t[:, n % 2, kt, :], prob[:, n % 2, kt * P:(kt + 1) * P], k.ident[:])
                        mm.then_inc(t_full, 1)
                        pe.wait_ge(t_evac, PER * it + n + 1 + 2)
                        pe.wait_ge(o_evac, PER * it + n + 1)
                        for kt in range(TPB):
                            mm = pe.matmul(ps_o[:, n % 2, 0:D], pT[:, n % 2, kt, :],
                                           v[:, bass.ds((2 * it + n // TPB) * TPB + kt, 1), :], start=kt == 0, stop=kt == TPB - 1)
                        mm.then_inc(o_full, 1)

            @block.scalar
            def _(act):
                act.sem_inc(exp_done, 2)
                with act.Fori(0, B // 2) as it:
                    for n in range(PER):
                        act.wait_ge(nbias_done, PER * it + n + 1)
                        act.wait_ge(t_full, PER * it + n)
                        act.wait_ge(r_step, PER * it + n)
                        act.activation(prob[:, n % 2, :], ps_s[:, n % 2, :], ACT.Exp, bias=nbias[:, n % 2:n % 2 + 1], scale=scale,
                                       accum_out=psum_row[:, n % 2:n % 2 + 1]).then_inc(exp_done, 1)

            @block.vector
            def _(dve):
                dve.sem_inc(t_evac, 2)
                dve.sem_inc(o_evac, 2)
                dve.sem_inc(r_step, 1)
                with dve.Fori(0, B // 2) as it:
                    def row_max(n):
                        dve.wait_ge(s_full, PER * it + n + 1)
                        dve.wait_ge(nbias_done, PER * it + n)
                        dve.tensor_reduce(negm[:, n % 2:n % 2 + 1], ps_s[:, n % 2, :], AX.X, ALU.max, negate=True).then_inc(negm_done, 1)
                        dve.wait_ge(negm_done, PER * it + n + 1)
                        dve.wait_ge(exp_done, PER * it + n + 1)
                        dve.tensor_scalar(nbias[:, n % 2:n % 2 + 1], negm[:, n % 2:n % 2 + 1], scale, None, ALU.mult).then_inc(nbias_done, 1)

                    def finish(n):
                        dve.wait_ge(exp_done, PER * it + n + 1 + 2)
                        dve.wait_ge(o_evac, PER * it + n + 2)
                        dve.reciprocal(rinv[:, n % 2:n % 2 + 1], psum_row[:, n % 2:n % 2 + 1]).then_inc(r_step, 1)
                        dve.wait_ge(o_full, PER * it + n + 1)
                        dve.wait_ge(r_step, PER * it + n + 2)
                        tile = bass.ds(PER * it + n, 1)
                        o = out[:, tile, :].rearrange("p t d -> p (t d)")
                        if gate is None:
                            dve.tensor_scalar(o, ps_o[:, n % 2, 0:D], rinv[:, n % 2:n % 2 + 1], None, ALU.mult).then_inc(o_evac, 1)
                        else:
                            dve.scalar_tensor_tensor(out=o, in0=ps_o[:, n % 2, 0:D], scalar=rinv[:, n % 2:n % 2 + 1], in1=o,
                                                     op0=ALU.mult, op1=ALU.add).then_inc(o_evac, 1)

                    row_max(0)
                    for n in range(PER):
                        if n + 1 < PER:
                            row_max(n + 1)
                        dve.wait_ge(t_full, PER * it + n + 1)
                        dve.wait_ge(o_full, PER * it + (n - 1 if n else 0))
                        dve.tensor_copy(pT[:, n % 2], ps_t[:, n % 2]).then_inc(t_evac, 1)
                        finish(n)


def feature_major_stage(nc, k, name, w_dram, bias_dram, dst_T):
    with Stage(nc, name) as st:
        w = st.sb("w", [P, DC, D])
        bias = st.sb("bias", [P, DC])
        po = st.ps("po", [P, 4, 512])
        loaded, full, evac = st.sem("loaded"), st.sem("full"), st.sem("evac")
        with nc.Block() as block:
            @block.sync
            def _(sp):
                sp.dma_start(w[:], w_dram.rearrange("(c p) n -> p c n", p=P)).then_inc(loaded, DMA)
                sp.dma_start(bias[:], bias_dram).then_inc(loaded, DMA)

            @block.tensor
            def _(pe):
                pe.wait_ge(loaded, 2 * DMA)
                for n in range(DC * B):
                    m, b = divmod(n, B)
                    if n >= 4:
                        pe.wait_ge(evac, n - 3)
                    for c in range(DC):
                        mm = pe.matmul(po[:, n % 4, :], w[:, c, m * P:(m + 1) * P], k.XNT[:, c, b * S:(b + 1) * S], start=c == 0, stop=c == DC - 1)
                    mm.then_inc(full, 1)

            @block.scalar
            def _(act):
                act.wait_ge(loaded, 2 * DMA)
                for n in range(DC * B):
                    m, b = divmod(n, B)
                    act.wait_ge(full, n + 1)
                    act.activation(dst_T[:, m, b * S:(b + 1) * S], po[:, n % 4, :], ACT.Identity, bias=bias[:, m:m + 1]).then_inc(evac, 1)


def fuse_stage(nc, k, name, w_dram, bias_dram, oT, gate):
    with Stage(nc, name) as st:
        w = st.sb("w", [P, 2 * DC, D])
        bias = st.sb("bias", [P, D])
        po = st.ps("po", [P, 4, 512])
        loaded, full, evac, step = st.sem("loaded"), st.sem("full"), st.sem("evac"), st.sem("step")
        with nc.Block() as block:
            @block.sync
            def _(sp):
                sp.dma_start(w[:], w_dram.rearrange("(c p) n -> p c n", p=P)).then_inc(loaded, DMA)
                sp.dma_start(bias[:], bias_dram).then_inc(loaded, DMA)

            @block.tensor
            def _(pe):
                pe.wait_ge(loaded, 2 * DMA)
                for t in range(TILES):
                    if t >= 4:
                        pe.wait_ge(evac, t - 3)
                    for c in range(2 * DC):
                        src = k.XNT if c < DC else oT
                        mm = pe.matmul(po[:, t % 4, 0:D], src[:, c % DC, t * P:(t + 1) * P], w[:, c, :], start=c == 0, stop=c == 2 * DC - 1)
                    mm.then_inc(full, 1)

            @block.vector
            def _(dve):
                dve.wait_ge(loaded, 2 * DMA)
                do = Chain(dve, step)
                do(dve.tensor_scalar(bias[:], bias[:], k.tg[:, gate:gate + 1], None, ALU.mult))
                do(dve.tensor_tensor(k.X[:], k.X[:], bias[:].unsqueeze(1).broadcast_to([P, TILES, D]), ALU.add))
                for t in range(TILES):
                    dve.wait_ge(full, t + 1)
                    dve.scalar_tensor_tensor(out=k.X[:, t, :], in0=po[:, t % 4, 0:D], scalar=k.tg[:, gate:gate + 1],
                                             in1=k.X[:, t, :], op0=ALU.mult, op1=ALU.add).then_inc(evac, 1)


def knowledge_layer(nc, k, a):
    layernorm_stage(nc, k, "l2x_ln", k.X, k.XN, k.XNT)
    with ExitStack() as ctx:
        def sb(name):
            return ctx.enter_context(nc.sbuf_tensor("l2x_" + name, [P, DC, B * S], F32))
        qT, ctxT, v = sb("qT"), sb("ctxT"), ctx.enter_context(nc.sbuf_tensor("l2x_v", [P, TILES, D], F32))
        with Stage(nc, "l2x_ld") as st:
            loaded = st.sem("loaded")
            with nc.Block() as block:
                @block.sync
                def _(sp):
                    sp.dma_start(ctxT[:], a["ctxT"].rearrange("(c p) n -> p c n", p=P)).then_inc(loaded, DMA)
                    sp.dma_start(v[:], a["ctx"].rearrange("(t p) d -> p t d", p=P)).then_inc(loaded, DMA)
                    sp.wait_ge(loaded, 2 * DMA)
        feature_major_stage(nc, k, "l2x_q", a["w2x1"], a["b2x1"], qT)
        single_head_stage(nc, k, "l2x_a", qT, ctxT, v, D ** -0.5, k.XN)
        transpose_stage(nc, k, "l2x_t", k.XN, qT)
        fuse_stage(nc, k, "l2x_f", a["w2x2"], a["b2x2"], qT, 2)


def tree_stage(nc, k, name, a, node_w, node_b, sel_T, sel_Tb):
    NODES, LEAVES = 15, 16
    with Stage(nc, name) as st:
        w = st.sb("w", [P, DC, NODES])
        nb = st.sb("nb", [P, NODES])
        bit = st.sb("bit", [P, TILES, NODES])
        ind = [st.sb(f"ind{lv}", [P, TILES, 2 ** (lv + 1)]) for lv in range(4)]
        ps = st.ps("ps_n", [P, TILES, NODES])
        tp = st.ps("tp", [LEAVES, TILES, P])
        loaded, full, step, sel_done, t_full = (st.sem(n) for n in ("loaded", "full", "step", "sel_done", "t_full"))
        with nc.Block() as block:
            @block.sync
            def _(sp):
                sp.dma_start(w[:], node_w.rearrange("(c p) e -> p c e", p=P)).then_inc(loaded, DMA)
                sp.dma_start(nb[:], node_b).then_inc(loaded, DMA)

            @block.tensor
            def _(pe):
                pe.wait_ge(loaded, 2 * DMA)
                for t in range(TILES):
                    for c in range(DC):
                        mm = pe.matmul(ps[:, t, :], k.XNT[:, c, t * P:(t + 1) * P], w[:, c, :], start=c == 0, stop=c == DC - 1)
                mm.then_inc(full, 1)
                pe.wait_ge(sel_done, 1)
                for t in range(TILES):
                    mm = pe.transpose(tp[:, t, :], ind[3][:, t, :], k.ident[:])
                mm.then_inc(t_full, 1)

            @block.vector
            def _(dve):
                do = Chain(dve, step)
                dve.wait_ge(loaded, 2 * DMA)
                dve.wait_ge(full, 1)
                do(dve.tensor_tensor(bit[:], ps[:], nb[:].unsqueeze(1).broadcast_to([P, TILES, NODES]), ALU.add))
                do(dve.tensor_scalar(bit[:], bit[:], 0.0, None, ALU.is_ge))
                do(dve.tensor_copy(ind[0][:, :, 1:2], bit[:, :, 0:1]))
                do(dve.tensor_scalar(ind[0][:, :, 0:1], bit[:, :, 0:1], -1.0, 1.0, ALU.mult, ALU.add))
                for lv in range(1, 4):
                    n = 2 ** lv
                    kids = ind[lv][:].rearrange("p t (n two) -> p t n two", two=2)
                    do(dve.tensor_tensor(kids[:, :, :, 1], ind[lv - 1][:], bit[:, :, n - 1:2 * n - 1], ALU.mult))
                    do(dve.tensor_tensor(kids[:, :, :, 0], ind[lv - 1][:], kids[:, :, :, 1], ALU.subtract))
                dve.sem_inc(sel_done, 1)
                dve.wait_ge(t_full, 1)
                do(dve.tensor_copy(sel_T, tp[:].rearrange("l t p -> l (t p)")))
                do(dve.tensor_copy(sel_Tb, sel_T))


def leaves_stage(nc, k, name, a, w1, b1, w2, b2, sel_T, sel_Tb, dst, feature_major):
    FC = 8
    LEAVES = 16
    with Stage(nc, name) as st:
        w1s = st.sb("w1", [P, DC, FC * P])
        w2s = st.sb("w2", [P, FC, D])
        b1s = st.sb("b1", [P, FC])
        b2s = st.sb("b2", [LEAVES, D])
        spread = st.sb("spread", [LEAVES, FC * P], BF16)
        spread_f = st.sb("spread_f", [LEAVES, FC * P])
        selb = st.sb("selb", [LEAVES, S])
        relu = st.sb("relu", [P, 2, S])
        ht = st.sb("ht", [P, FC, S])
        ph = st.ps("ph", [P, 2, S])
        pm = st.ps("pm", [P, 2, S])
        po = st.ps("po", [P, 4, 512])
        loaded, spread_done, selb_ready, h_full, relu_done, h_ready, o_full, o_evac, tick = (
            st.sem(n) for n in ("loaded", "spread_done", "selb_ready", "h_full", "relu_done", "h_ready", "o_full", "o_evac", "tick"))
        NO = DC if feature_major else TPB
        with nc.Block() as block:
            @block.sync
            def _(sp):
                for c in range(DC):
                    sp.dma_start(w1s[:, c, :].rearrange("p (l h) -> p l h", l=LEAVES),
                                 w1[:, c * P:(c + 1) * P, :].rearrange("l p h -> p l h")).then_inc(loaded, DMA)
                sp.dma_start(w2s[:], w2.rearrange("(j two) h n -> (two h) j n", two=2)).then_inc(loaded, DMA)
                sp.dma_start(b1s[:], b1).then_inc(loaded, DMA)
                sp.dma_start(b2s[:], b2).then_inc(loaded, DMA)
                sp.dma_start(spread_f[:], a["spread"]).then_inc(loaded, DMA)

            @block.gpsimd
            def _(pool):
                with pool.Fori(0, B) as b:
                    pool.wait_ge(o_full, NO * b)
                    pool.sem_inc(tick, 1)
                    pool.tensor_copy(selb[:], sel_T[:, bass.ds(b * S, S)]).then_inc(selb_ready, 1)

            @block.tensor
            def _(pe):
                pe.wait_ge(loaded, 6 * DMA)
                pe.wait_ge(spread_done, 1)
                with pe.Fori(0, B) as b:
                    row = bass.ds(b * S, S)
                    for j in range(FC):
                        pe.wait_ge(h_ready, FC * b + j + 1)
                        for c in range(DC):
                            pe.matmul(ph[:, j % 2, :], w1s[:, c, j * P:(j + 1) * P], k.XNT[:, c, row], start=c == 0, stop=c == DC - 1)
                        pe.matmul(pm[:, j % 2, :], spread[:, j * P:(j + 1) * P], sel_Tb[:, row], start=True, stop=True).then_inc(h_full, 1)
                    pe.wait_ge(selb_ready, b + 1)
                    for n in range(NO):
                        pe.wait_ge(h_ready, FC * b + FC + 2)
                        pe.wait_ge(o_evac, NO * b + n + 1)
                        for j in range(FC):
                            if feature_major:
                                pe.matmul(po[:, n, :], w2s[:, j, n * P:(n + 1) * P], ht[:, j, :], start=j == 0, stop=False)
                            else:
                                pe.matmul(po[:, n, 0:D], ht[:, j, n * P:(n + 1) * P], w2s[:, j, :], start=j == 0, stop=False)
                        if feature_major:
                            mm = pe.matmul(po[:, n, :], b2s[:, n * P:(n + 1) * P], selb[:], start=False, stop=True)
                        else:
                            mm = pe.matmul(po[:, n, 0:D], selb[:, n * P:(n + 1) * P], b2s[:], start=False, stop=True)
                        mm.then_inc(o_full, 1)

            @block.scalar
            def _(act):
                act.sem_inc(o_evac, NO)
                act.wait_ge(loaded, 6 * DMA)
                with act.Fori(0, B) as b:
                    for j in range(FC):
                        act.wait_ge(h_full, FC * b + j + 1)
                        act.wait_ge(h_ready, FC * b + j + 1)
                        act.activation(relu[:, j % 2, :], ph[:, j % 2, :], ACT.Relu, bias=b1s[:, j:j + 1]).then_inc(relu_done, 1)
                    for n in range(NO):
                        act.wait_ge(o_full, NO * b + n + 1)
                        act.sem_inc(tick, 1)
                        if feature_major:
                            act.copy(dst[:, n, bass.ds(b * S, S)], po[:, n, :]).then_inc(o_evac, 1)
                        else:
                            act.copy(dst[:, bass.ds(TPB * b + n, 1), :].rearrange("p t d -> p (t d)"), po[:, n, 0:D]).then_inc(o_evac, 1)

            @block.vector
            def _(dve):
                dve.sem_inc(h_ready, 2)
                dve.wait_ge(loaded, 6 * DMA)
                dve.tensor_copy(spread[:], spread_f[:]).then_inc(spread_done, 1)
                with dve.Fori(0, B) as b:
                    for j in range(FC):
                        dve.wait_ge(relu_done, FC * b + j + 1)
                        dve.tensor_tensor(ht[:, j, :], pm[:, j % 2, :], relu[:, j % 2, :], ALU.mult).then_inc(h_ready, 1)


def scale_values_stage(nc, k, name, v, gate):
    with Stage(nc, name) as st:
        done = st.sem("done")
        with nc.Block() as block:
            @block.vector
            def _(dve):
                dve.tensor_scalar(v, v, k.tg[:, gate:gate + 1], None, ALU.mult).then_inc(done, 1)
                dve.wait_ge(done, 1)


def tree_layer(nc, k, a):
    layernorm_stage(nc, k, "l3f_ln", k.X, k.XN, k.XNT)
    with ExitStack() as ctx:
        def sb(name, shape, dt=F32):
            return ctx.enter_context(nc.sbuf_tensor("l3f_" + name, shape, dt))
        qT, kT, v = sb("qT", [P, DC, B * S]), sb("kT", [P, DC, B * S]), sb("v", [P, TILES, D])
        with ExitStack() as inner:
            sel_T = inner.enter_context(nc.sbuf_tensor("l3f_selT", [16, B * S], F32))
            sel_Tb = inner.enter_context(nc.sbuf_tensor("l3f_selTb", [16, B * S], BF16))
            for x, dst in (("q", qT), ("k", kT), ("v", v)):
                tree_stage(nc, k, f"l3f_{x}t", a, a[f"t{x}nw"], a[f"t{x}nb"], sel_T[:], sel_Tb[:])
                leaves_stage(nc, k, f"l3f_{x}l", a, a[f"t{x}w1"], a[f"t{x}b1"], a[f"t{x}w2"], a[f"t{x}b2"], sel_T, sel_Tb, dst, x != "v")
        scale_values_stage(nc, k, "l3f_g", v[:], 7)
        single_head_stage(nc, k, "l3f_a", qT, kT, v, D ** -0.5, k.X, gate=7)


def more_stages(nc, k, a):
    return [
        lambda: expert_layer_0(nc, k, a),
        lambda: attention_layer(nc, k, "l1x", a, a["w1q"], a["w1k"], a["w1v"], a["zero_col"], a["zero_col"], a["zero_rows"],
                                a["w1o"], a["b1o"], D ** -0.5, 1, mask=(a["m1"], a["m1T"], True)),
        lambda: expert_layer_1(nc, k, a),
        lambda: knowledge_layer(nc, k, a),
        lambda: expert_layer_2(nc, k, a),
        lambda: attention_layer(nc, k, "l3x", a, a["w3q"], a["w3k"], a["w3v"], a["b3q"], a["b3k"], a["b3v"], a["w3o"],
                                a["b3o"], HD ** -0.5, 3, tril2=a["tril2"]),
        lambda: tree_layer(nc, k, a),
    ]


def more_layout(n, all_rows, columns, T):
    import numpy as np
    f32 = np.float32
    a = {f"ranks{E}": all_rows(np.arange(E, 0, -1).astype(f32)) for E in (8, 16)}
    a["before"] = np.triu(np.ones((P, P), f32), 1)
    a |= {"r0w": T(n["L0_ffn_router_w"]), "r0b": all_rows(n["L0_ffn_router_b"]), "e0w": n["L0_ffn_expert_w"]}
    a |= {"r2w": T(n["L2_ffn_router_w"]), "r2b": all_rows(n["L2_ffn_router_b"]), "e2w1": T(n["L2_ffn_w1"]),
          "e2w2": T(n["L2_ffn_w2"]), "e2b1": n["L2_ffn_b1"].reshape(8, 16, P).transpose(2, 0, 1), "e2b2": n["L2_ffn_b2"]}
    p = "L1_ffn_"
    for x in ("ln1", "ln2"):
        a |= {x + "w": all_rows(n[p + x + "_weight"]), x + "b": all_rows(n[p + x + "_bias"])}
    a |= {"qkvw": T(n[p + "qkv_weight"]), "projw": T(n[p + "proj_weight"]), "r1w": n[p + "router_weight"],
          "e1w1": n[p + "moe_w1"], "e1w2": n[p + "moe_w2"]}
    p = "L2_xattn_"
    a |= {"w2x1": T(n[p + "w1_w"]), "b2x1": columns(n[p + "w1_b"]), "w2x2": T(n[p + "w2_w"]), "b2x2": all_rows(n[p + "w2_b"])}
    for x in "qkv":
        p = f"L3_ffn_{x}_"
        a |= {f"t{x}nw": T(n[p + "node_w"]), f"t{x}nb": all_rows(n[p + "node_b"]), f"t{x}w1": n[p + "w1"],
              f"t{x}b1": columns(n[p + "b1"].reshape(-1)), f"t{x}w2": n[p + "w2"], f"t{x}b2": n[p + "b2"]}
    a["spread"] = np.kron(np.eye(16, dtype=f32), np.ones((1, 64), f32))
    return a


_OUT = (B, S, D)


def build(nc, a, out, stop=99):
    k = Held()
    with ExitStack() as ctx:
        k.X = ctx.enter_context(nc.sbuf_tensor("X", [P, TILES, D], F32))
        norm = ctx.enter_context(nc.sbuf_tensor("norm", [P, 2 * TILES * D], F32))
        k.XN = norm[:, 0:TILES * D].rearrange("p (t d) -> p t d", t=TILES)
        k.XNT = norm[:, TILES * D:].rearrange("p (c n) -> p c n", c=DC)
        k.ATN = norm[:].rearrange("p (g n) -> p g n", g=B * GROUPS)
        k.tg = ctx.enter_context(nc.sbuf_tensor("tg", [P, 8], F32))
        k.ident = ctx.enter_context(nc.sbuf_tensor("ident_f32", [P, P], F32))
        k.ident_bf = ctx.enter_context(nc.sbuf_tensor("ident_bf", [P, P], BF16))
        k.qk_dram = nc.dram_tensor("qk_parts", [2, 3, B * GROUPS, GH, HD, S], BF16, kind="Internal").ap()
        load_stage(nc, k, a)
        stages = [
            lambda: attention_layer(nc, k, "l0x", a, a["w0q"], a["w0k"], a["w0v"], a["b0q"], a["b0k"], a["b0v"], a["w0o"],
                                    a["b0o"], HD ** -0.5, 0, mask=(a["m0"], a["m0T"], False)),
        ] + more_stages(nc, k, a)
        for n, stage in enumerate(stages):
            if n in range(*(stop if isinstance(stop, tuple) else (0, stop))):
                stage()
        store_stage(nc, k, out)


def store_stage(nc, k, out):
    with Stage(nc, "store") as st:
        stored = st.sem("stored")
        with nc.Block() as block:
            @block.sync
            def _(sp):
                sp.dma_start(out.rearrange("b (t p) d -> p (b t) d", p=P), k.X[:]).then_inc(stored, DMA)
                sp.wait_ge(stored, DMA)


def lay_out(v):
    import numpy as np
    n = {name: np.asarray(x) for name, x in v.items()}
    f32 = np.float32

    def all_rows(x):
        return np.ascontiguousarray(np.broadcast_to(x.reshape(1, -1), (P, x.size)))

    def columns(x):
        return np.ascontiguousarray(x.reshape(-1, P).T)

    def heads(w):
        full = np.zeros((H, HD, H, HD), w.dtype)
        for h in range(H):
            full[h, :, h, :] = w.T
        return full.reshape(D, D)

    def strips(w):
        full = np.zeros((GH, STRIP, GROUPS, w.shape[1]), w.dtype)
        full[:, :HD] = w.reshape(GROUPS, GH, HD, -1).transpose(1, 2, 0, 3)
        return full.reshape(P, GROUPS, -1)

    def T(x):
        return np.ascontiguousarray(np.swapaxes(x, -1, -2))

    selsum = np.zeros((P, P), f32)
    for i in range(GH):
        selsum[STRIP * i + HD, STRIP * i:STRIP * (i + 1)] = 1.0
    zero = np.zeros(D, f32)
    m0 = n["mask_SxS2_bk1"]
    m1 = n["mask_Bx1xSxS2_ik1"].reshape(B, S, S)
    a = {
        "x": n["x"].reshape(B * S, D),
        "ctx": n["ctx_1024"].reshape(B * S, D),
        "ctxT": T(n["ctx_1024"].reshape(B * S, D)),
        "gates": all_rows(np.concatenate([n["g_xattn"], n["g_ffn"]])),
        "ident": np.eye(P, dtype=f32),
        "selsum": selsum,
        "tril2": (1.0 + np.triu(np.ones((P, P)))).astype(f32),
        "m0": m0, "m0T": T(m0),
        "m1": m1.reshape(B * S, S), "m1T": T(m1).reshape(B * S, S),
    }
    for layer in (0, 3):
        p = f"L{layer}_xattn_"
        a |= {f"w{layer}q": n[p + "Wq"], f"w{layer}k": n[p + "Wk"], f"w{layer}v": n[p + "Wv"],
              f"b{layer}q": columns(n[p + "bq"]), f"b{layer}k": columns(n[p + "bk"]), f"b{layer}v": all_rows(n[p + "bv"]),
              f"w{layer}o": strips(n[p + "Wo"]), f"b{layer}o": all_rows(n[p + "bo"])}
    p = "L1_xattn_"
    a |= {"w1q": heads(n[p + "Wq"]), "w1k": heads(n[p + "Wk"]), "w1v": heads(n[p + "Wv"]), "zero_col": columns(zero),
          "zero_rows": all_rows(zero), "w1o": strips(T(n[p + "Wo"])), "b1o": all_rows(n[p + "bo"])}
    a |= more_layout(n, all_rows, columns, T)
    return {name: np.ascontiguousarray(x) for name, x in a.items()}


def kernel(**inputs):
    import concourse.bacc as bacc
    from concourse.bass_utils import run_bass_kernel_spmd

    nc = bacc.Bacc("TRN2", target_bir_lowering=False, num_devices=1)
    arrays = lay_out(inputs)
    args = {name: nc.dram_tensor(name, x.shape, mybir.dt.from_np(x.dtype), kind="ExternalInput").ap()
            for name, x in arrays.items()}
    out = nc.dram_tensor("out", _OUT, F32, kind="ExternalOutput").ap()
    build(nc, args, out)
    return run_bass_kernel_spmd(nc, [arrays], core_ids=[0]).results[0]["out"]
```

```python
from contextlib import ExitStack

import concourse.bass as bass
from concourse import mybir

F32 = mybir.dt.float32
BF16 = mybir.dt.bfloat16
U32 = mybir.dt.uint32
ALU = mybir.AluOpType
ACT = mybir.ActivationFunctionType
AX = mybir.AxisListType

P = 128
B, S, D = 4, 512, 256
TILES = B * S // P
TPB = S // P
DC = D // P
H, HD = 16, 16
GH = 4
GROUPS = H // GH
STRIP = 32
LN_EPS = 1e-5
MASKED = -(2.0 ** 100)
Q_PART = (0, 0, 1, 1, 0, 2)
K_PART = (0, 1, 0, 1, 2, 0)
PAIRS = len(Q_PART)
STACK = PAIRS * HD
MROWS = 2
CAPACITY = 640
GROUP = 256
FILL_ROWS = 24 * GROUP
DMA = 16


class Stage:

    def __init__(self, nc, name):
        self.nc, self.name, self.ctx, self.sems = nc, name, ExitStack(), []

    def __enter__(self):
        return self

    def __exit__(self, *exc):
        if exc[0] is None:
            self.nc.clear_and_free_semaphores(self.sems)
            self.nc.all_engine_barrier()
        self.ctx.close()

    def sb(self, name, shape, dt=F32):
        return self.ctx.enter_context(self.nc.sbuf_tensor(f"{self.name}_{name}", shape, dt))

    def ps(self, name, shape, dt=F32):
        return self.ctx.enter_context(self.nc.psum_tensor(f"{self.name}_{name}", shape, dt))

    def sem(self, name):
        s = self.nc.alloc_semaphore(f"{self.name}_{name}")
        self.sems.append(s)
        return s


class Held:
    pass


def at(i, n=1):
    return slice(i, i + n) if isinstance(i, int) else bass.ds(i, n)


def load_stage(nc, k, a):
    with Stage(nc, "load") as st:
        loaded, tanh_done, cast_done = st.sem("loaded"), st.sem("tanh_done"), st.sem("cast_done")
        graw = st.sb("graw", [P, 8])
        with nc.Block() as block:
            @block.sync
            def _(sp):
                sp.dma_start(k.X[:], a["x"].rearrange("(t p) d -> p t d", p=P)).then_inc(loaded, DMA)
                sp.dma_start(graw[:], a["gates"]).then_inc(loaded, DMA)
                sp.dma_start(k.ident[:], a["ident"]).then_inc(loaded, DMA)
                sp.wait_ge(loaded, 3 * DMA)

            @block.scalar
            def _(act):
                act.wait_ge(loaded, 3 * DMA)
                act.activation(k.tg[:], graw[:], ACT.Tanh).then_inc(tanh_done, 1)
                act.wait_ge(tanh_done, 1)

            @block.vector
            def _(dve):
                dve.wait_ge(loaded, 3 * DMA)
                dve.tensor_copy(k.ident_bf[:], k.ident[:]).then_inc(cast_done, 1)
                dve.wait_ge(cast_done, 1)


def layernorm_stage(nc, k, name, src, dst, dst_T, affine=None):
    with Stage(nc, name) as st:
        stats = st.sb("stats", [P, TILES, 6])
        mv = st.sb("mv", [P, TILES, 2])
        std = st.sb("std", [P, TILES])
        rstd = st.sb("rstd", [P, TILES])
        shift = st.sb("shift", [P, TILES])
        eps = st.sb("eps", [P, 1])
        wb = st.sb("wb", [P, 2, D]) if affine else None
        tp = st.ps("tp", [P, 4, 512])
        stat_step, aggr_done, std_done = st.sem("stat_step"), st.sem("aggr_done"), st.sem("std_done")
        scale_step, norm_done, tp_full = st.sem("scale_step"), st.sem("norm_done"), st.sem("tp_full")
        act_evac, dve_evac, wb_loaded = st.sem("act_evac"), st.sem("dve_evac"), st.sem("wb_loaded")
        norm_per_tile = 3 if affine else 1
        with nc.Block() as block:
            if affine:
                @block.sync
                def _(sp):
                    for j in range(2):
                        sp.dma_start(wb[:, j, :], affine[j]).then_inc(wb_loaded, DMA)

            @block.vector
            def _(dve):
                dve.memset(eps[:], LN_EPS).then_inc(stat_step, 1)
                for t in range(TILES):
                    dve.bn_stats(stats[:, t, :], src[:, t, :]).then_inc(stat_step, 1)
                for t in range(TILES):
                    dve.wait_ge(stat_step, t + 2)
                    dve.bn_aggr(mv[:, t, :], stats[:, t, :]).then_inc(aggr_done, 1)
                dve.wait_ge(std_done, 1)
                dve.reciprocal(rstd[:], std[:]).then_inc(scale_step, 1)
                dve.wait_ge(scale_step, 1)
                dve.scalar_tensor_tensor(out=shift[:], in0=mv[:, :, 0], scalar=-1.0, in1=rstd[:],
                                         op0=ALU.mult, op1=ALU.mult).then_inc(scale_step, 1)
                dve.wait_ge(scale_step, 2)
                if affine:
                    dve.wait_ge(wb_loaded, 2 * DMA)
                for t in range(TILES):
                    dve.tensor_scalar(dst[:, t, :], src[:, t, :], rstd[:, t:t + 1], shift[:, t:t + 1],
                                      ALU.mult, ALU.add).then_inc(norm_done, 1)
                    if affine:
                        dve.wait_ge(norm_done, 3 * t + 1)
                        dve.tensor_tensor(dst[:, t, :], dst[:, t, :], wb[:, 0, :], ALU.mult).then_inc(norm_done, 1)
                        dve.wait_ge(norm_done, 3 * t + 2)
                        dve.tensor_tensor(dst[:, t, :], dst[:, t, :], wb[:, 1, :], ALU.add).then_inc(norm_done, 1)
                for n in range(1, DC * B, 2):
                    dve.wait_ge(tp_full, n + 1)
                    dve.tensor_copy(dst_T[:, n % DC, (n // DC) * S:(n // DC + 1) * S], tp[:, n % 4, :]).then_inc(dve_evac, 1)

            @block.scalar
            def _(act):
                act.wait_ge(aggr_done, TILES)
                act.activation(std[:], mv[:, :, 1], ACT.Sqrt, bias=eps[:, 0:1]).then_inc(std_done, 1)
                for n in range(0, DC * B, 2):
                    act.wait_ge(tp_full, n + 1)
                    act.copy(dst_T[:, n % DC, (n // DC) * S:(n // DC + 1) * S], tp[:, n % 4, :]).then_inc(act_evac, 1)

            @block.tensor
            def _(pe):
                for n in range(DC * B):
                    b, c = n // DC, n % DC
                    pe.wait_ge(norm_done, norm_per_tile * TPB * (b + 1))
                    if n >= 4:
                        pe.wait_ge(act_evac if n % 2 == 0 else dve_evac, (n - 4) // 2 + 1)
                    for j in range(TPB):
                        mm = pe.transpose(tp[:, n % 4, j * P:(j + 1) * P],
                                          dst[:, TPB * b + j, c * P:(c + 1) * P], k.ident[:])
                    mm.then_inc(tp_full, 1)


def attention_project(nc, k, name, a, vp, qk_dram, wq, wk, wv, bq, bk, bv, mask=None, mb=None):
    ONE = 1
    with Stage(nc, name) as st:
        w = st.sb("w", [P, 3, DC, D])
        ctxb = st.sb("ctxb", [P, DC, S])
        qkb = st.sb("qkb", [P, 2, DC])
        bvb = st.sb("bvb", [P, D])
        parts = [st.sb(f"parts{u}", [P, 4, 3, S], BF16) for u in range(2)]
        rest = st.sb("rest", [P, 4, S])
        if mask:
            per_row = mask[2]
            raw = [st.sb(f"raw{n}", [P, TPB, S], mask[0].dtype) for n in range(2)]
            raw_loaded = [st.sem(f"raw_loaded{n}") for n in range(2)]
            mask_ready = st.sem("mask_ready")
        pj = st.ps("pj", [P, 4, S])
        pv = st.ps("pv", [P, 4, S])
        w_loaded, ctx_loaded, v_full, v_evac = (st.sem(n) for n in ("w_loaded", "ctx_loaded", "v_full", "v_evac"))
        proj_full, hi_done, rest_done, mid_done, lo_done, stored = (
            st.sem(n) for n in ("proj_full", "hi_done", "rest_done", "mid_done", "lo_done", "stored"))
        vp_zero, parts_free = st.sem("vp_zero"), st.sem("parts_free")
        ORDER = [(1, 0), (1, 1), (0, 0), (0, 1)]
        with nc.Block() as block:
            @block.sync
            def _(sp):
                for j, ww in enumerate((wq, wk, wv)):
                    sp.dma_start(w[:, j], ww.rearrange("(c p) n -> p c n", p=P)).then_inc(w_loaded, DMA)
                sp.dma_start(qkb[:, 0, :], bq).then_inc(w_loaded, DMA)
                sp.dma_start(qkb[:, 1, :], bk).then_inc(w_loaded, DMA)
                sp.dma_start(bvb[:], bv).then_inc(w_loaded, DMA)
                with sp.Fori(0, B) as b:
                    sp.wait_ge(v_full, TPB * b + ONE)
                    sp.dma_start(ctxb[:], a["ctxT"].rearrange("(c p) n -> p c n", p=P)[:, :, bass.ds(b * S, S)]).then_inc(ctx_loaded, DMA)
                    if mask and per_row:
                        sp.wait_ge(mask_ready, 2 * b + ONE)
                        for n in range(2):
                            sp.dma_start(raw[n][:], mask[n][bass.ds(b * S, S)].rearrange("(t p) c -> p t c", p=P)).then_inc(raw_loaded[n], DMA)
                if mask and not per_row:
                    for n in range(2):
                        sp.dma_start(raw[n][:], mask[n].rearrange("(t p) c -> p t c", p=P)).then_inc(raw_loaded[n], DMA)

            @block.tensor
            def _(pe):
                pe.sem_inc(v_full, ONE)
                pe.wait_ge(w_loaded, 6 * DMA)
                with pe.Fori(0, B) as b:
                    def project(o):
                        which, m = ORDER[o]
                        pe.wait_ge(rest_done, 4 * b + ONE)
                        for c in range(DC):
                            rhs = ctxb[:, c, :] if which else k.XNT[:, c, bass.ds(b * S, S)]
                            mm = pe.matmul(pj[:, o, :], w[:, which, c, m * P:(m + 1) * P], rhs,
                                           start=c == 0, stop=c == DC - 1)
                        mm.then_inc(proj_full, 1)
                    pe.wait_ge(ctx_loaded, DMA * b + DMA)
                    project(0)
                    project(1)
                    pe.wait_ge(v_evac, TPB * b + ONE)
                    for t in range(TPB):
                        for c in range(DC):
                            mm = pe.matmul(pv[:, t, 0:D], ctxb[:, c, t * P:(t + 1) * P], w[:, 2, c, :],
                                           start=c == 0, stop=c == DC - 1)
                        mm.then_inc(v_full, 1)
                    project(2)
                    project(3)

            @block.scalar
            def _(act):
                act.wait_ge(w_loaded, 6 * DMA)

                def high(b, u, o):
                    which, m = ORDER[o]
                    act.wait_ge(proj_full, 4 * b + o + 1)
                    act.wait_ge(parts_free, b + 1)
                    act.activation(parts[u][:, o, 0, :], pj[:, o, :], ACT.Identity,
                                   bias=qkb[:, which, m:m + 1]).then_inc(hi_done, 1)

                def middle(b, u, o):
                    act.wait_ge(rest_done, 4 * b + o + 1 + ONE)
                    act.copy(parts[u][:, o, 1, :], rest[:, o, :]).then_inc(mid_done, 1)

                with act.Fori(0, B // 2) as b2:
                    for u in range(2):
                        for half in (0, 2):
                            for part in (high, middle):
                                for o in (half, half + 1):
                                    part(2 * b2 + u, u, o)

            @block.vector
            def _(dve):
                for credit in (rest_done, v_evac, lo_done):
                    dve.sem_inc(credit, ONE)
                if mask:
                    dve.sem_inc(mask_ready, ONE)

                def convert(b):
                    for n in range(2):
                        dve.wait_ge(raw_loaded[n], DMA * b + DMA)
                        dve.tensor_scalar(mb[n][:, at(TPB * b, TPB), :], raw[n][:], 0, MASKED, ALU.is_equal, ALU.mult).then_inc(mask_ready, 1)

                dve.wait_ge(vp_zero, 2)
                dve.wait_ge(w_loaded, 6 * DMA)
                with dve.Fori(0, B // 2) as b2:
                    for u in range(2):
                        b = 2 * b2 + u

                        def first_rest(o):
                            which, m = ORDER[o]
                            dve.wait_ge(hi_done, 4 * b + o + 1)
                            dve.wait_ge(lo_done, 4 * b + ONE)
                            dve.scalar_tensor_tensor(out=rest[:, o, :], in0=pj[:, o, :], scalar=qkb[:, which, m:m + 1],
                                                     in1=parts[u][:, o, 0, :], op0=ALU.add, op1=ALU.subtract).then_inc(rest_done, 1)

                        def low(o):
                            dve.wait_ge(mid_done, 4 * b + o + 1)
                            dve.tensor_tensor(parts[u][:, o, 2, :], rest[:, o, :], parts[u][:, o, 1, :],
                                              ALU.subtract).then_inc(lo_done, 1)

                        first_rest(0)
                        first_rest(1)
                        for t in range(TPB):
                            dve.wait_ge(v_full, TPB * b + t + 1 + ONE)
                            dve.tensor_tensor(vp[:, bass.ds(GROUPS * b, GROUPS), t, :, 0:HD],
                                              pv[:, t, 0:D].rearrange("p (g i d) -> p g i d", g=GROUPS, i=GH),
                                              bvb[:].rearrange("p (g i d) -> p g i d", g=GROUPS, i=GH), ALU.add).then_inc(v_evac, 1)
                        low(0)
                        low(1)
                        first_rest(2)
                        first_rest(3)
                        low(2)
                        low(3)
                        if mask and per_row:
                            convert(b)
                if mask and not per_row:
                    convert(0)

            @block.gpsimd
            def _(pool):
                pool.sem_inc(parts_free, 2)
                pool.memset(vp[:, :, :, :, HD:STRIP], 0.0).then_inc(vp_zero, 1)
                pool.wait_ge(vp_zero, 1)
                pool.memset(vp[:, :, :, :, HD:HD + 1], 1.0).then_inc(vp_zero, 1)
                with pool.Fori(0, B // 2) as b2:
                    for u in range(2):
                        b = 2 * b2 + u
                        for o, (which, m) in enumerate(ORDER):
                            pool.wait_ge(lo_done, 4 * b + o + 1 + ONE)
                            dst = qk_dram[which, :, bass.ds(GROUPS * b + 2 * m, 2)].rearrange("r g i d t -> (g i d) r t")
                            pool.dma_start(dst, parts[u][:, o, :, :]).then_inc(stored, DMA)
                        pool.wait_ge(stored, 4 * DMA * b + 4 * DMA)
                        pool.sem_inc(parts_free, 1)



def attention_core(nc, k, name, vp, atn, qk_dram, scale, selsum, bo, gate, mask=None, tril2=None):
    AV0, EXP0, S0, M0, AVS0, ONE = 3, 2, 2, 1, 2, 1
    with Stage(nc, name) as st:
        rows = mask[0].shape[1] // TPB if mask else 1
        qs = [st.sb(f"qs{u}", [P, GH, S], BF16) for u in range(2)]
        ks = [st.sb(f"ks{u}", [P, GH, S], BF16) for u in range(2)]
        vg = [st.sb(f"vg{u}", [P, TPB, GH, STRIP]) for u in range(2)]
        vg2 = [st.sb(f"vgd{u}", [P, TPB, GH, STRIP]) for u in range(2)] if tril2 is not None else None
        prob_wide = [st.sb(f"prob{u}", [P, TPB * (S + P) if tril2 is not None else TPB * S]) for u in range(4)]
        prob = [w[:, 0:TPB * S].rearrange("p (k q) -> p k q", k=TPB) for w in prob_wide]
        avs = [st.sb(f"avs{u}", [P, S]) for u in range(2)]
        rsum = st.sb("rsum", [P, TPB, GH])
        rdup = st.sb("rdup", [P, TPB, GH, STRIP])
        sel = st.sb("sel", [P, GH])
        maxes = st.sb("maxes", [P, TPB])
        nmp = st.sb("nmp", [P, 4, TPB, MROWS], BF16)
        bob = st.sb("bob", [P, D])
        if mask:
            junk = st.sb("junk", [P, 2, S], BF16)
            mb, mbT = mask
        if tril2 is not None:
            tril = st.sb("tril", [P, P])
        ps_s = st.ps("s", [P, 2, S])
        ps_st = st.ps("st", [P, 4, S])
        ps_av = st.ps("av", [P, S])
        ps_m = st.ps("m", [P, S])
        (const_loaded, vg_ready, s_full, s_free, split_step, negmax_ready, mt_full, mrow_ready,
         st_full, exp_done, av_done, av_evac, sums_full, recip_done, dup_done, bc_full, atn_done, ones_done,
         diag_done, bias_step, pool_tick) = (st.sem(n) for n in (
             "const_loaded", "vg_ready", "s_full", "s_free", "split_step", "negmax_ready", "mt_full",
             "mrow_ready", "st_full", "exp_done", "av_done", "av_evac", "sums_full", "recip_done", "dup_done", "bc_full",
             "atn_done", "ones_done", "diag_done", "bias_step", "pool_tick"))
        loaded = [st.sem(f"stack_loaded{u}") for u in range(2)]
        dve_tick = st.sem("dve_tick")
        NIT = B * GROUPS // 2
        PAIRS_IT = 4
        PER_LOAD = 2 * PAIRS * DMA
        NCONST = 2 + (tril2 is not None)
        VG_STEPS = 2 if vg2 is not None else 1

        def load_stack(sp, u, G):
            for which, part_of, dst in ((0, Q_PART, qs[u]), (1, K_PART, ks[u])):
                for r in range(PAIRS):
                    sp.dma_start(dst[r * HD:(r + 1) * HD, :, :],
                                 qk_dram[which, part_of[r], at(G)].rearrange("g i d t -> d (g i) t")).then_inc(loaded[u], DMA)

        def iterations(eng, body):
            body(0, True, False)
            with eng.Fori(1, NIT - 1) as it:
                body(it, False, False)
            body(NIT - 1, False, True)

        with nc.Block() as block:
            @block.sync
            def _(sp):
                sp.dma_start(sel[:], selsum).then_inc(const_loaded, DMA)
                sp.dma_start(bob[:], bo).then_inc(const_loaded, DMA)
                if tril2 is not None:
                    sp.dma_start(tril[:], tril2).then_inc(const_loaded, DMA)
                load_stack(sp, 0, 0)
                load_stack(sp, 1, 1)
                with sp.Fori(0, NIT - 1) as it:
                    for u in range(2):
                        sp.wait_ge(st_full, 16 * it + 8 * u + 8)
                        load_stack(sp, u, 2 * it + (2 + u))

            @block.gpsimd
            def _(pool):
                if tril2 is not None:
                    pool.wait_ge(const_loaded, NCONST * DMA)
                for u in range(2):
                    pool.memset(ks[u][STACK:STACK + MROWS, :, :], 1.0).then_inc(ones_done, 1)
                pool.wait_ge(ones_done, 2)
                with pool.Fori(0, NIT) as it:
                    def copy_values(u):
                        pool.wait_ge(av_done, PAIRS_IT * it + 2 * u - 2 + AV0)
                        pool.sem_inc(pool_tick, 1)
                        pool.tensor_copy(vg[u][:], vp[:, bass.ds(2 * it + u, 1)].rearrange("p g t i c -> p (g t) i c")).then_inc(vg_ready, 1)
                        if vg2 is not None:
                            pool.wait_ge(vg_ready, 4 * it + 2 * u + 1)
                            pool.tensor_tensor(vg2[u][:], vg[u][:], vg[u][:], ALU.add).then_inc(vg_ready, 1)

                    def weigh_diagonals(heads):
                        for j in heads:
                            pool.wait_ge(exp_done, 16 * it + 2 * j + 2 + EXP0)
                            diag = prob_wide[j % 4][:].rearrange("p (k q) -> p k q", k=TPB)[:, :, 0:P]
                            pool.tensor_tensor(diag, diag, tril[:].unsqueeze(1).broadcast_to([P, TPB, P]), ALU.mult).then_inc(diag_done, 1)

                    copy_values(0)
                    if tril2 is not None:
                        weigh_diagonals((0, 1))
                    copy_values(1)
                    if tril2 is not None:
                        weigh_diagonals(range(2, 2 * GH))

            @block.tensor
            def _(pe):
                pe.sem_inc(av_done, AV0)
                pe.wait_ge(ones_done, 2)

                def scores(it, j, qt):
                    it, j = (it + 1, j - 2 * GH) if j >= 2 * GH else (it, j)
                    u, i = divmod(j, GH)
                    if qt == 0 and i == 0:
                        pe.wait_ge(loaded[u], PER_LOAD * it + PER_LOAD)
                    T = 4 * j + qt
                    pe.wait_ge(s_free, 32 * it + T - 1 + S0)
                    mm = pe.matmul(ps_s[:, T % 2, :], qs[u][0:STACK, i, qt * P:(qt + 1) * P], ks[u][0:STACK, i, :],
                                   start=True, stop=rows == 1)
                    if rows > 1:
                        mm = pe.matmul(ps_s[:, T % 2, :], k.ident_bf[:], mb[:, at(TPB * (it // 2) + qt), :], start=False, stop=True)
                    mm.then_inc(s_full, 1)

                def max_rows(it, j, sums, bcs):
                    it, j = (it + 1, j - 2 * GH) if j >= 2 * GH else (it, j)
                    pe.wait_ge(negmax_ready, 8 * it + j + 1 + ONE)
                    pe.wait_ge(mrow_ready, 8 * it + j + M0)
                    pe.wait_ge(recip_done, sums + ONE)
                    pe.wait_ge(atn_done, bcs + AVS0)
                    for qt in range(TPB):
                        mm = pe.matmul(ps_m[STACK:STACK + MROWS, qt * P:(qt + 1) * P], nmp[:, j % 4, qt, :], k.ident_bf[:],
                                       start=True, stop=True)
                    mm.then_inc(mt_full, 1)

                def scores_T(it, j, hb):
                    u, i = divmod(j, GH)
                    if hb == 0:
                        pe.wait_ge(mrow_ready, 8 * it + j + 1 + M0)
                    pe.wait_ge(exp_done, 16 * it + 2 * j + hb - 1 + EXP0)
                    for kt in (2 * hb, 2 * hb + 1):
                        mm = pe.matmul(ps_st[:, kt, :], ks[u][0:STACK + MROWS, i, kt * P:(kt + 1) * P],
                                       qs[u][0:STACK + MROWS, i, :], start=True, stop=not mask)
                        if mask:
                            mm = pe.matmul(ps_st[:, kt, :], k.ident_bf[:],
                                           mbT[:, at(TPB * (it // 2) + kt), :] if rows > 1 else mbT[:, kt, :],
                                           start=False, stop=True)
                    mm.then_inc(st_full, 1)

                def values(it, m, kt):
                    it, m = (it - 1, m + PAIRS_IT) if m < 0 else (it, m)
                    u = m // 2
                    if kt == 0:
                        if m % 2 == 0:
                            pe.wait_ge(vg_ready, (2 * it + u + 1) * VG_STEPS)
                            pe.wait_ge(av_evac, 2 * it + u + ONE)
                        pe.wait_ge(exp_done, 16 * it + 4 * m + 4 + EXP0)
                        if tril2 is not None:
                            pe.wait_ge(diag_done, 8 * it + 2 * m + 2)
                    cut = (kt + 1) * P if tril2 is not None else S
                    for j in (2 * m, 2 * m + 1):
                        i = j % GH
                        mm = pe.matmul(ps_av[STRIP * i:STRIP * (i + 1), 0:cut], vg[u][:, kt, i, :], prob[j % 4][:, kt, 0:cut],
                                       start=kt == 0, stop=kt == TPB - 1, skip_group_check=True)
                    if cut < S:
                        for j in (2 * m, 2 * m + 1):
                            i = j % GH
                            mm = pe.matmul(ps_av[STRIP * i:STRIP * (i + 1), cut:S], vg2[u][:, kt, i, :], prob[j % 4][:, kt, cut:S],
                                           start=False, stop=False, skip_group_check=True)
                    if kt == TPB - 1:
                        mm.then_inc(av_done, 1)

                def sums(G, mrows):
                    pe.wait_ge(av_evac, G + 1 + ONE)
                    pe.wait_ge(mrow_ready, mrows + M0)
                    pe.wait_ge(atn_done, G + AVS0)
                    for qt in range(TPB):
                        mm = pe.matmul(ps_m[:, qt * GH:(qt + 1) * GH], avs[sums_u[0]][:, qt * P:(qt + 1) * P], sel[:], start=True, stop=True)
                    mm.then_inc(sums_full, 1)

                def broadcast(G, mrows):
                    pe.wait_ge(dup_done, G + 1)
                    pe.wait_ge(mrow_ready, mrows + M0)
                    for qt in range(TPB):
                        mm = pe.matmul(ps_m[:, qt * P:(qt + 1) * P], rdup[:, qt].rearrange("p i c -> p (i c)"), k.ident[:], start=True, stop=True)
                    mm.then_inc(bc_full, 1)

                sums_u = [0]

                def body(it, first, last):
                    G = 2 * it
                    nsum = nbc = 0 if first else G - 1
                    for m in range(PAIRS_IT):
                        a, b = 2 * m, 2 * m + 1
                        ahead = not (last and m == PAIRS_IT - 1)
                        behind = not (first and m == 0)
                        div = {1: None if first else G - 1, 3: G}.get(m)
                        has_div = m in (1, 3) and not (m == 1 and first)
                        scores_T(it, a, 0)
                        if ahead:
                            scores(it, a + 2, 0)
                        scores_T(it, a, 1)
                        max_rows(it, b, nsum, nbc)
                        if ahead:
                            scores(it, a + 2, 1)
                        if behind:
                            values(it, m - 1, 0)
                        if has_div:
                            sums_u[0] = 1 if m == 1 else 0
                            sums(div, 8 * it + b + 1)
                            nsum = div + 1
                        if ahead:
                            scores(it, a + 2, 2)
                            scores(it, a + 2, 3)
                        if behind:
                            values(it, m - 1, 1)
                        scores_T(it, b, 0)
                        if has_div:
                            broadcast(div, 8 * it + b + 1)
                            nbc = div + 1
                        if ahead:
                            scores(it, b + 2, 0)
                        scores_T(it, b, 1)
                        if ahead:
                            max_rows(it, a + 2, nsum, nbc)
                            scores(it, b + 2, 1)
                        if behind:
                            values(it, m - 1, 2)
                        if ahead:
                            scores(it, b + 2, 2)
                            scores(it, b + 2, 3)
                        if behind:
                            values(it, m - 1, 3)

                for j in range(2):
                    for qt in range(TPB):
                        scores(0, j, qt)
                pe.wait_ge(const_loaded, NCONST * DMA)
                max_rows(0, 0, 0, 0)
                iterations(pe, body)
                for kt in range(TPB):
                    values(NIT - 1, PAIRS_IT - 1, kt)
                sums_u[0] = 1
                sums(2 * NIT - 1, 8 * NIT)
                broadcast(2 * NIT - 1, 8 * NIT)

            @block.scalar
            def _(act):
                act.sem_inc(exp_done, EXP0)
                act.sem_inc(mrow_ready, M0)
                act.sem_inc(av_evac, ONE)
                act.wait_ge(ones_done, 2)

                def max_row(it, j):
                    it, j = (it + 1, j - 2 * GH) if j >= 2 * GH else (it, j)
                    u, i = divmod(j, GH)
                    act.wait_ge(mt_full, 8 * it + j + 1)
                    act.copy(qs[u][STACK:STACK + MROWS, i, :], ps_m[STACK:STACK + MROWS, :]).then_inc(mrow_ready, 1)

                def exps(it, j, next_row):
                    for hb in range(2):
                        act.wait_ge(st_full, 16 * it + 2 * j + hb + 1)
                        act.wait_ge(av_done, PAIRS_IT * it + j // 2 - 1 + AV0)
                        act.activation(prob[j % 4][:, 2 * hb:2 * hb + 2, :], ps_st[:, 2 * hb:2 * hb + 2, :], ACT.Exp,
                                       scale=scale).then_inc(exp_done, 1)
                        if hb == 0 and next_row:
                            max_row(it, j + 1)

                def evacuate(G, u):
                    act.wait_ge(av_done, 2 * G + 2 + AV0)
                    act.wait_ge(atn_done, G - 1 + AVS0)
                    act.copy(avs[u][:], ps_av[:]).then_inc(av_evac, 1)

                def body(it, first, last):
                    for m in range(PAIRS_IT):
                        if m == 1 and not first:
                            evacuate(2 * it - 1, 1)
                        if m == 3:
                            evacuate(2 * it, 0)
                        exps(it, 2 * m, True)
                        exps(it, 2 * m + 1, not (last and m == PAIRS_IT - 1))

                max_row(0, 0)
                iterations(act, body)
                evacuate(2 * NIT - 1, 1)

            @block.vector
            def _(dve):
                dve.sem_inc(s_free, S0)
                dve.sem_inc(atn_done, AVS0)
                dve.sem_inc(negmax_ready, ONE)
                dve.sem_inc(recip_done, ONE)
                def row_max(it, j, qt):
                    it, j = (it + 1, j - 2 * GH) if j >= 2 * GH else (it, j)
                    if qt == 0:
                        dve.wait_ge(negmax_ready, 8 * it + j + ONE)
                    T = 4 * j + qt
                    dve.wait_ge(s_full, 32 * it + T + 1)
                    if mask and rows == 1:
                        dve.wait_ge(s_free, 32 * it + T - 1 + S0)
                        dve.sem_inc(dve_tick, 1)
                        dve.tensor_tensor_reduce(out=junk[:, T % 2, :], in0=ps_s[:, T % 2, :], in1=mb[:, qt, :],
                                                 scale=1.0, scalar=-3.0e38, op0=ALU.add, op1=ALU.max,
                                                 accum_out=maxes[:, qt:qt + 1]).then_inc(s_free, 1)
                    else:
                        dve.tensor_reduce(maxes[:, qt:qt + 1], ps_s[:, T % 2, :], AX.X, ALU.max).then_inc(s_free, 1)

                def split(it, j):
                    it, j = (it + 1, j - 2 * GH) if j >= 2 * GH else (it, j)
                    dve.wait_ge(s_free, 32 * it + 4 * j + 4 + S0)
                    dve.tensor_scalar(nmp[:, j % 4, :, 0], maxes[:], -1.0, None, ALU.mult).then_inc(split_step, 1)
                    dve.wait_ge(split_step, 8 * it + j + 1)
                    dve.scalar_tensor_tensor(out=nmp[:, j % 4, :, 1], in0=maxes[:], scalar=-1.0, in1=nmp[:, j % 4, :, 0],
                                             op0=ALU.mult, op1=ALU.subtract).then_inc(negmax_ready, 1)

                def reciprocals(G):
                    dve.wait_ge(sums_full, G + 1)
                    dve.reciprocal(rsum[:], ps_m[:, 0:TPB * GH].rearrange("p (t i) -> p t i", t=TPB)).then_inc(recip_done, 1)
                    dve.wait_ge(recip_done, G + 1 + ONE)
                    dve.tensor_copy(rdup[:], rsum[:].unsqueeze(3).broadcast_to([P, TPB, GH, STRIP])).then_inc(dup_done, 1)

                def divide(G, u):
                    dve.wait_ge(bc_full, G + 1)
                    dve.tensor_tensor(atn[:, at(G), :].rearrange("p g q -> p (g q)"), avs[u][:], ps_m[:], ALU.mult).then_inc(atn_done, 1)

                def body(it, first, last):
                    for m in range(PAIRS_IT):
                        a, b = 2 * m, 2 * m + 1
                        ahead = not (last and m == PAIRS_IT - 1)
                        has_div = m == 3 or (m == 1 and not first)
                        G, u = (2 * it - 1, 1) if m == 1 else (2 * it, 0)
                        if ahead:
                            row_max(it, a + 2, 0)
                            row_max(it, a + 2, 1)
                        if has_div:
                            reciprocals(G)
                        if ahead:
                            row_max(it, a + 2, 2)
                            row_max(it, a + 2, 3)
                            split(it, a + 2)
                        if has_div:
                            divide(G, u)
                        if ahead:
                            for qt in range(TPB):
                                row_max(it, b + 2, qt)
                            split(it, b + 2)

                for j in range(2):
                    for qt in range(TPB):
                        row_max(0, j, qt)
                    split(0, j)
                dve.wait_ge(const_loaded, NCONST * DMA)
                dve.tensor_scalar(bob[:], bob[:], k.tg[:, gate:gate + 1], None, ALU.mult).then_inc(bias_step, 1)
                dve.wait_ge(bias_step, 1)
                dve.tensor_tensor(k.X[:], k.X[:], bob[:].unsqueeze(1).broadcast_to([P, TILES, D]), ALU.add).then_inc(bias_step, 1)
                dve.wait_ge(bias_step, 2)
                iterations(dve, body)
                reciprocals(2 * NIT - 1)
                divide(2 * NIT - 1, 1)


def attention_out(nc, k, name, atn, wo, gate):
    with Stage(nc, name) as st:
        w = st.sb("w", [P, GROUPS, D])
        po = st.ps("po", [P, 8, 512])
        w_loaded, out_full, out_evac = st.sem("w_loaded"), st.sem("out_full"), st.sem("out_evac")
        with nc.Block() as block:
            @block.sync
            def _(sp):
                sp.dma_start(w[:], wo).then_inc(w_loaded, DMA)

            @block.tensor
            def _(pe):
                pe.wait_ge(w_loaded, DMA)
                for t in range(TILES):
                    if t >= 8:
                        pe.wait_ge(out_evac, t - 7)
                    for g in range(GROUPS):
                        mm = pe.matmul(po[:, t % 8, 0:D], atn[:, GROUPS * (t // TPB) + g, (t % TPB) * P:(t % TPB + 1) * P],
                                       w[:, g, :], start=g == 0, stop=g == GROUPS - 1)
                    mm.then_inc(out_full, 1)

            @block.vector
            def _(dve):
                for t in range(TILES):
                    dve.wait_ge(out_full, t + 1)
                    dve.scalar_tensor_tensor(out=k.X[:, t, :], in0=po[:, t % 8, 0:D], scalar=k.tg[:, gate:gate + 1],
                                             in1=k.X[:, t, :], op0=ALU.mult, op1=ALU.add).then_inc(out_evac, 1)


def attention_layer(nc, k, name, a, wq, wk, wv, bq, bk, bv, wo, bo, scale, gate, mask=None, tril2=None):
    layernorm_stage(nc, k, name + "_ln", k.X, k.XN, k.XNT)
    with ExitStack() as ctx:
        vp = ctx.enter_context(nc.sbuf_tensor(name + "_vp", [P, B * GROUPS, TPB, GH, STRIP], F32))
        mb = None
        if mask:
            n = (B if mask[2] else 1) * TPB
            mb = [ctx.enter_context(nc.sbuf_tensor(f"{name}_mb{u}", [P, n, S], BF16)) for u in range(2)]
        attention_project(nc, k, name + "_p", a, vp, k.qk_dram, wq, wk, wv, bq, bk, bv, mask, mb)
        attention_core(nc, k, name + "_a", vp, k.ATN, k.qk_dram, scale, a["selsum"], bo, gate, mb, tril2)
    attention_out(nc, k, name + "_o", k.ATN, wo, gate)


class Chain:

    def __init__(self, eng, sem, base=0):
        self.eng, self.sem, self.base, self.n = eng, sem, base, 0

    def __call__(self, ins):
        self.n += 1
        ins.then_inc(self.sem, 1)
        self.eng.wait_ge(self.sem, self.base + self.n)


def over(x, n):
    return x.unsqueeze(2).broadcast_to([x.shape[0], x.shape[1], n])


def transpose_stage(nc, k, name, src, dst_T):
    with Stage(nc, name) as st:
        tp = st.ps("tp", [P, 4, 512])
        tp_full, act_evac, dve_evac = st.sem("tp_full"), st.sem("act_evac"), st.sem("dve_evac")

        def bank(n):
            return dst_T[:, n % DC, (n // DC) * S:(n // DC + 1) * S], tp[:, n % 4, :]

        with nc.Block() as block:
            @block.tensor
            def _(pe):
                for n in range(DC * B):
                    if n >= 4:
                        pe.wait_ge(act_evac if n % 2 == 0 else dve_evac, (n - 4) // 2 + 1)
                    for j in range(TPB):
                        mm = pe.transpose(tp[:, n % 4, j * P:(j + 1) * P],
                                          src[:, TPB * (n // DC) + j, (n % DC) * P:(n % DC + 1) * P], k.ident[:])
                    mm.then_inc(tp_full, 1)

            @block.scalar
            def _(act):
                for n in range(0, DC * B, 2):
                    act.wait_ge(tp_full, n + 1)
                    act.copy(*bank(n)).then_inc(act_evac, 1)

            @block.vector
            def _(dve):
                for n in range(1, DC * B, 2):
                    dve.wait_ge(tp_full, n + 1)
                    dve.tensor_copy(*bank(n)).then_inc(dve_evac, 1)


def router_stage(nc, k, name, a, src_T, rw, rb, E, K, kind, gate_col, gates, floor=True, pick=None):
    EPS = 1e-10
    with Stage(nc, name) as st:
        w = st.sb("w", [P, DC, E])
        rbb = st.sb("rbb", [P, E])
        ranks = st.sb("ranks", [P, E])
        lg, pr, work, sel, one, tmp = (st.sb(n, [P, TILES, E]) for n in ("lg", "pr", "work", "sel", "one", "tmp"))
        m, s, r = (st.sb(n, [P, TILES]) for n in ("m", "s", "r"))
        ps = st.ps("ps_lg", [P, TILES, E])
        loaded, lg_full, step, shifted, exp_done = (st.sem(n) for n in ("loaded", "lg_full", "step", "shifted", "exp_done"))
        n_loads = 3
        with nc.Block() as block:
            @block.sync
            def _(sp):
                sp.dma_start(w[:], rw.rearrange("(c p) e -> p c e", p=P)).then_inc(loaded, DMA)
                sp.dma_start(rbb[:], rb).then_inc(loaded, DMA)
                sp.dma_start(ranks[:], a[f"ranks{E}"]).then_inc(loaded, DMA)

            @block.tensor
            def _(pe):
                pe.wait_ge(loaded, n_loads * DMA)
                for t in range(TILES):
                    for c in range(DC):
                        mm = pe.matmul(ps[:, t, :], src_T[:, c, t * P:(t + 1) * P], w[:, c, :], start=c == 0, stop=c == DC - 1)
                mm.then_inc(lg_full, 1)

            @block.scalar
            def _(act):
                act.wait_ge(shifted, 1)
                act.activation(pr[:], lg[:], ACT.Exp).then_inc(exp_done, 1)

            @block.vector
            def _(dve):
                do = Chain(dve, step)

                def row_sum(out, x):
                    do(dve.tensor_reduce(out, x, AX.X, ALU.add))

                dve.wait_ge(loaded, n_loads * DMA)
                dve.wait_ge(lg_full, 1)
                do(dve.tensor_tensor(lg[:], ps[:], rbb[:].unsqueeze(1).broadcast_to([P, TILES, E]), ALU.add))
                do(dve.tensor_reduce(m[:], lg[:], AX.X, ALU.max))
                dve.tensor_tensor(lg[:], lg[:], over(m[:], E), ALU.subtract).then_inc(shifted, 1)
                dve.wait_ge(exp_done, 1)
                if kind == "probs":
                    row_sum(s[:], pr[:])
                    do(dve.reciprocal(r[:], s[:]))
                    do(dve.tensor_tensor(pr[:], pr[:], over(r[:], E), ALU.mult))
                do(dve.tensor_copy(work[:], pr[:] if kind == "probs" else lg[:]))
                do(dve.memset(sel[:], 0.0))
                for i in range(K):
                    do(dve.tensor_reduce(m[:], work[:], AX.X, ALU.max))
                    do(dve.tensor_tensor(one[:], work[:], over(m[:], E), ALU.is_equal))
                    do(dve.tensor_tensor(one[:], one[:], ranks[:].unsqueeze(1).broadcast_to([P, TILES, E]), ALU.mult))
                    do(dve.tensor_reduce(m[:], one[:], AX.X, ALU.max))
                    do(dve.tensor_tensor(one[:], one[:], over(m[:], E), ALU.is_equal))
                    do(dve.tensor_tensor(sel[:], sel[:], one[:], ALU.add))
                    if pick is not None:
                        do(dve.tensor_copy(pick[:, i], one[:]))
                    do(dve.scalar_tensor_tensor(out=work[:], in0=one[:], scalar=MASKED, in1=work[:], op0=ALU.mult, op1=ALU.add))
                do(dve.tensor_tensor(tmp[:], pr[:], sel[:], ALU.mult))
                row_sum(s[:], tmp[:])
                if kind == "probs" and floor:
                    do(dve.tensor_scalar(s[:], s[:], EPS, None, ALU.add))
                do(dve.reciprocal(r[:], s[:]))
                do(dve.tensor_tensor(tmp[:], tmp[:], over(r[:], E), ALU.mult))
                if kind == "probs" and floor:
                    row_sum(s[:], tmp[:])
                    do(dve.tensor_scalar(r[:], s[:], EPS, None, ALU.max))
                    do(dve.reciprocal(m[:], r[:]))
                    do(dve.tensor_tensor(tmp[:], tmp[:], over(m[:], E), ALU.mult))
                    do(dve.tensor_scalar(s[:], s[:], EPS, k.tg[:, gate_col:gate_col + 1], ALU.mult, ALU.mult))
                    do(dve.tensor_tensor(k.X[:], k.X[:], over(s[:], D), ALU.add))
                do(dve.tensor_scalar(gates[:], tmp[:], k.tg[:, gate_col:gate_col + 1], None, ALU.mult))


def linear_experts_stage(nc, k, name, expert_w, gates, E):
    BANKS = 8
    with Stage(nc, name) as st:
        w = st.sb("w", [P, DC, E, D])
        po = st.ps("po", [P, BANKS, 512])
        w_loaded, full, evac, x_step = (st.sem(n) for n in ("w_loaded", "full", "evac", "x_step"))
        FILLS = 4
        zero = st.sb("zero", [P, FILL_ROWS * D // (P * FILLS)])
        zero_ready, filled = st.sem("zero_ready"), st.sem("filled")
        with nc.Block() as block:
            @block.gpsimd
            def _(pool):
                pool.memset(zero[:], 0.0).then_inc(zero_ready, 1)

            @block.sync
            def _(sp):
                for c in range(DC):
                    sp.dma_start(w[:, c], expert_w[:, c * P:(c + 1) * P, :].rearrange("e p n -> p e n")).then_inc(w_loaded, DMA)
                sp.wait_ge(zero_ready, 1)
                for n in range(FILLS):
                    rows = FILL_ROWS // FILLS
                    sp.dma_start(k.slot_x[n * rows:(n + 1) * rows, :].rearrange("(p r) d -> p (r d)", p=P), zero[:]).then_inc(filled, DMA)
                sp.wait_ge(filled, FILLS * DMA)

            @block.tensor
            def _(pe):
                pe.wait_ge(w_loaded, DC * DMA)
                with pe.Fori(0, E // 2) as pair:
                    for t in range(TILES):
                        pe.wait_ge(evac, TILES * pair + t + 1)
                        for c in range(DC):
                            mm = pe.matmul(po[:, t % BANKS, :], k.XNT[:, c, t * P:(t + 1) * P],
                                           w[:, c, bass.ds(2 * pair, 2), :], start=c == 0, stop=c == DC - 1)
                        mm.then_inc(full, 1)

            @block.vector
            def _(dve):
                dve.sem_inc(evac, BANKS)
                with dve.Fori(0, E // 2) as pair:
                    for t in range(TILES):
                        dve.wait_ge(full, TILES * pair + t + 1)
                        dve.scalar_tensor_tensor(out=k.X[:, t, :], in0=po[:, t % BANKS, 0:D], scalar=gates[:, t, bass.ds(2 * pair, 1)],
                                                 in1=k.X[:, t, :], op0=ALU.mult, op1=ALU.add).then_inc(x_step, 1)
                        dve.wait_ge(x_step, TILES * pair + t + 1)
                        dve.scalar_tensor_tensor(out=k.X[:, t, :], in0=po[:, t % BANKS, D:2 * D], scalar=gates[:, t, bass.ds(2 * pair + 1, 1)],
                                                 in1=k.X[:, t, :], op0=ALU.mult, op1=ALU.add).then_inc(evac, 1)


class Plan:

    def __init__(self, nc, ctx, name, E, GS, capacity):
        def sb(n, shape, dt=F32):
            return ctx.enter_context(nc.sbuf_tensor(f"{name}_{n}", shape, dt))
        self.E, self.GS, self.capacity = E, GS, capacity
        self.NG = E if capacity else (2 * B * S + E * (GS - 1)) // GS
        self.pick = sb("pick", [P, 2, TILES, E])
        self.weight = sb("weight", [P, 2, TILES])
        self.to = sb("to", [P, 2 * TILES], U32)
        self.back = self.to
        if capacity:
            self.back = sb("back", [P, 2 * TILES], U32)
        else:
            self.w_row = sb("w_row", [P, self.NG], U32)


def slots_stage(nc, k, name, a, plan, gates):
    E, GS, NG = plan.E, plan.GS, plan.NG
    with Stage(nc, name) as st:
        before = st.sb("before", [P, P])
        ones = st.sb("ones", [P, P])
        sel, slot, fits, prod = (st.sb(n, [P, TILES, E]) for n in ("sel", "slot", "fits", "prod"))
        cum = st.sb("cum", [P, TILES + 1, E])
        to, ok = st.sb("to", [P, 2, TILES]), st.sb("ok", [P, 2, TILES])
        base = st.sb("base", [P, E])
        ps_rank = st.ps("ps_rank", [P, TILES, E])
        ps_count = st.ps("ps_count", [P, E])
        loaded, step, sel_done, rank_full = (st.sem(n) for n in ("loaded", "step", "sel_done", "rank_full"))
        if plan.capacity:
            spare = st.sb("spare", [P, 2, TILES])
        else:
            count, need, more = st.sb("count", [P, E]), st.sb("need", [P, E]), st.sb("more", [P, E])
            end = st.sb("end", [P, E])
            index = st.sb("index", [P, NG])
            lane = st.sb("lane", [P, 1])
            past = st.sb("past", [P, NG, E])
            row = st.sb("row", [P, NG])
        with nc.Block() as block:
            @block.sync
            def _(sp):
                sp.dma_start(before[:], a["before"]).then_inc(loaded, DMA)
                if plan.capacity:
                    sp.dma_start(base[:], a["first_slots"]).then_inc(loaded, DMA)
                    sp.dma_start(spare[:], a["spare_slots"]).then_inc(loaded, DMA)
                else:
                    sp.dma_start(index[:], a["index"][:, 0:NG]).then_inc(loaded, DMA)
                    sp.dma_start(lane[:], a["lane"]).then_inc(loaded, DMA)

            @block.tensor
            def _(pe):
                pe.wait_ge(loaded, 3 * DMA)
                pe.wait_ge(sel_done, 1)
                pe.matmul(ps_rank[:], before[:], sel[:], start=True, stop=False)
                mm = pe.matmul(ps_rank[:], ones[:], cum[:, 0:TILES, :], start=False, stop=True)
                if not plan.capacity:
                    mm = pe.matmul(ps_count[:], ones[:], cum[:, TILES, :], start=True, stop=True)
                mm.then_inc(rank_full, 1)

            @block.vector
            def _(dve):
                do = Chain(dve, step)
                do(dve.memset(ones[:], 1.0))
                do(dve.memset(cum[:, 0, :], 0.0))
                do(dve.tensor_tensor(sel[:], plan.pick[:, 0], plan.pick[:, 1], ALU.add))
                for t in range(TILES):
                    do(dve.tensor_tensor(cum[:, t + 1, :], cum[:, t, :], sel[:, t, :], ALU.add))
                dve.sem_inc(sel_done, 1)
                dve.wait_ge(loaded, 3 * DMA)
                dve.wait_ge(rank_full, 1)
                if plan.capacity:
                    do(dve.tensor_scalar(fits[:], ps_rank[:], float(GS), None, ALU.is_lt))
                    do(dve.tensor_tensor(gates[:], gates[:], fits[:], ALU.mult))
                else:
                    do(dve.tensor_copy(count[:], ps_count[:]))
                    do(dve.tensor_scalar(need[:], count[:], 0.0, None, ALU.is_gt))
                    for n in range(1, B * S // GS):
                        do(dve.tensor_scalar(more[:], count[:], float(n * GS), None, ALU.is_gt))
                        do(dve.tensor_tensor(need[:], need[:], more[:], ALU.add))
                    do(dve.tensor_copy(end[:, 0:1], need[:, 0:1]))
                    for e in range(1, E):
                        do(dve.tensor_tensor(end[:, e:e + 1], end[:, e - 1:e], need[:, e:e + 1], ALU.add))
                    do(dve.tensor_tensor(base[:], end[:], need[:], ALU.subtract))
                    do(dve.tensor_scalar(base[:], base[:], float(GS), None, ALU.mult))
                    do(dve.tensor_tensor(past[:], end[:].unsqueeze(1).broadcast_to([P, NG, E]), over(index[:], E), ALU.is_le))
                    do(dve.tensor_reduce(row[:], past[:], AX.X, ALU.add))
                    do(dve.tensor_scalar(row[:], row[:], float(E - 1), float(P), ALU.min, ALU.mult))
                    do(dve.tensor_scalar(row[:], row[:], lane[:, 0:1], None, ALU.add))
                    do(dve.tensor_copy(plan.w_row[:], row[:]))
                do(dve.tensor_tensor(slot[:], ps_rank[:], base[:].unsqueeze(1).broadcast_to([P, TILES, E]), ALU.add))
                for i in range(2):
                    for what, out in [(gates, plan.weight), (slot, to)] + ([(fits, ok)] if plan.capacity else []):
                        do(dve.tensor_tensor(prod[:], plan.pick[:, i], what[:], ALU.mult))
                        do(dve.tensor_reduce(out[:, i, :], prod[:], AX.X, ALU.add))
                flat = to[:].rearrange("p i t -> p (i t)")
                if plan.capacity:
                    do(dve.tensor_tensor(to[:], to[:], ok[:], ALU.mult))
                    do(dve.tensor_copy(plan.back[:], flat))
                    do(dve.tensor_scalar(ok[:], ok[:], -1.0, 1.0, ALU.mult, ALU.add))
                    do(dve.tensor_tensor(ok[:], ok[:], spare[:], ALU.mult))
                    do(dve.tensor_tensor(to[:], to[:], ok[:], ALU.add))
                do(dve.tensor_copy(plan.to[:], flat))


def grouped_experts_stage(nc, k, name, src, plan, w_rows, FC, gated):
    GS, NG = plan.GS, plan.NG
    GT = GS // P
    NW = 2 if gated else 1
    NB = -(-GS // 512)
    BW = GS // NB
    HB = 2 if gated else 4
    F = NW * FC * P
    TP = [(c, t, min(t + 4, GT)) for c in range(DC) for t in range(0, GT, 4)]
    NTP = len(TP)
    STEPS = FC * NB
    LOOPS = (NG - 2) // 2
    with Stage(nc, name) as st:
        w = [st.sb(f"w{u}", [P, w_rows.shape[1]]) for u in range(2)]
        w1 = [x[:, 0:DC * F].rearrange("p (c f) -> p c f", c=DC) for x in w]
        w2 = [x[:, DC * F:DC * F + FC * D].rearrange("p (j n) -> p j n", j=FC) for x in w]
        b1 = [x[:, DC * F + FC * D:] for x in w]
        xg = [st.sb(f"xg{u}", [P, GT, D]) for u in range(2)]
        xT = [st.sb(f"xT{u}", [P, DC, GS]) for u in range(2)]
        y = [st.sb(f"y{u}", [P, GT, D]) for u in range(2)]
        ht = st.sb("ht", [P, FC, GS])
        sg = st.sb("sg", [P, 2, GS]) if gated else None
        ph = [st.ps(f"ph{n}", [P, HB, 512]) for n in range(NW)]
        po = st.ps("po", [P, 2, 512])
        tp = st.ps("tp", [P, 2, 512])
        w_loaded = [st.sem(f"w_loaded{u}") for u in range(2)]
        x_loaded = [st.sem(f"x_loaded{u}") for u in range(2)]
        scattered, tp_full, tp_evac, h_full, act_done, h_ready, o_full, y_ready, y_stored, y_free = (st.sem(n) for n in (
            "scattered", "tp_full", "tp_evac", "h_full", "act_done", "h_ready", "o_full", "y_ready", "y_stored", "y_free"))
        hidden_ready = h_ready if gated else act_done

        def groups(eng, body):
            with eng.Fori(0, LOOPS) as it:
                for u in range(2):
                    body(2 * it + u, u, it)
            for g in range(2 * LOOPS, NG):
                body(g, g % 2, g // 2)

        with nc.Block() as block:
            @block.sync
            def _(sp):
                def load_w(g, u):
                    sp.dma_start(w[u][:], w_rows[at(P * g, P), :]).then_inc(w_loaded[u], DMA)

                def load_x(g, u):
                    sp.dma_start(xg[u][:], k.slot_x[at(GS * g, GS), :].rearrange("(t p) d -> p t d", p=P)).then_inc(x_loaded[u], DMA)

                if plan.capacity:
                    load_w(0, 0)
                    load_w(1, 1)
                sp.sem_inc(y_free, 2)
                sp.wait_ge(scattered, 2 * TILES * DMA)
                load_x(0, 0)
                load_x(1, 1)

                def body(g, u, turn):
                    more = not (isinstance(g, int) and g + 2 >= NG)
                    if more:
                        sp.wait_ge(tp_full, NTP * g + NTP)
                        load_x(g + 2, u)
                    sp.wait_ge(y_ready, GT * g + GT + 2)
                    sp.dma_start(k.slot_y[at(GS * g, GS), :].rearrange("(t p) d -> p t d", p=P), y[u][:]).then_inc(y_stored, DMA)
                    if plan.capacity and more:
                        load_w(g + 2, u)
                    sp.wait_ge(y_stored, DMA * g + DMA)
                    sp.sem_inc(y_free, 1)
                groups(sp, body)

            @block.gpsimd
            def _(pool):
                def gather_w(g):
                    pool.indirect_dma_start(w[g % 2][:], None, w_rows,
                                            bass.IndirectOffsetOnAxis(plan.w_row[:, g:g + 1], 0)).then_inc(w_loaded[g % 2], DMA)
                if not plan.capacity:
                    gather_w(0)
                    gather_w(1)
                for n in range(2 * TILES):
                    pool.indirect_dma_start(k.slot_x, bass.IndirectOffsetOnAxis(plan.to[:, n:n + 1], 0),
                                            src[:, n % TILES, :], None).then_inc(scattered, DMA)
                pool.wait_ge(scattered, 2 * TILES * DMA)
                if not plan.capacity:
                    for g in range(2, NG):
                        pool.wait_ge(o_full, GT * (g - 1))
                        gather_w(g)

            @block.tensor
            def _(pe):
                def transposes(g, u, turn):
                    pe.wait_ge(x_loaded[u], DMA * turn + DMA)
                    for n, (c, t0, t1) in enumerate(TP):
                        pe.wait_ge(tp_evac, NTP * g + n + 1)
                        for t in range(t0, t1):
                            mm = pe.transpose(tp[:, n % 2, (t - t0) * P:(t - t0 + 1) * P], xg[u][:, t, c * P:(c + 1) * P], k.ident[:])
                        mm.then_inc(tp_full, 1)

                def body(g, u, turn):
                    pe.wait_ge(w_loaded[u], DMA * turn + DMA)
                    pe.wait_ge(tp_evac, NTP * g + NTP + 2)
                    for s in range(STEPS):
                        j, b = divmod(s, NB)
                        pe.wait_ge(hidden_ready, STEPS * g + s + 1)
                        for n in range(NW):
                            for c in range(DC):
                                mm = pe.matmul(ph[n][:, s % HB, 0:BW], w1[u][:, c, (n * FC + j) * P:(n * FC + j + 1) * P],
                                               xT[u][:, c, b * BW:(b + 1) * BW], start=c == 0, stop=c == DC - 1)
                        mm.then_inc(h_full, 1)
                    if not (isinstance(g, int) and g + 1 >= NG):
                        transposes(g + 1, 1 - u, turn + u)
                    pe.wait_ge(hidden_ready, STEPS * g + STEPS + HB)
                    for t in range(GT):
                        pe.wait_ge(y_ready, GT * g + t + 1)
                        for j in range(FC):
                            mm = pe.matmul(po[:, (GT * u + t) % 2, 0:D], ht[:, j, t * P:(t + 1) * P], w2[u][:, j, :],
                                           start=j == 0, stop=j == FC - 1)
                        mm.then_inc(o_full, 1)

                transposes(0, 0, 0)
                groups(pe, body)

            @block.scalar
            def _(act):
                act.sem_inc(act_done, HB)
                act.sem_inc(tp_evac, 2)

                def evacuate(g, u):
                    for n, (c, t0, t1) in enumerate(TP):
                        act.wait_ge(tp_full, NTP * g + n + 1)
                        act.copy(xT[u][:, c, t0 * P:t1 * P], tp[:, n % 2, 0:(t1 - t0) * P]).then_inc(tp_evac, 1)

                def body(g, u, turn):
                    for s in range(STEPS):
                        j, b = divmod(s, NB)
                        act.wait_ge(h_full, STEPS * g + s + 1)
                        if gated:
                            act.wait_ge(h_ready, STEPS * g + s + 1)
                            act.activation(sg[:, s % 2, :], ph[0][:, s % HB, 0:BW], ACT.Silu, bias=b1[u][:, j:j + 1]).then_inc(act_done, 1)
                        else:
                            act.activation(ht[:, j, b * BW:(b + 1) * BW], ph[0][:, s % HB, 0:BW], ACT.Gelu_apprx_tanh).then_inc(act_done, 1)
                    if not (isinstance(g, int) and g + 1 >= NG):
                        evacuate(g + 1, 1 - u)

                evacuate(0, 0)
                groups(act, body)

            @block.vector
            def _(dve):
                dve.sem_inc(y_ready, 2)
                if gated:
                    dve.sem_inc(h_ready, HB)

                def body(g, u, turn):
                    if gated:
                        for s in range(STEPS):
                            dve.wait_ge(act_done, STEPS * g + s + 1 + HB)
                            dve.scalar_tensor_tensor(out=ht[:, s, :], in0=ph[1][:, s % HB, 0:BW], scalar=b1[u][:, FC + s:FC + s + 1],
                                                     in1=sg[:, s % 2, :], op0=ALU.add, op1=ALU.mult).then_inc(h_ready, 1)
                    dve.wait_ge(y_free, g + 1)
                    for t in range(GT):
                        dve.wait_ge(o_full, GT * g + t + 1)
                        dve.tensor_copy(y[u][:, t, :], po[:, (GT * u + t) % 2, 0:D]).then_inc(y_ready, 1)

                groups(dve, body)


def combine_stage(nc, k, name, plan):
    BATCH = 4
    with Stage(nc, name) as st:
        back = k.ATN.rearrange("p g n -> p (g n)").rearrange("p (n d) -> p n d", d=D)
        got = [st.sem(f"got{b}") for b in range(2 * TILES // BATCH)]
        done = st.sem("done")
        with nc.Block() as block:
            @block.gpsimd
            def _(pool):
                for n in range(2 * TILES):
                    pool.indirect_dma_start(back[:, n, :], None, k.slot_y[0:plan.NG * plan.GS, :],
                                            bass.IndirectOffsetOnAxis(plan.back[:, n:n + 1], 0)).then_inc(got[n // BATCH], DMA)

            @block.vector
            def _(dve):
                for n in range(2 * TILES):
                    i, t = divmod(n, TILES)
                    if n % BATCH == 0:
                        dve.wait_ge(got[n // BATCH], BATCH * DMA)
                    if i == 1:
                        dve.wait_ge(done, t + 1)
                    dve.scalar_tensor_tensor(out=k.X[:, t, :], in0=back[:, n, :], scalar=plan.weight[:, i, t:t + 1],
                                             in1=k.X[:, t, :], op0=ALU.mult, op1=ALU.add).then_inc(done, 1)
                dve.wait_ge(done, 2 * TILES)


def gated_bias_stage(nc, k, name, gates, b2, E):
    with Stage(nc, name) as st:
        b2s = st.sb("b2", [E, D])
        gT = st.sb("gT", [E, TILES, P])
        tp = st.ps("tp", [E, TILES, P])
        po = st.ps("po", [P, 4, 512])
        loaded, t_full, t_evac, o_full, o_evac = (st.sem(n) for n in ("loaded", "t_full", "t_evac", "o_full", "o_evac"))
        with nc.Block() as block:
            @block.sync
            def _(sp):
                sp.dma_start(b2s[:], b2).then_inc(loaded, DMA)

            @block.tensor
            def _(pe):
                for t in range(TILES):
                    mm = pe.transpose(tp[:, t, :], gates[:, t, :], k.ident[:])
                mm.then_inc(t_full, 1)
                pe.wait_ge(loaded, DMA)
                pe.wait_ge(t_evac, 1)
                for t in range(TILES):
                    if t >= 4:
                        pe.wait_ge(o_evac, t - 3)
                    pe.matmul(po[:, t % 4, 0:D], gT[:, t, :], b2s[:], start=True, stop=True).then_inc(o_full, 1)

            @block.vector
            def _(dve):
                dve.wait_ge(t_full, 1)
                dve.tensor_copy(gT[:], tp[:]).then_inc(t_evac, 1)
                for t in range(TILES):
                    dve.wait_ge(o_full, t + 1)
                    dve.tensor_tensor(k.X[:, t, :], po[:, t % 4, 0:D], k.X[:, t, :], ALU.add).then_inc(o_evac, 1)


def expert_layer_0(nc, k, a):
    layernorm_stage(nc, k, "l0f_ln", k.X, k.XN, k.XNT)
    with ExitStack() as ctx:
        gates = ctx.enter_context(nc.sbuf_tensor("l0f_gates", [P, TILES, 16], F32))
        router_stage(nc, k, "l0f_r", a, k.XNT, a["r0w"], a["r0b"], 16, 6, "probs", 4, gates)
        linear_experts_stage(nc, k, "l0f_e", a["e0w"], gates, 16)


def expert_layer_2(nc, k, a):
    layernorm_stage(nc, k, "l2f_ln", k.X, k.XN, k.XNT)
    with ExitStack() as ctx:
        plan = Plan(nc, ctx, "l2f", 8, GROUP, False)
        gates = ctx.enter_context(nc.sbuf_tensor("l2f_gates", [P, TILES, 8], F32))
        router_stage(nc, k, "l2f_r", a, k.XNT, a["r2w"], a["r2b"], 8, 2, "logits", 6, gates, pick=plan.pick)
        slots_stage(nc, k, "l2f_s", a, plan, gates)
        gated_bias_stage(nc, k, "l2f_b", gates, a["e2b2"], 8)
        grouped_experts_stage(nc, k, "l2f_e", k.XN, plan, a["e2rows"], 8, True)
        combine_stage(nc, k, "l2f_c", plan)


def qkv_stage(nc, k, name, w_dram, qkv, width):
    with Stage(nc, name) as st:
        w = st.sb("w", [P, DC, width])
        po = st.ps("po", [P, 4, 512])
        loaded, full, evac = st.sem("loaded"), st.sem("full"), st.sem("evac")
        with nc.Block() as block:
            @block.sync
            def _(sp):
                sp.dma_start(w[:], w_dram.rearrange("(c p) n -> p c n", p=P)).then_inc(loaded, DMA)

            @block.tensor
            def _(pe):
                pe.wait_ge(loaded, DMA)
                for t in range(TILES):
                    if t >= 4:
                        pe.wait_ge(evac, t - 3)
                    for c in range(DC):
                        mm = pe.matmul(po[:, t % 4, 0:width], k.XNT[:, c, t * P:(t + 1) * P], w[:, c, :], start=c == 0, stop=c == DC - 1)
                    mm.then_inc(full, 1)

            @block.scalar
            def _(act):
                for t in range(TILES):
                    act.wait_ge(full, t + 1)
                    act.copy(qkv[:, t, :], po[:, t % 4, 0:width]).then_inc(evac, 1)


def short_attention_stage(nc, k, name, qkv, ao):
    KV, QH = 4, 4
    W = (QH + 2) * HD
    NEG = -3.4028234663852886e38
    PAIRS_CAUSAL = [(s, t) for s in range(B) for t in range(s + 1)]
    with Stage(nc, name) as st:
        prod = st.sb("prod", [P, 2, KV, QH, HD])
        sc = st.sb("sc", [P, TPB, B, B, H])
        m, s, r = (st.sb(n, [P, TPB * B, H]) for n in ("m", "s", "r"))
        step, prod_full, prod_used, shifted, exp_done, p_ready, ao_step = (
            st.sem(n) for n in ("step", "prod_full", "prod_used", "shifted", "exp_done", "p_ready", "ao_step"))
        q5 = qkv[:].rearrange("p (s a) (g f) -> p s a g f", s=B, f=W)
        ao5 = ao.rearrange("p (s a) (g h d) -> p s a g h d", s=B, g=KV, h=QH)
        sc3 = sc[:].rearrange("p a s t h -> p (a s) t h")

        def heads(x):
            return x.unsqueeze(2).broadcast_to([P, KV, QH, HD])

        NP_ = len(PAIRS_CAUSAL)
        with nc.Block() as block:
            @block.gpsimd
            def _(pool):
                pool.sem_inc(prod_used, 2)
                with pool.Fori(0, TPB) as a:
                    for n, (sq, t) in enumerate(PAIRS_CAUSAL):
                        pool.wait_ge(prod_used, NP_ * a + n + 1)
                        pool.sem_inc(ao_step, 1)
                        q = q5[:, sq, bass.ds(a, 1), :, 0:QH * HD].rearrange("p a g (h d) -> p (a g) h d", h=QH)
                        key = q5[:, t, bass.ds(a, 1), :, QH * HD:(QH + 1) * HD].rearrange("p a g d -> p (a g) d")
                        pool.tensor_tensor(prod[:, n % 2], q, heads(key), ALU.mult).then_inc(prod_full, 1)
                pool.wait_ge(p_ready, 1)
                with pool.Fori(0, TPB) as a:
                    for n, (sq, t) in enumerate(PAIRS_CAUSAL):
                        pool.wait_ge(prod_used, NP_ * a + NP_ * TPB + n + 1)
                        pool.sem_inc(ao_step, 1)
                        v = q5[:, t, bass.ds(a, 1), :, (QH + 1) * HD:W].rearrange("p a g d -> p (a g) d")
                        prob = sc[:, bass.ds(a, 1), sq, t, :].rearrange("p a (g h) -> p (a g) h", g=KV)
                        pool.tensor_tensor(prod[:, n % 2], heads(v), prob.unsqueeze(3).broadcast_to([P, KV, QH, HD]),
                                           ALU.mult).then_inc(prod_full, 1)

            @block.scalar
            def _(act):
                act.wait_ge(shifted, 1)
                act.activation(sc3, sc3, ACT.Exp, scale=HD ** -0.5).then_inc(exp_done, 1)

            @block.vector
            def _(dve):
                dve.memset(sc[:], NEG).then_inc(step, 1)
                dve.wait_ge(step, 1)
                with dve.Fori(0, TPB) as a:
                    for n, (sq, t) in enumerate(PAIRS_CAUSAL):
                        dve.wait_ge(prod_full, NP_ * a + n + 1)
                        dve.tensor_reduce(sc[:, bass.ds(a, 1), sq, t, :].rearrange("p a (g h) -> p (a g) h", g=KV),
                                          prod[:, n % 2], AX.X, ALU.add).then_inc(prod_used, 1)
                dve.wait_ge(prod_used, NP_ * TPB + 2)
                do = Chain(dve, step, 1)
                by_head = sc3.rearrange("p n t h -> p n h t")

                def over_keys(x):
                    return x.unsqueeze(2).broadcast_to([P, TPB * B, B, H])

                do(dve.tensor_reduce(m[:], by_head, AX.X, ALU.max))
                dve.tensor_tensor(sc3, sc3, over_keys(m[:]), ALU.subtract).then_inc(shifted, 1)
                dve.wait_ge(exp_done, 1)
                do(dve.tensor_reduce(s[:], by_head, AX.X, ALU.add))
                do(dve.reciprocal(r[:], s[:]))
                dve.tensor_tensor(sc3, sc3, over_keys(r[:]), ALU.mult).then_inc(p_ready, 1)
                with dve.Fori(0, TPB) as a:
                    for n, (sq, t) in enumerate(PAIRS_CAUSAL):
                        dve.wait_ge(prod_full, NP_ * a + NP_ * TPB + n + 1)
                        out = ao5[:, sq, bass.ds(a, 1)].rearrange("p a g h d -> p (a g h d)")
                        src = prod[:, n % 2].rearrange("p g h d -> p (g h d)")
                        if t == 0:
                            dve.tensor_scalar(out, src, 1.0, None, ALU.mult).then_inc(prod_used, 1)
                        else:
                            dve.wait_ge(prod_used, NP_ * a + NP_ * TPB + n + 2)
                            dve.tensor_tensor(out, out, src, ALU.add).then_inc(prod_used, 1)


def expert_layer_1(nc, k, a):
    E, GATE = 8, 5
    with ExitStack() as ctx:
        y = ctx.enter_context(nc.sbuf_tensor("l1f_y", [P, TILES, D], F32))
        layernorm_stage(nc, k, "l1f_ln", k.X, k.XN, k.XNT)
        layernorm_stage(nc, k, "l1f_ln1", k.XN, y, k.XNT, affine=(a["ln1w"], a["ln1b"]))
        with ExitStack() as inner:
            qkv = inner.enter_context(nc.sbuf_tensor("l1f_qkv", [P, TILES, 384], F32))
            qkv_stage(nc, k, "l1f_qkv_s", a["qkvw"], qkv, 384)
            short_attention_stage(nc, k, "l1f_sa", qkv, y[:])
        transpose_stage(nc, k, "l1f_t", y, k.XNT)
        project_add_stage(nc, k, "l1f_pr", a["projw"], k.XN)
        layernorm_stage(nc, k, "l1f_ln2", k.XN, y, k.XNT, affine=(a["ln2w"], a["ln2b"]))
        gates = ctx.enter_context(nc.sbuf_tensor("l1f_gates", [P, TILES, E], F32))
        plan = Plan(nc, ctx, "l1f", E, CAPACITY, True)
        router_stage(nc, k, "l1f_r", a, k.XNT, a["r1w"], a["zero_rows"][:, 0:E], E, 2, "probs", GATE, gates, floor=False, pick=plan.pick)
        slots_stage(nc, k, "l1f_s", a, plan, gates)
        add_scaled_stage(nc, k, "l1f_x", k.XN, GATE)
        grouped_experts_stage(nc, k, "l1f_e", y, plan, a["e1rows"], 4, False)
        combine_stage(nc, k, "l1f_c", plan)


def project_add_stage(nc, k, name, w_dram, acc):
    with Stage(nc, name) as st:
        w = st.sb("w", [P, DC, D])
        po = st.ps("po", [P, 4, 512])
        loaded, full, evac = st.sem("loaded"), st.sem("full"), st.sem("evac")
        with nc.Block() as block:
            @block.sync
            def _(sp):
                sp.dma_start(w[:], w_dram.rearrange("(c p) n -> p c n", p=P)).then_inc(loaded, DMA)

            @block.tensor
            def _(pe):
                pe.wait_ge(loaded, DMA)
                for t in range(TILES):
                    if t >= 4:
                        pe.wait_ge(evac, t - 3)
                    for c in range(DC):
                        mm = pe.matmul(po[:, t % 4, 0:D], k.XNT[:, c, t * P:(t + 1) * P], w[:, c, :], start=c == 0, stop=c == DC - 1)
                    mm.then_inc(full, 1)

            @block.vector
            def _(dve):
                for t in range(TILES):
                    dve.wait_ge(full, t + 1)
                    dve.tensor_tensor(acc[:, t, :], po[:, t % 4, 0:D], acc[:, t, :], ALU.add).then_inc(evac, 1)


def add_scaled_stage(nc, k, name, src, gate):
    with Stage(nc, name) as st:
        done = st.sem("done")
        with nc.Block() as block:
            @block.vector
            def _(dve):
                dve.scalar_tensor_tensor(out=k.X[:].rearrange("p t d -> p (t d)"), in0=src.rearrange("p t d -> p (t d)"),
                                         scalar=k.tg[:, gate:gate + 1], in1=k.X[:].rearrange("p t d -> p (t d)"),
                                         op0=ALU.mult, op1=ALU.add).then_inc(done, 1)
                dve.wait_ge(done, 1)


def single_head_stage(nc, k, name, qT, kT, v, scale, out, gate=None):
    with Stage(nc, name) as st:
        qb = [st.sb(f"qb{u}", [P, DC, S]) for u in range(2)]
        prob = st.sb("prob", [P, 2, S])
        pT = st.sb("pT", [P, 2, TPB, P])
        negm = st.sb("negm", [P, 2])
        nbias = st.sb("nbias", [P, 2])
        psum_row = st.sb("sum", [P, 2])
        rinv = st.sb("rinv", [P, 2])
        ps_s = st.ps("ps_s", [P, 2, S])
        ps_t = st.ps("ps_t", [P, 2, TPB, P])
        ps_o = st.ps("ps_o", [P, 2, 512])
        (qb_ready, s_full, negm_done, nbias_done, exp_done, t_full, t_evac, o_full, o_evac, r_step, tick) = (
            st.sem(n) for n in ("qb_ready", "s_full", "negm_done", "nbias_done", "exp_done", "t_full", "t_evac",
                                "o_full", "o_evac", "r_step", "tick"))
        PER = 2 * TPB
        with nc.Block() as block:
            @block.gpsimd
            def _(pool):
                with pool.Fori(0, B // 2) as it:
                    for u in range(2):
                        pool.wait_ge(s_full, PER * it + 1)
                        pool.sem_inc(tick, 1)
                        pool.tensor_copy(qb[u][:], qT[:, :, bass.ds((2 * it + u) * S, S)]).then_inc(qb_ready, 1)

            @block.tensor
            def _(pe):
                pe.sem_inc(s_full, 1)
                pe.sem_inc(t_full, 1)
                pe.sem_inc(o_full, 2)
                with pe.Fori(0, B // 2) as it:
                    def scores(n):
                        u, qt = divmod(n, TPB)
                        if qt == 0:
                            pe.wait_ge(qb_ready, 2 * it + u + 1)
                        pe.wait_ge(exp_done, PER * it + n + 1)
                        for c in range(DC):
                            mm = pe.matmul(ps_s[:, n % 2, :], qb[u][:, c, qt * P:(qt + 1) * P],
                                           kT[:, c, bass.ds((2 * it + u) * S, S)], start=c == 0, stop=c == DC - 1)
                        mm.then_inc(s_full, 1)

                    def transposes(n):
                        pe.wait_ge(exp_done, PER * it + n + 1 + 2)
                        pe.wait_ge(t_evac, PER * it + n + 1)
                        for kt in range(TPB):
                            mm = pe.transpose(ps_t[:, n % 2, kt, :], prob[:, n % 2, kt * P:(kt + 1) * P], k.ident[:])
                        mm.then_inc(t_full, 1)

                    def values(n):
                        pe.wait_ge(t_evac, PER * it + n + 1 + 2)
                        pe.wait_ge(o_evac, PER * it + n + 1)
                        for kt in range(TPB):
                            mm = pe.matmul(ps_o[:, n % 2, 0:D], pT[:, n % 2, kt, :],
                                           v[:, bass.ds((2 * it + n // TPB) * TPB + kt, 1), :], start=kt == 0, stop=kt == TPB - 1)
                        mm.then_inc(o_full, 1)

                    scores(0)
                    for n in range(PER):
                        if n + 1 < PER:
                            scores(n + 1)
                        if n:
                            values(n - 1)
                        transposes(n)
                    values(PER - 1)

            @block.scalar
            def _(act):
                act.sem_inc(exp_done, 2)
                with act.Fori(0, B // 2) as it:
                    for n in range(PER):
                        act.wait_ge(nbias_done, PER * it + n + 1 + 1)
                        act.wait_ge(t_full, PER * it + n + 1)
                        act.wait_ge(r_step, PER * it + n + 1)
                        act.activation(prob[:, n % 2, :], ps_s[:, n % 2, :], ACT.Exp, bias=nbias[:, n % 2:n % 2 + 1], scale=scale,
                                       accum_out=psum_row[:, n % 2:n % 2 + 1]).then_inc(exp_done, 1)

            @block.vector
            def _(dve):
                dve.sem_inc(t_evac, 2)
                dve.sem_inc(o_evac, 2)
                dve.sem_inc(r_step, 2)
                dve.sem_inc(nbias_done, 1)
                with dve.Fori(0, B // 2) as it:
                    def row_max(n):
                        dve.wait_ge(s_full, PER * it + n + 1 + 1)
                        dve.wait_ge(nbias_done, PER * it + n + 1)
                        dve.tensor_reduce(negm[:, n % 2:n % 2 + 1], ps_s[:, n % 2, :], AX.X, ALU.max, negate=True).then_inc(negm_done, 1)
                        dve.wait_ge(negm_done, PER * it + n + 1)
                        dve.wait_ge(exp_done, PER * it + n + 1)
                        dve.tensor_scalar(nbias[:, n % 2:n % 2 + 1], negm[:, n % 2:n % 2 + 1], scale, None, ALU.mult).then_inc(nbias_done, 1)

                    def finish(n):
                        dve.wait_ge(exp_done, PER * it + n + 1 + 2)
                        dve.wait_ge(o_evac, PER * it + n + 2)
                        dve.reciprocal(rinv[:, n % 2:n % 2 + 1], psum_row[:, n % 2:n % 2 + 1]).then_inc(r_step, 1)
                        dve.wait_ge(o_full, PER * it + n + 1 + 2)
                        dve.wait_ge(r_step, PER * it + n + 1 + 2)
                        tile = bass.ds(PER * it + n, 1)
                        o = out[:, tile, :].rearrange("p t d -> p (t d)")
                        if gate is None:
                            dve.tensor_scalar(o, ps_o[:, n % 2, 0:D], rinv[:, n % 2:n % 2 + 1], None, ALU.mult).then_inc(o_evac, 1)
                        else:
                            dve.scalar_tensor_tensor(out=o, in0=ps_o[:, n % 2, 0:D], scalar=rinv[:, n % 2:n % 2 + 1], in1=o,
                                                     op0=ALU.mult, op1=ALU.add).then_inc(o_evac, 1)

                    row_max(0)
                    for n in range(PER):
                        if n + 1 < PER:
                            row_max(n + 1)
                        if n:
                            finish(n - 1)
                        dve.wait_ge(t_full, PER * it + n + 1 + 1)
                        dve.wait_ge(o_full, PER * it + n + 1)
                        dve.tensor_copy(pT[:, n % 2], ps_t[:, n % 2]).then_inc(t_evac, 1)
                    finish(PER - 1)


def feature_major_stage(nc, k, name, w_dram, bias_dram, dst_T):
    with Stage(nc, name) as st:
        w = st.sb("w", [P, DC, D])
        bias = st.sb("bias", [P, DC])
        po = st.ps("po", [P, 4, 512])
        loaded, full, evac = st.sem("loaded"), st.sem("full"), st.sem("evac")
        with nc.Block() as block:
            @block.sync
            def _(sp):
                sp.dma_start(w[:], w_dram.rearrange("(c p) n -> p c n", p=P)).then_inc(loaded, DMA)
                sp.dma_start(bias[:], bias_dram).then_inc(loaded, DMA)

            @block.tensor
            def _(pe):
                pe.wait_ge(loaded, 2 * DMA)
                for n in range(DC * B):
                    m, b = divmod(n, B)
                    if n >= 4:
                        pe.wait_ge(evac, n - 3)
                    for c in range(DC):
                        mm = pe.matmul(po[:, n % 4, :], w[:, c, m * P:(m + 1) * P], k.XNT[:, c, b * S:(b + 1) * S], start=c == 0, stop=c == DC - 1)
                    mm.then_inc(full, 1)

            @block.scalar
            def _(act):
                act.wait_ge(loaded, 2 * DMA)
                for n in range(DC * B):
                    m, b = divmod(n, B)
                    act.wait_ge(full, n + 1)
                    act.activation(dst_T[:, m, b * S:(b + 1) * S], po[:, n % 4, :], ACT.Identity, bias=bias[:, m:m + 1]).then_inc(evac, 1)


def fuse_stage(nc, k, name, w_dram, bias_dram, oT, gate):
    with Stage(nc, name) as st:
        w = st.sb("w", [P, 2 * DC, D])
        bias = st.sb("bias", [P, D])
        po = st.ps("po", [P, 4, 512])
        loaded, full, evac, step = st.sem("loaded"), st.sem("full"), st.sem("evac"), st.sem("step")
        with nc.Block() as block:
            @block.sync
            def _(sp):
                sp.dma_start(w[:], w_dram.rearrange("(c p) n -> p c n", p=P)).then_inc(loaded, DMA)
                sp.dma_start(bias[:], bias_dram).then_inc(loaded, DMA)

            @block.tensor
            def _(pe):
                pe.wait_ge(loaded, 2 * DMA)
                for t in range(TILES):
                    if t >= 4:
                        pe.wait_ge(evac, t - 3)
                    for c in range(2 * DC):
                        src = k.XNT if c < DC else oT
                        mm = pe.matmul(po[:, t % 4, 0:D], src[:, c % DC, t * P:(t + 1) * P], w[:, c, :], start=c == 0, stop=c == 2 * DC - 1)
                    mm.then_inc(full, 1)

            @block.vector
            def _(dve):
                dve.wait_ge(loaded, 2 * DMA)
                do = Chain(dve, step)
                do(dve.tensor_scalar(bias[:], bias[:], k.tg[:, gate:gate + 1], None, ALU.mult))
                do(dve.tensor_tensor(k.X[:], k.X[:], bias[:].unsqueeze(1).broadcast_to([P, TILES, D]), ALU.add))
                for t in range(TILES):
                    dve.wait_ge(full, t + 1)
                    dve.scalar_tensor_tensor(out=k.X[:, t, :], in0=po[:, t % 4, 0:D], scalar=k.tg[:, gate:gate + 1],
                                             in1=k.X[:, t, :], op0=ALU.mult, op1=ALU.add).then_inc(evac, 1)


def knowledge_layer(nc, k, a):
    layernorm_stage(nc, k, "l2x_ln", k.X, k.XN, k.XNT)
    with ExitStack() as ctx:
        def sb(name):
            return ctx.enter_context(nc.sbuf_tensor("l2x_" + name, [P, DC, B * S], F32))
        qT, ctxT, v = sb("qT"), sb("ctxT"), ctx.enter_context(nc.sbuf_tensor("l2x_v", [P, TILES, D], F32))
        with Stage(nc, "l2x_ld") as st:
            loaded = st.sem("loaded")
            with nc.Block() as block:
                @block.sync
                def _(sp):
                    sp.dma_start(ctxT[:], a["ctxT"].rearrange("(c p) n -> p c n", p=P)).then_inc(loaded, DMA)
                    sp.dma_start(v[:], a["ctx"].rearrange("(t p) d -> p t d", p=P)).then_inc(loaded, DMA)
                    sp.wait_ge(loaded, 2 * DMA)
        feature_major_stage(nc, k, "l2x_q", a["w2x1"], a["b2x1"], qT)
        single_head_stage(nc, k, "l2x_a", qT, ctxT, v, D ** -0.5, k.XN)
        transpose_stage(nc, k, "l2x_t", k.XN, qT)
        fuse_stage(nc, k, "l2x_f", a["w2x2"], a["b2x2"], qT, 2)


def tree_stage(nc, k, name, a, node_w, node_b, sel_T, sel_Tb):
    NODES, LEAVES = 15, 16
    with Stage(nc, name) as st:
        w = st.sb("w", [P, DC, NODES])
        nb = st.sb("nb", [P, NODES])
        bit = st.sb("bit", [P, TILES, NODES])
        ind = [st.sb(f"ind{lv}", [P, TILES, 2 ** (lv + 1)]) for lv in range(4)]
        ps = st.ps("ps_n", [P, TILES, NODES])
        tp = st.ps("tp", [LEAVES, TILES, P])
        loaded, full, step, sel_done, t_full = (st.sem(n) for n in ("loaded", "full", "step", "sel_done", "t_full"))
        with nc.Block() as block:
            @block.sync
            def _(sp):
                sp.dma_start(w[:], node_w.rearrange("(c p) e -> p c e", p=P)).then_inc(loaded, DMA)
                sp.dma_start(nb[:], node_b).then_inc(loaded, DMA)

            @block.tensor
            def _(pe):
                pe.wait_ge(loaded, 2 * DMA)
                for t in range(TILES):
                    for c in range(DC):
                        mm = pe.matmul(ps[:, t, :], k.XNT[:, c, t * P:(t + 1) * P], w[:, c, :], start=c == 0, stop=c == DC - 1)
                mm.then_inc(full, 1)
                pe.wait_ge(sel_done, 1)
                for t in range(TILES):
                    mm = pe.transpose(tp[:, t, :], ind[3][:, t, :], k.ident[:])
                mm.then_inc(t_full, 1)

            @block.vector
            def _(dve):
                do = Chain(dve, step)
                dve.wait_ge(loaded, 2 * DMA)
                dve.wait_ge(full, 1)
                do(dve.tensor_tensor(bit[:], ps[:], nb[:].unsqueeze(1).broadcast_to([P, TILES, NODES]), ALU.add))
                do(dve.tensor_scalar(bit[:], bit[:], 0.0, None, ALU.is_ge))
                do(dve.tensor_copy(ind[0][:, :, 1:2], bit[:, :, 0:1]))
                do(dve.tensor_scalar(ind[0][:, :, 0:1], bit[:, :, 0:1], -1.0, 1.0, ALU.mult, ALU.add))
                for lv in range(1, 4):
                    n = 2 ** lv
                    kids = ind[lv][:].rearrange("p t (n two) -> p t n two", two=2)
                    do(dve.tensor_tensor(kids[:, :, :, 1], ind[lv - 1][:], bit[:, :, n - 1:2 * n - 1], ALU.mult))
                    do(dve.tensor_tensor(kids[:, :, :, 0], ind[lv - 1][:], kids[:, :, :, 1], ALU.subtract))
                dve.sem_inc(sel_done, 1)
                dve.wait_ge(t_full, 1)
                do(dve.tensor_copy(sel_T, tp[:].rearrange("l t p -> l (t p)")))
                do(dve.tensor_copy(sel_Tb, sel_T))


def leaves_stage(nc, k, name, a, w1, b1, w2, b2, sel_T, sel_Tb, dst, feature_major):
    FC = 8
    LEAVES = 16
    with Stage(nc, name) as st:
        w1s = st.sb("w1", [P, DC, FC * P])
        w2s = st.sb("w2", [P, FC, D])
        b1s = st.sb("b1", [P, FC])
        b2s = st.sb("b2", [LEAVES, D])
        spread = st.sb("spread", [LEAVES, FC * P], BF16)
        spread_f = st.sb("spread_f", [LEAVES, FC * P])
        selb = st.sb("selb", [LEAVES, S])
        relu = st.sb("relu", [P, 2, S])
        ht = st.sb("ht", [P, FC, S])
        ph = st.ps("ph", [P, 2, S])
        pm = st.ps("pm", [P, 2, S])
        po = st.ps("po", [P, 4, 512])
        loaded, spread_done, selb_ready, h_full, relu_done, h_ready, o_full, o_evac, tick = (
            st.sem(n) for n in ("loaded", "spread_done", "selb_ready", "h_full", "relu_done", "h_ready", "o_full", "o_evac", "tick"))
        NO = DC if feature_major else TPB
        with nc.Block() as block:
            @block.sync
            def _(sp):
                for c in range(DC):
                    sp.dma_start(w1s[:, c, :].rearrange("p (l h) -> p l h", l=LEAVES),
                                 w1[:, c * P:(c + 1) * P, :].rearrange("l p h -> p l h")).then_inc(loaded, DMA)
                sp.dma_start(w2s[:], w2.rearrange("(j two) h n -> (two h) j n", two=2)).then_inc(loaded, DMA)
                sp.dma_start(b1s[:], b1).then_inc(loaded, DMA)
                sp.dma_start(b2s[:], b2).then_inc(loaded, DMA)
                sp.dma_start(spread_f[:], a["spread"]).then_inc(loaded, DMA)

            @block.gpsimd
            def _(pool):
                with pool.Fori(0, B) as b:
                    pool.wait_ge(o_full, NO * b + 1)
                    pool.sem_inc(tick, 1)
                    pool.tensor_copy(selb[:], sel_T[:, bass.ds(b * S, S)]).then_inc(selb_ready, 1)

            @block.tensor
            def _(pe):
                pe.wait_ge(loaded, 6 * DMA)
                pe.wait_ge(spread_done, 1)
                pe.sem_inc(o_full, 1)
                with pe.Fori(0, B) as b:
                    row = bass.ds(b * S, S)
                    for j in range(FC):
                        pe.wait_ge(h_ready, FC * b + j + 1)
                        for c in range(DC):
                            pe.matmul(ph[:, j % 2, :], w1s[:, c, j * P:(j + 1) * P], k.XNT[:, c, row], start=c == 0, stop=c == DC - 1)
                        pe.matmul(pm[:, j % 2, :], spread[:, j * P:(j + 1) * P], sel_Tb[:, row], start=True, stop=True).then_inc(h_full, 1)
                    pe.wait_ge(selb_ready, b + 1)
                    for n in range(NO):
                        pe.wait_ge(h_ready, FC * b + FC + 2)
                        pe.wait_ge(o_evac, NO * b + n + 1)
                        for j in range(FC):
                            if feature_major:
                                pe.matmul(po[:, n, :], w2s[:, j, n * P:(n + 1) * P], ht[:, j, :], start=j == 0, stop=False)
                            else:
                                pe.matmul(po[:, n, 0:D], ht[:, j, n * P:(n + 1) * P], w2s[:, j, :], start=j == 0, stop=False)
                        if feature_major:
                            mm = pe.matmul(po[:, n, :], b2s[:, n * P:(n + 1) * P], selb[:], start=False, stop=True)
                        else:
                            mm = pe.matmul(po[:, n, 0:D], selb[:, n * P:(n + 1) * P], b2s[:], start=False, stop=True)
                        mm.then_inc(o_full, 1)

            @block.scalar
            def _(act):
                act.sem_inc(o_evac, NO)
                act.wait_ge(loaded, 6 * DMA)
                with act.Fori(0, B) as b:
                    for j in range(FC):
                        act.wait_ge(h_full, FC * b + j + 1)
                        act.wait_ge(h_ready, FC * b + j + 1)
                        act.activation(relu[:, j % 2, :], ph[:, j % 2, :], ACT.Relu, bias=b1s[:, j:j + 1]).then_inc(relu_done, 1)
                    for n in range(NO):
                        act.wait_ge(o_full, NO * b + n + 1 + 1)
                        act.sem_inc(tick, 1)
                        if feature_major:
                            act.copy(dst[:, n, bass.ds(b * S, S)], po[:, n, :]).then_inc(o_evac, 1)
                        else:
                            act.copy(dst[:, bass.ds(TPB * b + n, 1), :].rearrange("p t d -> p (t d)"), po[:, n, 0:D]).then_inc(o_evac, 1)

            @block.vector
            def _(dve):
                dve.sem_inc(h_ready, 2)
                dve.wait_ge(loaded, 6 * DMA)
                dve.tensor_copy(spread[:], spread_f[:]).then_inc(spread_done, 1)
                with dve.Fori(0, B) as b:
                    for j in range(FC):
                        dve.wait_ge(relu_done, FC * b + j + 1)
                        dve.tensor_tensor(ht[:, j, :], pm[:, j % 2, :], relu[:, j % 2, :], ALU.mult).then_inc(h_ready, 1)


def scale_values_stage(nc, k, name, v, gate):
    with Stage(nc, name) as st:
        done = st.sem("done")
        with nc.Block() as block:
            @block.vector
            def _(dve):
                dve.tensor_scalar(v, v, k.tg[:, gate:gate + 1], None, ALU.mult).then_inc(done, 1)
                dve.wait_ge(done, 1)


def tree_layer(nc, k, a):
    layernorm_stage(nc, k, "l3f_ln", k.X, k.XN, k.XNT)
    with ExitStack() as ctx:
        def sb(name, shape, dt=F32):
            return ctx.enter_context(nc.sbuf_tensor("l3f_" + name, shape, dt))
        qT, kT, v = sb("qT", [P, DC, B * S]), sb("kT", [P, DC, B * S]), sb("v", [P, TILES, D])
        with ExitStack() as inner:
            sel_T = inner.enter_context(nc.sbuf_tensor("l3f_selT", [16, B * S], F32))
            sel_Tb = inner.enter_context(nc.sbuf_tensor("l3f_selTb", [16, B * S], BF16))
            for x, dst in (("q", qT), ("k", kT), ("v", v)):
                tree_stage(nc, k, f"l3f_{x}t", a, a[f"t{x}nw"], a[f"t{x}nb"], sel_T[:], sel_Tb[:])
                leaves_stage(nc, k, f"l3f_{x}l", a, a[f"t{x}w1"], a[f"t{x}b1"], a[f"t{x}w2"], a[f"t{x}b2"], sel_T, sel_Tb, dst, x != "v")
        scale_values_stage(nc, k, "l3f_g", v[:], 7)
        single_head_stage(nc, k, "l3f_a", qT, kT, v, D ** -0.5, k.X, gate=7)


def more_stages(nc, k, a):
    return [
        lambda: expert_layer_0(nc, k, a),
        lambda: attention_layer(nc, k, "l1x", a, a["w1q"], a["w1k"], a["w1v"], a["zero_col"], a["zero_col"], a["zero_rows"],
                                a["w1o"], a["b1o"], D ** -0.5, 1, mask=(a["m1"], a["m1T"], True)),
        lambda: expert_layer_1(nc, k, a),
        lambda: knowledge_layer(nc, k, a),
        lambda: expert_layer_2(nc, k, a),
        lambda: attention_layer(nc, k, "l3x", a, a["w3q"], a["w3k"], a["w3v"], a["b3q"], a["b3k"], a["b3v"], a["w3o"],
                                a["b3o"], HD ** -0.5, 3, tril2=a["tril2"]),
        lambda: tree_layer(nc, k, a),
    ]


def more_layout(n, all_rows, columns, T):
    import numpy as np
    f32 = np.float32

    def expert_rows(w1, w2, b1=None):
        E = w1.shape[0]
        parts = [w1.reshape(E, DC, P, -1).transpose(0, 2, 1, 3), w2.reshape(E, -1, P, D).transpose(0, 2, 1, 3)]
        if b1 is not None:
            parts.append(b1.reshape(E, -1, P).transpose(0, 2, 1))
        return np.concatenate([x.reshape(E * P, -1) for x in parts], 1)

    a = {f"ranks{E}": all_rows(np.arange(E, 0, -1).astype(f32)) for E in (8, 16)}
    a["before"] = np.triu(np.ones((P, P), f32), 1)
    a |= {"r0w": T(n["L0_ffn_router_w"]), "r0b": all_rows(n["L0_ffn_router_b"]), "e0w": n["L0_ffn_expert_w"]}
    a |= {"r2w": T(n["L2_ffn_router_w"]), "r2b": all_rows(n["L2_ffn_router_b"]), "e2b2": n["L2_ffn_b2"],
          "e2rows": expert_rows(T(n["L2_ffn_w1"]), T(n["L2_ffn_w2"]), n["L2_ffn_b1"])}
    p = "L1_ffn_"
    for x in ("ln1", "ln2"):
        a |= {x + "w": all_rows(n[p + x + "_weight"]), x + "b": all_rows(n[p + x + "_bias"])}
    a |= {"qkvw": T(n[p + "qkv_weight"]), "projw": T(n[p + "proj_weight"]), "r1w": n[p + "router_weight"],
          "e1rows": expert_rows(n[p + "moe_w1"], n[p + "moe_w2"])}
    a["first_slots"] = all_rows((CAPACITY * np.arange(8)).astype(f32))
    a["spare_slots"] = (8 * CAPACITY + np.arange(2 * B * S)).reshape(2, TILES, P).transpose(2, 0, 1).astype(f32)
    a["index"] = all_rows(np.arange(2 * TILES).astype(f32))
    a["lane"] = np.arange(P).astype(f32).reshape(P, 1)
    p = "L2_xattn_"
    a |= {"w2x1": T(n[p + "w1_w"]), "b2x1": columns(n[p + "w1_b"]), "w2x2": T(n[p + "w2_w"]), "b2x2": all_rows(n[p + "w2_b"])}
    for x in "qkv":
        p = f"L3_ffn_{x}_"
        a |= {f"t{x}nw": T(n[p + "node_w"]), f"t{x}nb": all_rows(n[p + "node_b"]), f"t{x}w1": n[p + "w1"],
              f"t{x}b1": columns(n[p + "b1"].reshape(-1)), f"t{x}w2": n[p + "w2"], f"t{x}b2": n[p + "b2"]}
    a["spread"] = np.kron(np.eye(16, dtype=f32), np.ones((1, 64), f32))
    return a


_OUT = (B, S, D)


def build(nc, a, out, stop=99):
    k = Held()
    with ExitStack() as ctx:
        k.X = ctx.enter_context(nc.sbuf_tensor("X", [P, TILES, D], F32))
        norm = ctx.enter_context(nc.sbuf_tensor("norm", [P, 2 * TILES * D], F32))
        k.XN = norm[:, 0:TILES * D].rearrange("p (t d) -> p t d", t=TILES)
        k.XNT = norm[:, TILES * D:].rearrange("p (c n) -> p c n", c=DC)
        k.ATN = norm[:].rearrange("p (g n) -> p g n", g=B * GROUPS)
        k.tg = ctx.enter_context(nc.sbuf_tensor("tg", [P, 8], F32))
        k.ident = ctx.enter_context(nc.sbuf_tensor("ident_f32", [P, P], F32))
        k.ident_bf = ctx.enter_context(nc.sbuf_tensor("ident_bf", [P, P], BF16))
        k.qk_dram = nc.dram_tensor("qk_parts", [2, 3, B * GROUPS, GH, HD, S], BF16, kind="Internal").ap()
        k.slot_x = nc.dram_tensor("slot_x", [8 * CAPACITY + 2 * B * S, D], F32, kind="Internal").ap()
        k.slot_y = nc.dram_tensor("slot_y", [FILL_ROWS, D], F32, kind="Internal").ap()
        load_stage(nc, k, a)
        stages = [
            lambda: attention_layer(nc, k, "l0x", a, a["w0q"], a["w0k"], a["w0v"], a["b0q"], a["b0k"], a["b0v"], a["w0o"],
                                    a["b0o"], HD ** -0.5, 0, mask=(a["m0"], a["m0T"], False)),
        ] + more_stages(nc, k, a)
        for n, stage in enumerate(stages):
            if n in range(*(stop if isinstance(stop, tuple) else (0, stop))):
                stage()
        store_stage(nc, k, out)


def store_stage(nc, k, out):
    with Stage(nc, "store") as st:
        stored = st.sem("stored")
        with nc.Block() as block:
            @block.sync
            def _(sp):
                sp.dma_start(out.rearrange("b (t p) d -> p (b t) d", p=P), k.X[:]).then_inc(stored, DMA)
                sp.wait_ge(stored, DMA)


def lay_out(v):
    import numpy as np
    n = {name: np.asarray(x) for name, x in v.items()}
    f32 = np.float32

    def all_rows(x):
        return np.ascontiguousarray(np.broadcast_to(x.reshape(1, -1), (P, x.size)))

    def columns(x):
        return np.ascontiguousarray(x.reshape(-1, P).T)

    def heads(w):
        full = np.zeros((H, HD, H, HD), w.dtype)
        for h in range(H):
            full[h, :, h, :] = w.T
        return full.reshape(D, D)

    def strips(w):
        full = np.zeros((GH, STRIP, GROUPS, w.shape[1]), w.dtype)
        full[:, :HD] = w.reshape(GROUPS, GH, HD, -1).transpose(1, 2, 0, 3)
        return full.reshape(P, GROUPS, -1)

    def T(x):
        return np.ascontiguousarray(np.swapaxes(x, -1, -2))

    selsum = np.zeros((P, GH), f32)
    for i in range(GH):
        selsum[STRIP * i + HD, i] = 1.0
    zero = np.zeros(D, f32)
    m0 = n["mask_SxS2_bk1"]
    m1 = n["mask_Bx1xSxS2_ik1"].reshape(B, S, S)
    a = {
        "x": n["x"].reshape(B * S, D),
        "ctx": n["ctx_1024"].reshape(B * S, D),
        "ctxT": T(n["ctx_1024"].reshape(B * S, D)),
        "gates": all_rows(np.concatenate([n["g_xattn"], n["g_ffn"]])),
        "ident": np.eye(P, dtype=f32),
        "selsum": selsum,
        "tril2": (1.0 + np.triu(np.ones((P, P)))).astype(f32),
        "m0": m0, "m0T": T(m0),
        "m1": m1.reshape(B * S, S), "m1T": T(m1).reshape(B * S, S),
    }
    for layer in (0, 3):
        p = f"L{layer}_xattn_"
        a |= {f"w{layer}q": n[p + "Wq"], f"w{layer}k": n[p + "Wk"], f"w{layer}v": n[p + "Wv"],
              f"b{layer}q": columns(n[p + "bq"]), f"b{layer}k": columns(n[p + "bk"]), f"b{layer}v": all_rows(n[p + "bv"]),
              f"w{layer}o": strips(n[p + "Wo"]), f"b{layer}o": all_rows(n[p + "bo"])}
    p = "L1_xattn_"
    a |= {"w1q": heads(n[p + "Wq"]), "w1k": heads(n[p + "Wk"]), "w1v": heads(n[p + "Wv"]), "zero_col": columns(zero),
          "zero_rows": all_rows(zero), "w1o": strips(T(n[p + "Wo"])), "b1o": all_rows(n[p + "bo"])}
    a |= more_layout(n, all_rows, columns, T)
    return {name: np.ascontiguousarray(x) for name, x in a.items()}


def kernel(**inputs):
    import concourse.bacc as bacc
    from concourse.bass_utils import run_bass_kernel_spmd

    nc = bacc.Bacc("TRN2", target_bir_lowering=False, num_devices=1)
    arrays = lay_out(inputs)
    args = {name: nc.dram_tensor(name, x.shape, mybir.dt.from_np(x.dtype), kind="ExternalInput").ap()
            for name, x in arrays.items()}
    out = nc.dram_tensor("out", _OUT, F32, kind="ExternalOutput").ap()
    build(nc, args, out)
    return run_bass_kernel_spmd(nc, [arrays], core_ids=[0]).results[0]["out"]
```

```python
from contextlib import ExitStack

import concourse.bass as bass
from concourse import mybir

F32 = mybir.dt.float32
BF16 = mybir.dt.bfloat16
F32R = mybir.dt.float32r
U32 = mybir.dt.uint32
ALU = mybir.AluOpType
ACT = mybir.ActivationFunctionType
AX = mybir.AxisListType

P = 128
B, S, D = 4, 512, 256
TILES = B * S // P
TPB = S // P
DC = D // P
H, HD = 16, 16
GH = 4
GROUPS = H // GH
STRIP = 32
LN_EPS = 1e-5
MASKED = -(2.0 ** 100)
Q_PART = (0, 0, 1, 1, 0, 2)
K_PART = (0, 1, 0, 1, 2, 0)
PAIRS = len(Q_PART)
STACK = PAIRS * HD
MROWS = 2
CAPACITY = 640
GROUP = 256
FILL_ROWS = 24 * GROUP
DMA = 16


class Stage:

    def __init__(self, nc, name):
        self.nc, self.name, self.ctx, self.sems = nc, name, ExitStack(), []

    def __enter__(self):
        return self

    def __exit__(self, *exc):
        if exc[0] is None:
            self.nc.clear_and_free_semaphores(self.sems)
            self.nc.all_engine_barrier()
        self.ctx.close()

    def sb(self, name, shape, dt=F32):
        return self.ctx.enter_context(self.nc.sbuf_tensor(f"{self.name}_{name}", shape, dt))

    def ps(self, name, shape, dt=F32):
        return self.ctx.enter_context(self.nc.psum_tensor(f"{self.name}_{name}", shape, dt))

    def sem(self, name):
        s = self.nc.alloc_semaphore(f"{self.name}_{name}")
        self.sems.append(s)
        return s


class Held:
    pass


def at(i, n=1):
    return slice(i, i + n) if isinstance(i, int) else bass.ds(i, n)


def load_stage(nc, k, a):
    with Stage(nc, "load") as st:
        loaded, tanh_done, cast_done = st.sem("loaded"), st.sem("tanh_done"), st.sem("cast_done")
        graw = st.sb("graw", [P, 8])
        with nc.Block() as block:
            @block.sync
            def _(sp):
                sp.dma_start(k.X[:], a["x"].rearrange("(t p) d -> p t d", p=P)).then_inc(loaded, DMA)
                sp.dma_start(graw[:], a["gates"]).then_inc(loaded, DMA)
                sp.dma_start(k.ident[:], a["ident"]).then_inc(loaded, DMA)
                sp.wait_ge(loaded, 3 * DMA)

            @block.scalar
            def _(act):
                act.wait_ge(loaded, 3 * DMA)
                act.activation(k.tg[:], graw[:], ACT.Tanh).then_inc(tanh_done, 1)
                act.wait_ge(tanh_done, 1)

            @block.vector
            def _(dve):
                dve.wait_ge(loaded, 3 * DMA)
                dve.tensor_copy(k.ident_bf[:], k.ident[:]).then_inc(cast_done, 1)
                dve.wait_ge(cast_done, 1)


def row_stats(dve, k, src, t, written, count, done):
    dve.wait_ge(written, count)
    dve.bn_stats(k.stats[:, t, :], src[:, t, :]).then_inc(done, 1)


def layernorm_stage(nc, k, name, src, dst, dst_T=None, affine=None, prefetch=(), fill=None, have_stats=True):
    with Stage(nc, name) as st:
        mv = st.sb("mv", [P, TILES, 2])
        std = st.sb("std", [P, TILES])
        rstd = st.sb("rstd", [P, TILES])
        shift = st.sb("shift", [P, TILES])
        eps = st.sb("eps", [P, 1])
        wb = st.sb("wb", [P, 2, D]) if affine else None
        tp = st.ps("tp", [P, 4, 512])
        stat_step, aggr_done, std_done = st.sem("stat_step"), st.sem("aggr_done"), st.sem("std_done")
        scale_step, normed, tp_full = st.sem("scale_step"), st.sem("normed"), st.sem("tp_full")
        weighted, even_done, odd_done = st.sem("weighted"), st.sem("even_done"), st.sem("odd_done")
        act_evac, dve_evac, wb_loaded = st.sem("act_evac"), st.sem("dve_evac"), st.sem("wb_loaded")
        prefetched, filled = st.sem("prefetched"), st.sem("filled")
        with nc.Block() as block:
            @block.sync
            def _(sp):
                if affine:
                    for j in range(2):
                        sp.dma_start(wb[:, j, :], affine[j]).then_inc(wb_loaded, DMA)
                for to, what in prefetch:
                    sp.dma_start(to, what).then_inc(prefetched, DMA)
                if prefetch:
                    sp.wait_ge(prefetched, DMA * len(prefetch))

            @block.gpsimd
            def _(pool):
                if fill:
                    fill(pool, filled)
                if affine:
                    pool.wait_ge(wb_loaded, 2 * DMA)
                    for t in range(0, TILES, 2):
                        pool.wait_ge(weighted, t + 1)
                        pool.tensor_tensor(dst[:, t, :], dst[:, t, :], wb[:, 1, :], ALU.add).then_inc(even_done, 1)

            @block.vector
            def _(dve):
                dve.memset(eps[:], LN_EPS).then_inc(stat_step, 1)
                if not have_stats:
                    for t in range(TILES):
                        dve.bn_stats(k.stats[:, t, :], src[:, t, :]).then_inc(stat_step, 1)
                for t in range(TILES):
                    dve.wait_ge(stat_step, 1 if have_stats else t + 2)
                    dve.bn_aggr(mv[:, t, :], k.stats[:, t, :]).then_inc(aggr_done, 1)
                dve.wait_ge(std_done, 1)
                dve.reciprocal(rstd[:], std[:]).then_inc(scale_step, 1)
                dve.wait_ge(scale_step, 1)
                dve.scalar_tensor_tensor(out=shift[:], in0=mv[:, :, 0], scalar=-1.0, in1=rstd[:],
                                         op0=ALU.mult, op1=ALU.mult).then_inc(scale_step, 1)
                if affine:
                    def add_bias(t):
                        dve.wait_ge(weighted, t + 1)
                        dve.tensor_tensor(dst[:, t, :], dst[:, t, :], wb[:, 1, :], ALU.add).then_inc(odd_done, 1)

                    dve.wait_ge(wb_loaded, 2 * DMA)
                    for t in range(TILES):
                        dve.wait_ge(normed, t + 1)
                        dve.tensor_tensor(dst[:, t, :], dst[:, t, :], wb[:, 0, :], ALU.mult).then_inc(weighted, 1)
                        if t and t % 2 == 0:
                            add_bias(t - 1)
                    add_bias(TILES - 1)
                else:
                    dve.wait_ge(scale_step, 2)
                    for t in range(1, TILES, 2):
                        dve.tensor_scalar(dst[:, t, :], src[:, t, :], rstd[:, t:t + 1], shift[:, t:t + 1],
                                          ALU.mult, ALU.add).then_inc(odd_done, 1)
                if dst_T is not None:
                    for n in range(1, DC * B, 2):
                        dve.wait_ge(tp_full, n + 1)
                        dve.tensor_copy(dst_T[:, n % DC, (n // DC) * S:(n // DC + 1) * S], tp[:, n % 4, :]).then_inc(dve_evac, 1)

            @block.scalar
            def _(act):
                act.wait_ge(aggr_done, TILES)
                act.activation(std[:], mv[:, :, 1], ACT.Sqrt, bias=eps[:, 0:1]).then_inc(std_done, 1)
                act.wait_ge(scale_step, 2)
                for t in range(0, TILES, 1 if affine else 2):
                    act.activation(dst[:, t, :], src[:, t, :], ACT.Identity, bias=shift[:, t:t + 1],
                                   scale=rstd[:, t:t + 1]).then_inc(normed if affine else even_done, 1)
                if dst_T is not None:
                    for n in range(0, DC * B, 2):
                        act.wait_ge(tp_full, n + 1)
                        act.copy(dst_T[:, n % DC, (n // DC) * S:(n // DC + 1) * S], tp[:, n % 4, :]).then_inc(act_evac, 1)

            if dst_T is not None:
                @block.tensor
                def _(pe):
                    for n in range(DC * B):
                        b, c = n // DC, n % DC
                        pe.wait_ge(even_done, TPB // 2 * (b + 1))
                        pe.wait_ge(odd_done, TPB // 2 * (b + 1))
                        if n >= 4:
                            pe.wait_ge(act_evac if n % 2 == 0 else dve_evac, (n - 4) // 2 + 1)
                        for j in range(TPB):
                            mm = pe.transpose(tp[:, n % 4, j * P:(j + 1) * P],
                                              dst[:, TPB * b + j, c * P:(c + 1) * P], k.ident[:])
                        mm.then_inc(tp_full, 1)


def load_stack(sp, qs, ks, qk_dram, G, loaded):
    for which, part_of, dst in ((0, Q_PART, qs), (1, K_PART, ks)):
        for r in range(PAIRS):
            sp.dma_start(dst[r * HD:(r + 1) * HD, :, :],
                         qk_dram[which, part_of[r], at(G)].rearrange("g i d t -> d (g i) t")).then_inc(loaded, DMA)


def attention_project(nc, k, name, a, vp, qk_dram, w, qkb, bvb, ctxb, qs, ks, mask=None, mb=None):
    ONE = 1
    with Stage(nc, name) as st:
        parts = [st.sb(f"parts{u}", [P, 4, 3, S], BF16) for u in range(2)]
        rest = st.sb("rest", [P, 4, S])
        if mask:
            per_row = mask[2]
            raw = [st.sb(f"raw{n}", [P, TPB, S], mask[0].dtype) for n in range(2)]
            raw_loaded = [st.sem(f"raw_loaded{n}") for n in range(2)]
            mask_ready = st.sem("mask_ready")
        pj = st.ps("pj", [P, 4, S])
        pv = st.ps("pv", [P, 4, S])
        ctx_loaded, ctx_ready, v_full, v_evac = (st.sem(n) for n in ("ctx_loaded", "ctx_ready", "v_full", "v_evac"))
        proj_full, hi_done, rest_done, mid_done, lo_done, stored = (
            st.sem(n) for n in ("proj_full", "hi_done", "rest_done", "mid_done", "lo_done", "stored"))
        parts_free, stacks_loaded, ones_done = st.sem("parts_free"), st.sem("stacks_loaded"), st.sem("ones_done")
        ORDER = [(1, 0), (1, 1), (0, 0), (0, 1)]
        with nc.Block() as block:
            @block.sync
            def _(sp):
                def load_masks(b):
                    for n in range(2):
                        sp.dma_start(raw[n][:], mask[n][at(b * S, S)].rearrange("(t p) c -> p t c", p=P)).then_inc(raw_loaded[n], DMA)

                sp.sem_inc(ctx_ready, 1)
                if mask and per_row:
                    load_masks(0)
                with sp.Fori(1, B) as b:
                    sp.wait_ge(v_full, TPB * b + ONE)
                    sp.dma_start(ctxb[:], a["ctxT"].rearrange("(c p) n -> p c n", p=P)[:, :, bass.ds(b * S, S)]).then_inc(ctx_loaded, DMA)
                    sp.wait_ge(ctx_loaded, DMA * b)
                    sp.sem_inc(ctx_ready, 1)
                    if mask and per_row:
                        sp.wait_ge(mask_ready, 2 * b + ONE)
                        load_masks(b)
                if mask and not per_row:
                    for n in range(2):
                        sp.dma_start(raw[n][:], mask[n].rearrange("(t p) c -> p t c", p=P)).then_inc(raw_loaded[n], DMA)
                sp.wait_ge(parts_free, 2 + 1)
                for u in range(2):
                    load_stack(sp, qs[u], ks[u], qk_dram, u, stacks_loaded)
                sp.wait_ge(stacks_loaded, 2 * 2 * PAIRS * DMA)

            @block.tensor
            def _(pe):
                pe.sem_inc(v_full, ONE)
                with pe.Fori(0, B) as b:
                    def project(o):
                        which, m = ORDER[o]
                        pe.wait_ge(rest_done, 4 * b + o + 1)
                        for c in range(DC):
                            rhs = ctxb[:, c, :] if which else k.XNT[:, c, bass.ds(b * S, S)]
                            mm = pe.matmul(pj[:, o, :], w[:, which, c, m * P:(m + 1) * P], rhs,
                                           start=c == 0, stop=c == DC - 1)
                        mm.then_inc(proj_full, 1)
                    pe.wait_ge(ctx_ready, b + 1)
                    project(0)
                    project(1)
                    pe.wait_ge(v_evac, TPB * b + ONE)
                    for t in range(TPB):
                        for c in range(DC):
                            mm = pe.matmul(pv[:, t, 0:D], ctxb[:, c, t * P:(t + 1) * P], w[:, 2, c, :],
                                           start=c == 0, stop=c == DC - 1)
                        mm.then_inc(v_full, 1)
                    project(2)
                    project(3)

            @block.scalar
            def _(act):

                def high(b, u, o):
                    which, m = ORDER[o]
                    act.wait_ge(proj_full, 4 * b + o + 1)
                    act.wait_ge(parts_free, b + 1)
                    act.activation(parts[u][:, o, 0, :], pj[:, o, :], ACT.Identity,
                                   bias=qkb[:, which, m:m + 1]).then_inc(hi_done, 1)

                def middle(b, u, o):
                    act.wait_ge(rest_done, 4 * b + o + 1 + 4)
                    act.copy(parts[u][:, o, 1, :], rest[:, o, :]).then_inc(mid_done, 1)

                with act.Fori(0, B // 2) as b2:
                    for u in range(2):
                        for half in (0, 2):
                            for part in (high, middle):
                                for o in (half, half + 1):
                                    part(2 * b2 + u, u, o)

            @block.vector
            def _(dve):
                for credit in (v_evac, lo_done):
                    dve.sem_inc(credit, ONE)
                dve.sem_inc(rest_done, 4)
                if mask:
                    dve.sem_inc(mask_ready, ONE)

                def convert(b):
                    for n in range(2):
                        dve.wait_ge(raw_loaded[n], DMA * b + DMA)
                        dve.tensor_scalar(mb[n][:, at(TPB * b, TPB), :], raw[n][:], 0, MASKED, ALU.is_equal, ALU.mult).then_inc(mask_ready, 1)

                with dve.Fori(0, B // 2) as b2:
                    for u in range(2):
                        b = 2 * b2 + u

                        def first_rest(o):
                            which, m = ORDER[o]
                            dve.wait_ge(hi_done, 4 * b + o + 1)
                            dve.wait_ge(lo_done, 4 * b + ONE)
                            dve.scalar_tensor_tensor(out=rest[:, o, :], in0=pj[:, o, :], scalar=qkb[:, which, m:m + 1],
                                                     in1=parts[u][:, o, 0, :], op0=ALU.add, op1=ALU.subtract).then_inc(rest_done, 1)

                        def low(o):
                            dve.wait_ge(mid_done, 4 * b + o + 1)
                            dve.tensor_tensor(parts[u][:, o, 2, :], rest[:, o, :], parts[u][:, o, 1, :],
                                              ALU.subtract).then_inc(lo_done, 1)

                        first_rest(0)
                        first_rest(1)
                        for t in range(TPB):
                            dve.wait_ge(v_full, TPB * b + t + 1 + ONE)
                            dve.tensor_tensor(vp[:, bass.ds(GROUPS * b, GROUPS), t, :, 0:HD],
                                              pv[:, t, 0:D].rearrange("p (g i d) -> p g i d", g=GROUPS, i=GH),
                                              bvb[:].rearrange("p (g i d) -> p g i d", g=GROUPS, i=GH), ALU.add).then_inc(v_evac, 1)
                        low(0)
                        low(1)
                        first_rest(2)
                        first_rest(3)
                        low(2)
                        low(3)
                        if mask and per_row:
                            convert(b)
                if mask and not per_row:
                    convert(0)

            @block.gpsimd
            def _(pool):
                pool.sem_inc(parts_free, 2)
                for u in range(2):
                    pool.memset(ks[u][STACK:STACK + MROWS, :, :], 1.0).then_inc(ones_done, 1)
                with pool.Fori(0, B // 2) as b2:
                    for u in range(2):
                        b = 2 * b2 + u
                        for o, (which, m) in enumerate(ORDER):
                            pool.wait_ge(lo_done, 4 * b + o + 1 + ONE)
                            dst = qk_dram[which, :, bass.ds(GROUPS * b + 2 * m, 2)].rearrange("r g i d t -> (g i d) r t")
                            pool.dma_start(dst, parts[u][:, o, :, :]).then_inc(stored, DMA)
                        pool.wait_ge(stored, 4 * DMA * b + 4 * DMA)
                        pool.sem_inc(parts_free, 1)



def attention_core(nc, k, name, vp, atn, qk_dram, qs, ks, scale, selsum, bo, gate, mask=None, tril2=None, prefetch=()):
    AV0, EXP0, S0, M0, AVS0, ONE = 3, 2, 2, 1, 2, 1
    with Stage(nc, name) as st:
        rows = mask[0].shape[1] // TPB if mask else 1
        vg = [st.sb(f"vg{u}", [P, TPB, GH, STRIP]) for u in range(2)]
        vg2 = [st.sb(f"vgd{u}", [P, TPB, GH, STRIP]) for u in range(2)] if tril2 is not None else None
        prob_wide = [st.sb(f"prob{u}", [P, TPB * (S + P) if tril2 is not None else TPB * S]) for u in range(4)]
        prob = [w[:, 0:TPB * S].rearrange("p (k q) -> p k q", k=TPB) for w in prob_wide]
        avs = [st.sb(f"avs{u}", [P, S]) for u in range(2)]
        rsum = st.sb("rsum", [P, TPB, GH])
        rdup = st.sb("rdup", [P, TPB, GH, STRIP])
        sel = st.sb("sel", [P, GH])
        maxes = st.sb("maxes", [P, TPB])
        nmp = st.sb("nmp", [P, 4, TPB, MROWS], BF16)
        bob = st.sb("bob", [P, D])
        if mask:
            junk = st.sb("junk", [P, 2, S], BF16)
            mb, mbT = mask
            here = st.sb("here", [P, TPB, S], BF16) if rows > 1 else mb
        if tril2 is not None:
            tril = st.sb("tril", [P, P])
        ps_s = st.ps("s", [P, 2, S])
        ps_st = st.ps("st", [P, 4, S])
        ps_av = st.ps("av", [P, S])
        ps_m = st.ps("m", [P, S])
        (const_loaded, vg_ready, s_full, s_free, split_step, negmax_ready, mt_full, mrow_ready,
         st_full, exp_done, av_done, av_evac, sums_full, recip_done, dup_done, bc_full, atn_done,
         diag_done, bias_step, pool_tick) = (st.sem(n) for n in (
             "const_loaded", "vg_ready", "s_full", "s_free", "split_step", "negmax_ready", "mt_full",
             "mrow_ready", "st_full", "exp_done", "av_done", "av_evac", "sums_full", "recip_done", "dup_done", "bc_full",
             "atn_done", "diag_done", "bias_step", "pool_tick"))
        loaded = [st.sem(f"stack_loaded{u}") for u in range(2)]
        dve_tick, prefetched, fetched = st.sem("dve_tick"), st.sem("prefetched"), st.sem("fetched")
        NIT = B * GROUPS // 2
        PAIRS_IT = 4
        PER_LOAD = 2 * PAIRS * DMA
        NCONST = 2 + (tril2 is not None)
        VG_STEPS = 2 if vg2 is not None else 1

        def iterations(eng, body):
            body(0, True, False)
            with eng.Fori(1, NIT - 1) as it:
                body(it, False, False)
            body(NIT - 1, False, True)

        with nc.Block() as block:
            @block.sync
            def _(sp):
                sp.dma_start(sel[:], selsum).then_inc(const_loaded, DMA)
                sp.dma_start(bob[:], bo).then_inc(const_loaded, DMA)
                if tril2 is not None:
                    sp.dma_start(tril[:], tril2).then_inc(const_loaded, DMA)
                with sp.Fori(0, NIT - 1) as it:
                    for u in range(2):
                        sp.wait_ge(st_full, 16 * it + 8 * u + 8)
                        load_stack(sp, qs[u], ks[u], qk_dram, 2 * it + (2 + u), loaded[u])
                for to, what in prefetch:
                    sp.dma_start(to, what).then_inc(prefetched, DMA)
                if prefetch:
                    sp.wait_ge(prefetched, DMA * len(prefetch))

            @block.gpsimd
            def _(pool):
                if tril2 is not None:
                    pool.wait_ge(const_loaded, NCONST * DMA)
                with pool.Fori(0, NIT) as it:
                    def copy_values(u):
                        pool.wait_ge(av_done, PAIRS_IT * it + 2 * u - 2 + AV0)
                        pool.sem_inc(pool_tick, 1)
                        pool.tensor_copy(vg[u][:], vp[:, bass.ds(2 * it + u, 1)].rearrange("p g t i c -> p (g t) i c")).then_inc(vg_ready, 1)
                        if vg2 is not None:
                            pool.wait_ge(vg_ready, 4 * it + 2 * u + 1)
                            pool.tensor_tensor(vg2[u][:], vg[u][:], vg[u][:], ALU.add).then_inc(vg_ready, 1)

                    def weigh_diagonals(heads):
                        for j in heads:
                            pool.wait_ge(exp_done, 16 * it + 2 * j + 2 + EXP0)
                            diag = prob_wide[j % 4][:].rearrange("p (k q) -> p k q", k=TPB)[:, :, 0:P]
                            pool.tensor_tensor(diag, diag, tril[:].unsqueeze(1).broadcast_to([P, TPB, P]), ALU.mult).then_inc(diag_done, 1)

                    copy_values(0)
                    if tril2 is not None:
                        weigh_diagonals((0, 1))
                    copy_values(1)
                    if tril2 is not None:
                        weigh_diagonals(range(2, 2 * GH))

            @block.tensor
            def _(pe):
                pe.sem_inc(av_done, AV0)

                def scores(it, j, qt):
                    it, j = (it + 1, j - 2 * GH) if j >= 2 * GH else (it, j)
                    u, i = divmod(j, GH)
                    if qt == 0 and i == 0 and not (isinstance(it, int) and it == 0):
                        pe.wait_ge(loaded[u], PER_LOAD * it)
                    T = 4 * j + qt
                    pe.wait_ge(s_free, 32 * it + T - 1 + S0)
                    pe.matmul(ps_s[:, T % 2, :], qs[u][0:STACK, i, qt * P:(qt + 1) * P], ks[u][0:STACK, i, :],
                              start=True, stop=True).then_inc(s_full, 1)

                def max_rows(it, j, sums, bcs):
                    it, j = (it + 1, j - 2 * GH) if j >= 2 * GH else (it, j)
                    pe.wait_ge(negmax_ready, 8 * it + j + 1 + ONE)
                    pe.wait_ge(mrow_ready, 8 * it + j + M0)
                    pe.wait_ge(recip_done, sums + ONE)
                    pe.wait_ge(atn_done, bcs + AVS0)
                    for qt in range(TPB):
                        mm = pe.matmul(ps_m[STACK:STACK + MROWS, qt * P:(qt + 1) * P], nmp[:, j % 4, qt, :], k.ident_bf[:],
                                       start=True, stop=True)
                    mm.then_inc(mt_full, 1)

                def scores_T(it, j, hb):
                    u, i = divmod(j, GH)
                    if hb == 0:
                        pe.wait_ge(mrow_ready, 8 * it + j + 1 + M0)
                    pe.wait_ge(exp_done, 16 * it + 2 * j + hb - 1 + EXP0)
                    for kt in (2 * hb, 2 * hb + 1):
                        mm = pe.matmul(ps_st[:, kt, :], ks[u][0:STACK + MROWS, i, kt * P:(kt + 1) * P],
                                       qs[u][0:STACK + MROWS, i, :], start=True, stop=not mask)
                        if mask:
                            mm = pe.matmul(ps_st[:, kt, :], k.ident_bf[:],
                                           mbT[:, at(TPB * (it // 2) + kt), :] if rows > 1 else mbT[:, kt, :],
                                           start=False, stop=True)
                    mm.then_inc(st_full, 1)

                def values(it, m, kt):
                    it, m = (it - 1, m + PAIRS_IT) if m < 0 else (it, m)
                    u = m // 2
                    if kt == 0:
                        if m % 2 == 0:
                            pe.wait_ge(vg_ready, (2 * it + u + 1) * VG_STEPS)
                            pe.wait_ge(av_evac, 2 * it + u + ONE)
                        pe.wait_ge(exp_done, 16 * it + 4 * m + 4 + EXP0)
                        if tril2 is not None:
                            pe.wait_ge(diag_done, 8 * it + 2 * m + 2)
                    cut = (kt + 1) * P if tril2 is not None else S
                    for j in (2 * m, 2 * m + 1):
                        i = j % GH
                        mm = pe.matmul(ps_av[STRIP * i:STRIP * (i + 1), 0:cut], vg[u][:, kt, i, :], prob[j % 4][:, kt, 0:cut],
                                       start=kt == 0, stop=kt == TPB - 1, skip_group_check=True)
                    if cut < S:
                        for j in (2 * m, 2 * m + 1):
                            i = j % GH
                            mm = pe.matmul(ps_av[STRIP * i:STRIP * (i + 1), cut:S], vg2[u][:, kt, i, :], prob[j % 4][:, kt, cut:S],
                                           start=False, stop=False, skip_group_check=True)
                    if kt == TPB - 1:
                        mm.then_inc(av_done, 1)

                def sums(G, mrows):
                    pe.wait_ge(av_evac, G + 1 + ONE)
                    pe.wait_ge(mrow_ready, mrows + M0)
                    pe.wait_ge(atn_done, G + AVS0)
                    for qt in range(TPB):
                        mm = pe.matmul(ps_m[:, qt * GH:(qt + 1) * GH], avs[sums_u[0]][:, qt * P:(qt + 1) * P], sel[:], start=True, stop=True)
                    mm.then_inc(sums_full, 1)

                def broadcast(G, mrows):
                    pe.wait_ge(dup_done, G + 1)
                    pe.wait_ge(mrow_ready, mrows + M0)
                    for qt in range(TPB):
                        mm = pe.matmul(ps_m[:, qt * P:(qt + 1) * P], rdup[:, qt].rearrange("p i c -> p (i c)"), k.ident[:], start=True, stop=True)
                    mm.then_inc(bc_full, 1)

                sums_u = [0]

                def body(it, first, last):
                    G = 2 * it
                    nsum = nbc = 0 if first else G - 1
                    for m in range(PAIRS_IT):
                        a, b = 2 * m, 2 * m + 1
                        ahead = not (last and m == PAIRS_IT - 1)
                        behind = not (first and m == 0)
                        div = {1: None if first else G - 1, 3: G}.get(m)
                        has_div = m in (1, 3) and not (m == 1 and first)
                        scores_T(it, a, 0)
                        if ahead:
                            scores(it, a + 2, 0)
                        scores_T(it, a, 1)
                        max_rows(it, b, nsum, nbc)
                        if ahead:
                            scores(it, a + 2, 1)
                        if behind:
                            values(it, m - 1, 0)
                        if has_div:
                            sums_u[0] = 1 if m == 1 else 0
                            sums(div, 8 * it + b + 1)
                            nsum = div + 1
                        if ahead:
                            scores(it, a + 2, 2)
                            scores(it, a + 2, 3)
                        if behind:
                            values(it, m - 1, 1)
                        scores_T(it, b, 0)
                        if has_div:
                            broadcast(div, 8 * it + b + 1)
                            nbc = div + 1
                        if ahead:
                            scores(it, b + 2, 0)
                        scores_T(it, b, 1)
                        if ahead:
                            max_rows(it, a + 2, nsum, nbc)
                            scores(it, b + 2, 1)
                        if behind:
                            values(it, m - 1, 2)
                        if ahead:
                            scores(it, b + 2, 2)
                            scores(it, b + 2, 3)
                        if behind:
                            values(it, m - 1, 3)

                for j in range(2):
                    for qt in range(TPB):
                        scores(0, j, qt)
                pe.wait_ge(const_loaded, NCONST * DMA)
                max_rows(0, 0, 0, 0)
                iterations(pe, body)
                for kt in range(TPB):
                    values(NIT - 1, PAIRS_IT - 1, kt)
                sums_u[0] = 1
                sums(2 * NIT - 1, 8 * NIT)
                broadcast(2 * NIT - 1, 8 * NIT)

            @block.scalar
            def _(act):
                act.sem_inc(exp_done, EXP0)
                act.sem_inc(mrow_ready, M0)
                act.sem_inc(av_evac, ONE)

                def max_row(it, j):
                    it, j = (it + 1, j - 2 * GH) if j >= 2 * GH else (it, j)
                    u, i = divmod(j, GH)
                    act.wait_ge(mt_full, 8 * it + j + 1)
                    act.copy(qs[u][STACK:STACK + MROWS, i, :], ps_m[STACK:STACK + MROWS, :]).then_inc(mrow_ready, 1)

                def exps(it, j, next_row):
                    for hb in range(2):
                        act.wait_ge(st_full, 16 * it + 2 * j + hb + 1)
                        act.wait_ge(av_done, PAIRS_IT * it + j // 2 - 1 + AV0)
                        act.activation(prob[j % 4][:, 2 * hb:2 * hb + 2, :], ps_st[:, 2 * hb:2 * hb + 2, :], ACT.Exp,
                                       scale=scale).then_inc(exp_done, 1)
                        if hb == 0 and next_row:
                            max_row(it, j + 1)

                def evacuate(G, u):
                    act.wait_ge(av_done, 2 * G + 2 + AV0)
                    act.wait_ge(atn_done, G - 1 + AVS0)
                    act.copy(avs[u][:], ps_av[:]).then_inc(av_evac, 1)

                def body(it, first, last):
                    for m in range(PAIRS_IT):
                        if m == 1 and not first:
                            evacuate(2 * it - 1, 1)
                        if m == 3:
                            evacuate(2 * it, 0)
                        exps(it, 2 * m, True)
                        exps(it, 2 * m + 1, not (last and m == PAIRS_IT - 1))

                max_row(0, 0)
                iterations(act, body)
                evacuate(2 * NIT - 1, 1)

            @block.vector
            def _(dve):
                dve.sem_inc(s_free, S0)
                dve.sem_inc(atn_done, AVS0)
                dve.sem_inc(negmax_ready, ONE)
                dve.sem_inc(recip_done, ONE)
                def fetch_mask(it):
                    if not (isinstance(it, int) and it == 0):
                        dve.wait_ge(s_free, 32 * it + S0)
                    dve.tensor_copy(here[:], mb[:, at(TPB * (it // 2), TPB), :]).then_inc(fetched, 1)
                    dve.wait_ge(fetched, it + 1)

                def row_max(it, j, qt):
                    it, j = (it + 1, j - 2 * GH) if j >= 2 * GH else (it, j)
                    if qt == 0:
                        dve.wait_ge(negmax_ready, 8 * it + j + ONE)
                    T = 4 * j + qt
                    dve.wait_ge(s_full, 32 * it + T + 1)
                    if mask:
                        dve.wait_ge(s_free, 32 * it + T - 1 + S0)
                        dve.sem_inc(dve_tick, 1)
                        dve.tensor_tensor_reduce(out=junk[:, T % 2, :], in0=ps_s[:, T % 2, :], in1=here[:, qt, :],
                                                 scale=1.0, scalar=-3.0e38, op0=ALU.add, op1=ALU.max,
                                                 accum_out=maxes[:, qt:qt + 1]).then_inc(s_free, 1)
                    else:
                        dve.tensor_reduce(maxes[:, qt:qt + 1], ps_s[:, T % 2, :], AX.X, ALU.max).then_inc(s_free, 1)

                def split(it, j):
                    it, j = (it + 1, j - 2 * GH) if j >= 2 * GH else (it, j)
                    dve.wait_ge(s_free, 32 * it + 4 * j + 4 + S0)
                    dve.tensor_scalar(nmp[:, j % 4, :, 0], maxes[:], -1.0, None, ALU.mult).then_inc(split_step, 1)
                    dve.wait_ge(split_step, 8 * it + j + 1)
                    dve.scalar_tensor_tensor(out=nmp[:, j % 4, :, 1], in0=maxes[:], scalar=-1.0, in1=nmp[:, j % 4, :, 0],
                                             op0=ALU.mult, op1=ALU.subtract).then_inc(negmax_ready, 1)

                def reciprocals(G):
                    dve.wait_ge(sums_full, G + 1)
                    dve.reciprocal(rsum[:], ps_m[:, 0:TPB * GH].rearrange("p (t i) -> p t i", t=TPB)).then_inc(recip_done, 1)
                    dve.wait_ge(recip_done, G + 1 + ONE)
                    dve.tensor_copy(rdup[:], rsum[:].unsqueeze(3).broadcast_to([P, TPB, GH, STRIP])).then_inc(dup_done, 1)

                def divide(G, u):
                    dve.wait_ge(bc_full, G + 1)
                    dve.tensor_tensor(atn[:, at(G), :].rearrange("p g q -> p (g q)"), avs[u][:], ps_m[:], ALU.mult).then_inc(atn_done, 1)

                def body(it, first, last):
                    for m in range(PAIRS_IT):
                        a, b = 2 * m, 2 * m + 1
                        ahead = not (last and m == PAIRS_IT - 1)
                        has_div = m == 3 or (m == 1 and not first)
                        G, u = (2 * it - 1, 1) if m == 1 else (2 * it, 0)
                        if ahead:
                            if m == PAIRS_IT - 1 and rows > 1:
                                fetch_mask(it + 1)
                            row_max(it, a + 2, 0)
                            row_max(it, a + 2, 1)
                        if has_div:
                            reciprocals(G)
                        if ahead:
                            row_max(it, a + 2, 2)
                            row_max(it, a + 2, 3)
                            split(it, a + 2)
                        if has_div:
                            divide(G, u)
                        if ahead:
                            for qt in range(TPB):
                                row_max(it, b + 2, qt)
                            split(it, b + 2)

                if rows > 1:
                    fetch_mask(0)
                for j in range(2):
                    for qt in range(TPB):
                        row_max(0, j, qt)
                    split(0, j)
                dve.wait_ge(const_loaded, NCONST * DMA)
                dve.tensor_scalar(bob[:], bob[:], k.tg[:, gate:gate + 1], None, ALU.mult).then_inc(bias_step, 1)
                dve.wait_ge(bias_step, 1)
                dve.tensor_tensor(k.X[:], k.X[:], bob[:].unsqueeze(1).broadcast_to([P, TILES, D]), ALU.add).then_inc(bias_step, 1)
                dve.wait_ge(bias_step, 2)
                iterations(dve, body)
                reciprocals(2 * NIT - 1)
                divide(2 * NIT - 1, 1)


def attention_out(nc, k, name, atn, w, gate):
    with Stage(nc, name) as st:
        po = st.ps("po", [P, 8, 512])
        out_full, out_evac, stats_done = st.sem("out_full"), st.sem("out_evac"), st.sem("stats_done")
        with nc.Block() as block:
            @block.tensor
            def _(pe):
                for t in range(TILES):
                    if t >= 8:
                        pe.wait_ge(out_evac, t - 7)
                    for g in range(GROUPS):
                        mm = pe.matmul(po[:, t % 8, 0:D], atn[:, GROUPS * (t // TPB) + g, (t % TPB) * P:(t % TPB + 1) * P],
                                       w[:, g, :], start=g == 0, stop=g == GROUPS - 1)
                    mm.then_inc(out_full, 1)

            @block.vector
            def _(dve):
                for t in range(TILES):
                    dve.wait_ge(out_full, t + 1)
                    dve.scalar_tensor_tensor(out=k.X[:, t, :], in0=po[:, t % 8, 0:D], scalar=k.tg[:, gate:gate + 1],
                                             in1=k.X[:, t, :], op0=ALU.mult, op1=ALU.add).then_inc(out_evac, 1)
                    if t:
                        row_stats(dve, k, k.X, t - 1, out_evac, t, stats_done)
                row_stats(dve, k, k.X, TILES - 1, out_evac, TILES, stats_done)


def attention_layer(nc, k, name, a, wq, wk, wv, bq, bk, bv, wo, bo, scale, gate, mask=None, tril2=None):
    with ExitStack() as ctx:
        def sb(within, what, shape, dt=F32):
            return within.enter_context(nc.sbuf_tensor(f"{name}_{what}", shape, dt))

        vp = sb(ctx, "vp", [P, B * GROUPS, TPB, GH, STRIP])
        w_out = sb(ctx, "w_out", [P, GROUPS, D])
        qs = [sb(ctx, f"qs{u}", [P, GH, S], BF16) for u in range(2)]
        ks = [sb(ctx, f"ks{u}", [P, GH, S], BF16) for u in range(2)]
        mb = None
        if mask:
            n = (B if mask[2] else 1) * TPB
            mb = [sb(ctx, f"mb{u}", [P, n, S], BF16) for u in range(2)]
        with ExitStack() as inner:
            w, qkb, bvb = sb(inner, "w", [P, 3, DC, D]), sb(inner, "qkb", [P, 2, DC]), sb(inner, "bvb", [P, D])

            ctxb = sb(inner, "ctxb", [P, DC, S])

            def ones_and_zeros(pool, done):
                pool.memset(vp[:, :, :, :, HD:STRIP], 0.0).then_inc(done, 1)
                pool.wait_ge(done, 1)
                pool.memset(vp[:, :, :, :, HD:HD + 1], 1.0).then_inc(done, 1)

            prefetch = [(w[:, j], x.rearrange("(c p) n -> p c n", p=P)) for j, x in enumerate((wq, wk, wv))]
            prefetch += [(qkb[:, 0, :], bq), (qkb[:, 1, :], bk), (bvb[:], bv),
                         (ctxb[:], a["ctxT"].rearrange("(c p) n -> p c n", p=P)[:, :, 0:S])]
            layernorm_stage(nc, k, name + "_ln", k.X, k.XN, k.XNT, prefetch=prefetch, fill=ones_and_zeros,
                            have_stats=gate > 0)
            attention_project(nc, k, name + "_p", a, vp, k.qk_dram, w, qkb, bvb, ctxb, qs, ks, mask, mb)
        attention_core(nc, k, name + "_a", vp, k.ATN, k.qk_dram, qs, ks, scale, a["selsum"], bo, gate, mb, tril2, [(w_out[:], wo)])
        attention_out(nc, k, name + "_o", k.ATN, w_out, gate)


class Chain:

    def __init__(self, eng, sem, base=0):
        self.eng, self.sem, self.base, self.n = eng, sem, base, 0

    def __call__(self, ins):
        self.n += 1
        ins.then_inc(self.sem, 1)
        self.eng.wait_ge(self.sem, self.base + self.n)


def over(x, n):
    return x.unsqueeze(2).broadcast_to([x.shape[0], x.shape[1], n])


def transpose_stage(nc, k, name, src, dst_T):
    with Stage(nc, name) as st:
        tp = st.ps("tp", [P, 4, 512])
        tp_full, act_evac, dve_evac = st.sem("tp_full"), st.sem("act_evac"), st.sem("dve_evac")

        def bank(n):
            return dst_T[:, n % DC, (n // DC) * S:(n // DC + 1) * S], tp[:, n % 4, :]

        with nc.Block() as block:
            @block.tensor
            def _(pe):
                for n in range(DC * B):
                    if n >= 4:
                        pe.wait_ge(act_evac if n % 2 == 0 else dve_evac, (n - 4) // 2 + 1)
                    for j in range(TPB):
                        mm = pe.transpose(tp[:, n % 4, j * P:(j + 1) * P],
                                          src[:, TPB * (n // DC) + j, (n % DC) * P:(n % DC + 1) * P], k.ident[:])
                    mm.then_inc(tp_full, 1)

            @block.scalar
            def _(act):
                for n in range(0, DC * B, 2):
                    act.wait_ge(tp_full, n + 1)
                    act.copy(*bank(n)).then_inc(act_evac, 1)

            @block.vector
            def _(dve):
                for n in range(1, DC * B, 2):
                    dve.wait_ge(tp_full, n + 1)
                    dve.tensor_copy(*bank(n)).then_inc(dve_evac, 1)


def router_stage(nc, k, name, a, src_T, rw, rb, E, K, kind, gate_col, gates, floor=None, pick=None):
    EPS = 1e-10
    with Stage(nc, name) as st:
        w = st.sb("w", [P, DC, E])
        rbb = st.sb("rbb", [P, E])
        ranks = st.sb("ranks", [P, E])
        lg, pr, work, sel, one, tmp = (st.sb(n, [P, TILES, E]) for n in ("lg", "pr", "work", "sel", "one", "tmp"))
        m, s, r = (st.sb(n, [P, TILES]) for n in ("m", "s", "r"))
        ps = st.ps("ps_lg", [P, TILES, E])
        loaded, lg_full, step, shifted, exp_done = (st.sem(n) for n in ("loaded", "lg_full", "step", "shifted", "exp_done"))
        n_loads = 3
        with nc.Block() as block:
            @block.sync
            def _(sp):
                sp.dma_start(w[:], rw.rearrange("(c p) e -> p c e", p=P)).then_inc(loaded, DMA)
                sp.dma_start(rbb[:], rb).then_inc(loaded, DMA)
                sp.dma_start(ranks[:], a[f"ranks{E}"]).then_inc(loaded, DMA)

            @block.tensor
            def _(pe):
                pe.wait_ge(loaded, n_loads * DMA)
                for t in range(TILES):
                    for c in range(DC):
                        mm = pe.matmul(ps[:, t, :], src_T[:, c, t * P:(t + 1) * P], w[:, c, :], start=c == 0, stop=c == DC - 1)
                mm.then_inc(lg_full, 1)

            @block.scalar
            def _(act):
                act.wait_ge(shifted, 1)
                act.activation(pr[:], lg[:], ACT.Exp).then_inc(exp_done, 1)

            @block.vector
            def _(dve):
                do = Chain(dve, step)

                def row_sum(out, x):
                    do(dve.tensor_reduce(out, x, AX.X, ALU.add))

                dve.wait_ge(loaded, n_loads * DMA)
                dve.wait_ge(lg_full, 1)
                do(dve.tensor_tensor(lg[:], ps[:], rbb[:].unsqueeze(1).broadcast_to([P, TILES, E]), ALU.add))
                do(dve.tensor_reduce(m[:], lg[:], AX.X, ALU.max))
                dve.tensor_tensor(lg[:], lg[:], over(m[:], E), ALU.subtract).then_inc(shifted, 1)
                dve.wait_ge(exp_done, 1)
                if kind == "probs":
                    row_sum(s[:], pr[:])
                    do(dve.reciprocal(r[:], s[:]))
                    do(dve.tensor_tensor(pr[:], pr[:], over(r[:], E), ALU.mult))
                do(dve.tensor_copy(work[:], pr[:] if kind == "probs" else lg[:]))
                do(dve.memset(sel[:], 0.0))
                for i in range(K):
                    do(dve.tensor_reduce(m[:], work[:], AX.X, ALU.max))
                    do(dve.tensor_tensor(one[:], work[:], over(m[:], E), ALU.is_equal))
                    do(dve.tensor_tensor(one[:], one[:], ranks[:].unsqueeze(1).broadcast_to([P, TILES, E]), ALU.mult))
                    do(dve.tensor_reduce(m[:], one[:], AX.X, ALU.max))
                    do(dve.tensor_tensor(one[:], one[:], over(m[:], E), ALU.is_equal))
                    do(dve.tensor_tensor(sel[:], sel[:], one[:], ALU.add))
                    if pick is not None:
                        do(dve.tensor_copy(pick[:, i], one[:]))
                    do(dve.scalar_tensor_tensor(out=work[:], in0=one[:], scalar=MASKED, in1=work[:], op0=ALU.mult, op1=ALU.add))
                do(dve.tensor_tensor(tmp[:], pr[:], sel[:], ALU.mult))
                row_sum(s[:], tmp[:])
                if kind == "probs" and floor is not None:
                    do(dve.tensor_scalar(s[:], s[:], EPS, None, ALU.add))
                do(dve.reciprocal(r[:], s[:]))
                do(dve.tensor_tensor(tmp[:], tmp[:], over(r[:], E), ALU.mult))
                if kind == "probs" and floor is not None:
                    row_sum(s[:], tmp[:])
                    do(dve.tensor_scalar(r[:], s[:], EPS, None, ALU.max))
                    do(dve.reciprocal(m[:], r[:]))
                    do(dve.tensor_tensor(tmp[:], tmp[:], over(m[:], E), ALU.mult))
                    do(dve.tensor_scalar(floor[:], s[:], EPS, k.tg[:, gate_col:gate_col + 1], ALU.mult, ALU.mult))
                do(dve.tensor_scalar(gates[:], tmp[:], k.tg[:, gate_col:gate_col + 1], None, ALU.mult))


PARTS = ((0, 0), (0, 1), (1, 0))


def linear_experts_stage(nc, k, name, expert_w, gates, floor, E):
    BANKS, FILLS = 8, 4
    with Stage(nc, name) as st:
        w = st.sb("w", [P, DC, E, D])
        x_parts = st.sb("x_parts", [P, 2, DC, B * S], F32R)
        w_parts = [st.sb(f"w_parts{u}", [P, 2, DC, 2 * D], F32R) for u in range(2)]
        zero = st.sb("zero", [P, FILL_ROWS * D // (P * FILLS)])
        po = st.ps("po", [P, BANKS, 512])
        stats_done, floor_added = st.sem("stats_done"), st.sem("floor_added")
        w_loaded, full, evac, x_step, x_high, x_low, w_high, w_low, zero_ready, filled = (st.sem(n) for n in (
            "w_loaded", "full", "evac", "x_step", "x_high", "x_low", "w_high", "w_low", "zero_ready", "filled"))

        def raw(pair):
            return w[:, :, at(2 * pair, 2), :].rearrange("p c e n -> p c (e n)")

        with nc.Block() as block:
            @block.gpsimd
            def _(pool):
                pool.memset(zero[:], 0.0).then_inc(zero_ready, 1)

            @block.sync
            def _(sp):
                for c in range(DC):
                    sp.dma_start(w[:, c], expert_w[:, c * P:(c + 1) * P, :].rearrange("e p n -> p e n")).then_inc(w_loaded, DMA)
                sp.wait_ge(zero_ready, 1)
                for n in range(FILLS):
                    rows = FILL_ROWS // FILLS
                    sp.dma_start(k.slot_x[n * rows:(n + 1) * rows, :].rearrange("(p r) d -> p (r d)", p=P), zero[:]).then_inc(filled, DMA)
                sp.wait_ge(filled, FILLS * DMA)

            @block.tensor
            def _(pe):
                with pe.Fori(0, E // 4) as quad:
                    for u in range(2):
                        pair = 2 * quad + u
                        pe.wait_ge(w_low, pair + 1 + 1)
                        for t in range(TILES):
                            if u == 0:
                                pe.wait_ge(x_low, t // TPB + 1)
                            pe.wait_ge(evac, TILES * pair + t + 1)
                            for n, (xp, wp) in enumerate(PARTS):
                                for c in range(DC):
                                    mm = pe.matmul(po[:, t % BANKS, :], x_parts[:, xp, c, t * P:(t + 1) * P], w_parts[u][:, wp, c, :],
                                                   start=n == 0 and c == 0, stop=n == len(PARTS) - 1 and c == DC - 1)
                            mm.then_inc(full, 1)

            @block.scalar
            def _(act):
                def high(pair, u):
                    act.wait_ge(evac, TILES * pair - BANKS)
                    act.copy(w_parts[u][:, 0], raw(pair)).then_inc(w_high, 1)

                for b in range(B):
                    act.copy(x_parts[:, 0, :, b * S:(b + 1) * S], k.XNT[:, :, b * S:(b + 1) * S]).then_inc(x_high, 1)
                    if b == 0:
                        act.wait_ge(w_loaded, DC * DMA)
                        for u in range(2):
                            act.copy(w_parts[u][:, 0], raw(u)).then_inc(w_high, 1)
                with act.Fori(1, E // 4) as quad:
                    for u in range(2):
                        high(2 * quad + u, u)

            @block.vector
            def _(dve):
                dve.sem_inc(evac, BANKS)
                dve.sem_inc(w_low, 1)

                def low(pair, u):
                    dve.wait_ge(w_high, pair + 1)
                    dve.tensor_tensor(w_parts[u][:, 1], raw(pair), w_parts[u][:, 0].bitcast(F32), ALU.subtract).then_inc(w_low, 1)

                def add(pair, u):
                    for t in range(TILES):
                        dve.wait_ge(full, TILES * pair + t + 1)
                        dve.scalar_tensor_tensor(out=k.X[:, t, :], in0=po[:, t % BANKS, 0:D], scalar=gates[:, t, at(2 * pair)],
                                                 in1=k.X[:, t, :], op0=ALU.mult, op1=ALU.add).then_inc(x_step, 1)
                        dve.wait_ge(x_step, TILES * pair + t + 1)
                        dve.scalar_tensor_tensor(out=k.X[:, t, :], in0=po[:, t % BANKS, D:2 * D], scalar=gates[:, t, at(2 * pair + 1)],
                                                 in1=k.X[:, t, :], op0=ALU.mult, op1=ALU.add).then_inc(evac, 1)
                        if isinstance(pair, int) and pair == E // 2 - 1 and t:
                            row_stats(dve, k, k.X, t - 1, evac, BANKS + TILES * pair + t, stats_done)

                for b in range(B):
                    dve.wait_ge(x_high, b + 1)
                    row = slice(b * S, (b + 1) * S)
                    dve.tensor_tensor(x_parts[:, 1, :, row], k.XNT[:, :, row], x_parts[:, 0, :, row].bitcast(F32),
                                      ALU.subtract).then_inc(x_low, 1)
                    if b == 0:
                        low(0, 0)
                        low(1, 1)
                dve.tensor_tensor(k.X[:], k.X[:], over(floor[:], D), ALU.add).then_inc(floor_added, 1)
                dve.wait_ge(floor_added, 1)
                add(0, 0)
                with dve.Fori(0, E // 4 - 1) as quad:
                    low(2 * quad + 2, 0)
                    add(2 * quad + 1, 1)
                    low(2 * quad + 3, 1)
                    add(2 * quad + 2, 0)
                add(E // 2 - 1, 1)
                row_stats(dve, k, k.X, TILES - 1, evac, BANKS + TILES * (E // 2), stats_done)


class Plan:

    def __init__(self, nc, ctx, name, E, GS, capacity):
        def sb(n, shape, dt=F32):
            return ctx.enter_context(nc.sbuf_tensor(f"{name}_{n}", shape, dt))
        self.E, self.GS, self.capacity = E, GS, capacity
        self.NG = E if capacity else (2 * B * S + E * (GS - 1)) // GS
        self.pick = sb("pick", [P, 2, TILES, E])
        self.weight = sb("weight", [P, 2, TILES])
        self.to = sb("to", [P, 2 * TILES], U32)
        self.back = self.to
        if capacity:
            self.back = sb("back", [P, 2 * TILES], U32)
        else:
            self.w_row = sb("w_row", [P, self.NG], U32)


def slots_stage(nc, k, name, a, plan, gates):
    E, GS, NG = plan.E, plan.GS, plan.NG
    with Stage(nc, name) as st:
        before = st.sb("before", [P, P])
        ones = st.sb("ones", [P, P])
        sel, slot, fits, prod = (st.sb(n, [P, TILES, E]) for n in ("sel", "slot", "fits", "prod"))
        cum = st.sb("cum", [P, TILES + 1, E])
        to, ok = st.sb("to", [P, 2, TILES]), st.sb("ok", [P, 2, TILES])
        base = st.sb("base", [P, E])
        ps_rank = st.ps("ps_rank", [P, TILES, E])
        ps_count = st.ps("ps_count", [P, E])
        loaded, step, sel_done, rank_full = (st.sem(n) for n in ("loaded", "step", "sel_done", "rank_full"))
        if plan.capacity:
            spare = st.sb("spare", [P, 2, TILES])
        else:
            count, need, more = st.sb("count", [P, E]), st.sb("need", [P, E]), st.sb("more", [P, E])
            end = st.sb("end", [P, E])
            index = st.sb("index", [P, NG])
            lane = st.sb("lane", [P, 1])
            past = st.sb("past", [P, NG, E])
            row = st.sb("row", [P, NG])
        with nc.Block() as block:
            @block.sync
            def _(sp):
                sp.dma_start(before[:], a["before"]).then_inc(loaded, DMA)
                if plan.capacity:
                    sp.dma_start(base[:], a["first_slots"]).then_inc(loaded, DMA)
                    sp.dma_start(spare[:], a["spare_slots"]).then_inc(loaded, DMA)
                else:
                    sp.dma_start(index[:], a["index"][:, 0:NG]).then_inc(loaded, DMA)
                    sp.dma_start(lane[:], a["lane"]).then_inc(loaded, DMA)

            @block.tensor
            def _(pe):
                pe.wait_ge(loaded, 3 * DMA)
                pe.wait_ge(sel_done, 1)
                pe.matmul(ps_rank[:], before[:], sel[:], start=True, stop=False)
                mm = pe.matmul(ps_rank[:], ones[:], cum[:, 0:TILES, :], start=False, stop=True)
                if not plan.capacity:
                    mm = pe.matmul(ps_count[:], ones[:], cum[:, TILES, :], start=True, stop=True)
                mm.then_inc(rank_full, 1)

            @block.vector
            def _(dve):
                do = Chain(dve, step)
                do(dve.memset(ones[:], 1.0))
                do(dve.memset(cum[:, 0, :], 0.0))
                do(dve.tensor_tensor(sel[:], plan.pick[:, 0], plan.pick[:, 1], ALU.add))
                for t in range(TILES):
                    do(dve.tensor_tensor(cum[:, t + 1, :], cum[:, t, :], sel[:, t, :], ALU.add))
                dve.sem_inc(sel_done, 1)
                dve.wait_ge(loaded, 3 * DMA)
                dve.wait_ge(rank_full, 1)
                if plan.capacity:
                    do(dve.tensor_scalar(fits[:], ps_rank[:], float(GS), None, ALU.is_lt))
                    do(dve.tensor_tensor(gates[:], gates[:], fits[:], ALU.mult))
                else:
                    do(dve.tensor_copy(count[:], ps_count[:]))
                    do(dve.tensor_scalar(need[:], count[:], 0.0, None, ALU.is_gt))
                    for n in range(1, B * S // GS):
                        do(dve.tensor_scalar(more[:], count[:], float(n * GS), None, ALU.is_gt))
                        do(dve.tensor_tensor(need[:], need[:], more[:], ALU.add))
                    do(dve.tensor_copy(end[:, 0:1], need[:, 0:1]))
                    for e in range(1, E):
                        do(dve.tensor_tensor(end[:, e:e + 1], end[:, e - 1:e], need[:, e:e + 1], ALU.add))
                    do(dve.tensor_tensor(base[:], end[:], need[:], ALU.subtract))
                    do(dve.tensor_scalar(base[:], base[:], float(GS), None, ALU.mult))
                    do(dve.tensor_tensor(past[:], end[:].unsqueeze(1).broadcast_to([P, NG, E]), over(index[:], E), ALU.is_le))
                    do(dve.tensor_reduce(row[:], past[:], AX.X, ALU.add))
                    do(dve.tensor_scalar(row[:], row[:], float(E - 1), float(P), ALU.min, ALU.mult))
                    do(dve.tensor_scalar(row[:], row[:], lane[:, 0:1], None, ALU.add))
                    do(dve.tensor_copy(plan.w_row[:], row[:]))
                do(dve.tensor_tensor(slot[:], ps_rank[:], base[:].unsqueeze(1).broadcast_to([P, TILES, E]), ALU.add))
                for i in range(2):
                    for what, out in [(gates, plan.weight), (slot, to)] + ([(fits, ok)] if plan.capacity else []):
                        do(dve.tensor_tensor(prod[:], plan.pick[:, i], what[:], ALU.mult))
                        do(dve.tensor_reduce(out[:, i, :], prod[:], AX.X, ALU.add))
                flat = to[:].rearrange("p i t -> p (i t)")
                if plan.capacity:
                    do(dve.tensor_tensor(to[:], to[:], ok[:], ALU.mult))
                    do(dve.tensor_copy(plan.back[:], flat))
                    do(dve.tensor_scalar(ok[:], ok[:], -1.0, 1.0, ALU.mult, ALU.add))
                    do(dve.tensor_tensor(ok[:], ok[:], spare[:], ALU.mult))
                    do(dve.tensor_tensor(to[:], to[:], ok[:], ALU.add))
                do(dve.tensor_copy(plan.to[:], flat))


def grouped_experts_stage(nc, k, name, src, plan, w_rows, FC, gated, out_bias=None, add=None):
    GS, NG = plan.GS, plan.NG
    GT = GS // P
    NW = 2 if gated else 1
    NB = -(-GS // 512)
    BW = GS // NB
    HB = 4
    F = NW * FC * P
    TP = [(c, t, min(t + 4, GT)) for c in range(DC) for t in range(0, GT, 4)]
    NTP = len(TP)
    STEPS = FC * NB
    LOOPS = (NG - 2) // 2
    with Stage(nc, name) as st:
        w = [st.sb(f"w{u}", [P, w_rows.shape[1]]) for u in range(2)]
        w1 = [x[:, 0:DC * F].rearrange("p (c n j f) -> p c n j f", c=DC, n=NW, j=FC) for x in w]
        w2 = [x[:, DC * F:DC * F + FC * D].rearrange("p (j n) -> p j n", j=FC) for x in w]
        b1 = [x[:, DC * F + FC * D:] for x in w]
        xg = [st.sb(f"xg{u}", [P, GT, D]) for u in range(2)]
        xT = [st.sb(f"xT{u}", [P, 2, DC, GS], F32R) for u in range(2)]
        w1p = st.sb("w1p", [P, 2, DC, NW, FC, P], F32R)
        y = [st.sb(f"y{u}", [P, GT, D]) for u in range(2)]
        if gated:
            w2p = st.sb("w2p", [P, 2, FC, D], F32R)
            sg = st.sb("sg", [P, 2, GS])
            hidden = st.sb("hidden", [P, 2, GS])
            ht = st.sb("ht", [P, 2, FC, GS], F32R)
        else:
            ht = st.sb("ht", [P, FC, GS])
        banks = st.ps("banks", [P, HB, NW, 512 // NW])
        ph = [banks[:, :, n, :] for n in range(NW)]
        po = st.ps("po", [P, 2, 512])
        tp = st.ps("tp", [P, 2, 512])
        w_loaded = [st.sem(f"w_loaded{u}") for u in range(2)]
        x_loaded = [st.sem(f"x_loaded{u}") for u in range(2)]
        w_high, w_low, w2_high, w2_low, ht_high, ht_low = (
            st.sem(n) for n in ("w_high", "w_low", "w2_high", "w2_low", "ht_high", "ht_low"))
        W2_AT = {STEPS // (FC // 2) * (i + 1) - 1: i for i in range(FC // 2)} if gated else {}
        scattered, tp_full, x_high, x_low, h_full, act_done, h_ready, o_full, y_ready, y_stored, y_free = (st.sem(n) for n in (
            "scattered", "tp_full", "x_high", "x_low", "h_full", "act_done", "h_ready", "o_full", "y_ready", "y_stored", "y_free"))
        hidden_ready = h_ready if gated else act_done
        added = st.sem("added")
        if out_bias:
            gates, b2 = out_bias
            b2s = st.sb("b2", [plan.E, D])
            gT = k.XNT[0:plan.E, 0, :]
            b2_loaded, gT_full, gT_done, bias_full, bias_done = (
                st.sem(n) for n in ("b2_loaded", "gT_full", "gT_done", "bias_full", "bias_done"))

        def groups(eng, body):
            with eng.Fori(0, LOOPS) as it:
                for u in range(2):
                    body(2 * it + u, u, it)
            for g in range(2 * LOOPS, NG):
                body(g, g % 2, g // 2)

        with nc.Block() as block:
            @block.sync
            def _(sp):
                def load_w(g, u):
                    sp.dma_start(w[u][:], w_rows[at(P * g, P), :]).then_inc(w_loaded[u], DMA)

                def load_x(g, u):
                    sp.dma_start(xg[u][:], k.slot_x[at(GS * g, GS), :].rearrange("(t p) d -> p t d", p=P)).then_inc(x_loaded[u], DMA)

                if plan.capacity:
                    load_w(0, 0)
                    load_w(1, 1)
                if out_bias:
                    sp.dma_start(b2s[:], b2).then_inc(b2_loaded, DMA)
                sp.sem_inc(y_free, 2)
                sp.wait_ge(scattered, 2 * TILES * DMA)
                load_x(0, 0)
                load_x(1, 1)

                def body(g, u, turn):
                    more = not (isinstance(g, int) and g + 2 >= NG)
                    if more:
                        sp.wait_ge(tp_full, NTP * g + NTP)
                        load_x(g + 2, u)
                    sp.wait_ge(y_ready, GT * g + GT + 2)
                    sp.dma_start(k.slot_y[at(GS * g, GS), :].rearrange("(t p) d -> p t d", p=P), y[u][:]).then_inc(y_stored, DMA)
                    if plan.capacity and more:
                        load_w(g + 2, u)
                    sp.wait_ge(y_stored, DMA * g + DMA)
                    sp.sem_inc(y_free, 1)
                groups(sp, body)

            @block.gpsimd
            def _(pool):
                def gather_w(g):
                    pool.indirect_dma_start(w[g % 2][:], None, w_rows,
                                            bass.IndirectOffsetOnAxis(plan.w_row[:, g:g + 1], 0)).then_inc(w_loaded[g % 2], DMA)
                if not plan.capacity:
                    gather_w(0)
                    gather_w(1)
                for n in range(2 * TILES):
                    pool.indirect_dma_start(k.slot_x, bass.IndirectOffsetOnAxis(plan.to[:, n:n + 1], 0),
                                            src[:, n % TILES, :], None).then_inc(scattered, DMA)
                pool.wait_ge(scattered, 2 * TILES * DMA)
                if not plan.capacity:
                    for g in range(NG):
                        if 2 <= g + 1 < NG:
                            pool.wait_ge(o_full, GT * g)
                            gather_w(g + 1)
                        for i in W2_AT.values():
                            rows = slice(2 * i, 2 * i + 2)
                            pool.wait_ge(w2_high, FC // 2 * g + i + 1)
                            pool.tensor_tensor(w2p[:, 1, rows, :], w2[g % 2][:, rows, :], w2p[:, 0, rows, :].bitcast(F32),
                                               ALU.subtract).then_inc(w2_low, 1)

            @block.tensor
            def _(pe):
                def transposes(g, u, turn):
                    pe.wait_ge(x_loaded[u], DMA * turn + DMA)
                    for n, (c, t0, t1) in enumerate(TP):
                        pe.wait_ge(x_low, NTP * g + n + 1)
                        for t in range(t0, t1):
                            mm = pe.transpose(tp[:, n % 2, (t - t0) * P:(t - t0 + 1) * P], xg[u][:, t, c * P:(c + 1) * P], k.ident[:])
                        mm.then_inc(tp_full, 1)

                def body(g, u, turn):
                    pe.wait_ge(x_low, NTP * g + NTP + 2)
                    for s in range(STEPS):
                        j, b = divmod(s, NB)
                        pe.wait_ge(hidden_ready, STEPS * g + s + 1)
                        if b == 0:
                            pe.wait_ge(w_low, FC * g + j + 1)
                        for n in range(NW):
                            for i, (wp, xp) in enumerate(PARTS):
                                for c in range(DC):
                                    mm = pe.matmul(ph[n][:, s % HB, 0:BW], w1p[:, wp, c, n, j, :], xT[u][:, xp, c, b * BW:(b + 1) * BW],
                                                   start=i == 0 and c == 0, stop=i == len(PARTS) - 1 and c == DC - 1)
                        mm.then_inc(h_full, 1)
                    if not (isinstance(g, int) and g + 1 >= NG):
                        transposes(g + 1, 1 - u, turn + u)
                    for t in range(GT):
                        pe.wait_ge(y_ready, GT * g + t + 1)
                        for j in range(FC):
                            if t == 0:
                                if gated:
                                    pe.wait_ge(ht_low, STEPS * g + NB * (j + 1) + 2)
                                    pe.wait_ge(w2_low, FC // 2 * g + j // 2 + 1)
                                else:
                                    pe.wait_ge(act_done, STEPS * g + NB * (j + 1) + HB)
                            factors = [(ht[:, hp], w2p[:, wp]) for wp, hp in PARTS] if gated else [(ht, w2[u])]
                            for i, (h, w2_) in enumerate(factors):
                                mm = pe.matmul(po[:, (GT * u + t) % 2, 0:D], h[:, j, t * P:(t + 1) * P], w2_[:, j, :],
                                               start=i == 0 and j == 0, stop=i == len(factors) - 1 and j == FC - 1)
                        mm.then_inc(o_full, 1)

                if out_bias:
                    for q in range(TPB):
                        if q >= 2:
                            pe.wait_ge(gT_done, q - 1)
                        for t in range(TPB * q, TPB * (q + 1)):
                            mm = pe.transpose(tp[0:plan.E, q % 2, (t - TPB * q) * P:(t - TPB * q + 1) * P], gates[:, t, :], k.ident[:])
                        mm.then_inc(gT_full, 1)
                    pe.wait_ge(gT_done, TPB)
                    pe.wait_ge(b2_loaded, DMA)
                    for t in range(TILES):
                        if t >= 2:
                            pe.wait_ge(bias_done, t - 1)
                        pe.matmul(po[:, t % 2, 0:D], gT[:, t * P:(t + 1) * P], b2s[:], start=True, stop=True).then_inc(bias_full, 1)
                    pe.wait_ge(bias_done, TILES)
                transposes(0, 0, 0)
                groups(pe, body)

            @block.scalar
            def _(act):
                act.sem_inc(act_done, HB)

                def x_highs(g, u):
                    for n, (c, t0, t1) in enumerate(TP):
                        act.wait_ge(tp_full, NTP * g + n + 1)
                        act.copy(xT[u][:, 0, c, t0 * P:t1 * P], tp[:, n % 2, 0:(t1 - t0) * P]).then_inc(x_high, 1)

                def w_highs(g, u, turn, first=False):
                    act.wait_ge(w_loaded[u], DMA * turn + DMA)
                    for j in range(FC):
                        if not first:
                            act.wait_ge(h_full, STEPS * (g - 1) + NB * (j + 1))
                        act.copy(w1p[:, 0, :, :, j, :], w1[u][:, :, :, j, :]).then_inc(w_high, 1)

                def body(g, u, turn):
                    def ht_high_part(s):
                        act.wait_ge(h_ready, STEPS * g + s + 1 + HB)
                        act.copy(ht[:, 0, s, :], hidden[:, s % 2, :]).then_inc(ht_high, 1)

                    for s in range(STEPS):
                        j, b = divmod(s, NB)
                        act.wait_ge(h_full, STEPS * g + s + 1)
                        if gated:
                            act.wait_ge(h_ready, STEPS * g + s - 1 + HB)
                            act.activation(sg[:, s % 2, :], ph[0][:, s % HB, 0:BW], ACT.Silu, bias=b1[u][:, j:j + 1]).then_inc(act_done, 1)
                        else:
                            act.activation(ht[:, j, b * BW:(b + 1) * BW], ph[0][:, s % HB, 0:BW], ACT.Gelu_apprx_tanh).then_inc(act_done, 1)
                        if gated and s:
                            ht_high_part(s - 1)
                        if s in W2_AT:
                            rows = slice(2 * W2_AT[s], 2 * W2_AT[s] + 2)
                            act.copy(w2p[:, 0, rows, :], w2[u][:, rows, :]).then_inc(w2_high, 1)
                    if gated:
                        ht_high_part(STEPS - 1)
                    if not (isinstance(g, int) and g + 1 >= NG):
                        x_highs(g + 1, 1 - u)
                        w_highs(g + 1, 1 - u, turn + u)

                x_highs(0, 0)
                w_highs(0, 0, 0, True)
                groups(act, body)

            @block.vector
            def _(dve):
                dve.sem_inc(y_ready, 2)
                dve.sem_inc(x_low, 2)
                dve.sem_inc(ht_low, 2)
                if gated:
                    dve.sem_inc(h_ready, HB)
                if add:
                    dve.scalar_tensor_tensor(out=k.X[:].rearrange("p t d -> p (t d)"), in0=add[0].rearrange("p t d -> p (t d)"),
                                             scalar=k.tg[:, add[1]:add[1] + 1], in1=k.X[:].rearrange("p t d -> p (t d)"),
                                             op0=ALU.mult, op1=ALU.add).then_inc(added, 1)
                if out_bias:
                    for q in range(TPB):
                        dve.wait_ge(gT_full, q + 1)
                        dve.tensor_copy(gT[:, q * S:(q + 1) * S], tp[0:plan.E, q % 2, :]).then_inc(gT_done, 1)
                    for t in range(TILES):
                        dve.wait_ge(bias_full, t + 1)
                        dve.tensor_tensor(k.X[:, t, :], po[:, t % 2, 0:D], k.X[:, t, :], ALU.add).then_inc(bias_done, 1)

                def x_lows(g, u):
                    for n, (c, t0, t1) in enumerate(TP):
                        dve.wait_ge(x_high, NTP * g + n + 1)
                        dve.tensor_tensor(xT[u][:, 1, c, t0 * P:t1 * P], tp[:, n % 2, 0:(t1 - t0) * P],
                                          xT[u][:, 0, c, t0 * P:t1 * P].bitcast(F32), ALU.subtract).then_inc(x_low, 1)

                def w_lows(g, u, chunks):
                    for j in chunks:
                        dve.wait_ge(w_high, FC * g + j + 1)
                        dve.tensor_tensor(w1p[:, 1, :, :, j, :], w1[u][:, :, :, j, :], w1p[:, 0, :, :, j, :].bitcast(F32),
                                          ALU.subtract).then_inc(w_low, 1)

                def body(g, u, turn):
                    def ht_low_part(s):
                        dve.wait_ge(ht_high, STEPS * g + s + 1)
                        dve.tensor_tensor(ht[:, 1, s, :], hidden[:, s % 2, :], ht[:, 0, s, :].bitcast(F32), ALU.subtract).then_inc(ht_low, 1)

                    for s in range(STEPS if gated else 0):
                        if s >= 2:
                            ht_low_part(s - 2)
                        dve.wait_ge(act_done, STEPS * g + s + 1 + HB)
                        dve.wait_ge(ht_low, STEPS * g + s + 1)
                        dve.scalar_tensor_tensor(out=hidden[:, s % 2, :], in0=ph[1][:, s % HB, 0:BW], scalar=b1[u][:, FC + s:FC + s + 1],
                                                 in1=sg[:, s % 2, :], op0=ALU.add, op1=ALU.mult).then_inc(h_ready, 1)
                    if gated:
                        ht_low_part(STEPS - 2)
                        ht_low_part(STEPS - 1)
                    more = not (isinstance(g, int) and g + 1 >= NG)
                    if more:
                        x_lows(g + 1, 1 - u)
                    dve.wait_ge(y_free, g + 1)
                    for t in range(GT):
                        if more:
                            w_lows(g + 1, 1 - u, range(FC * t // GT, FC * (t + 1) // GT))
                        dve.wait_ge(o_full, GT * g + t + 1)
                        dve.tensor_copy(y[u][:, t, :], po[:, (GT * u + t) % 2, 0:D]).then_inc(y_ready, 1)

                x_lows(0, 0)
                w_lows(0, 0, range(FC))
                groups(dve, body)


def combine_stage(nc, k, name, plan):
    BATCH = 4
    with Stage(nc, name) as st:
        back = k.ATN.rearrange("p g n -> p (g n)").rearrange("p (n d) -> p n d", d=D)
        got = [st.sem(f"got{b}") for b in range(2 * TILES // BATCH)]
        done, stats_done = st.sem("done"), st.sem("stats_done")
        with nc.Block() as block:
            @block.gpsimd
            def _(pool):
                for n in range(2 * TILES):
                    pool.indirect_dma_start(back[:, n, :], None, k.slot_y[0:plan.NG * plan.GS, :],
                                            bass.IndirectOffsetOnAxis(plan.back[:, n:n + 1], 0)).then_inc(got[n // BATCH], DMA)

            @block.vector
            def _(dve):
                for n in range(2 * TILES):
                    i, t = divmod(n, TILES)
                    if n % BATCH == 0:
                        dve.wait_ge(got[n // BATCH], BATCH * DMA)
                    if i == 1:
                        dve.wait_ge(done, t + 1)
                    dve.scalar_tensor_tensor(out=k.X[:, t, :], in0=back[:, n, :], scalar=plan.weight[:, i, t:t + 1],
                                             in1=k.X[:, t, :], op0=ALU.mult, op1=ALU.add).then_inc(done, 1)
                    if n > TILES:
                        row_stats(dve, k, k.X, t - 1, done, n, stats_done)
                row_stats(dve, k, k.X, TILES - 1, done, 2 * TILES, stats_done)


def expert_layer_0(nc, k, a):
    layernorm_stage(nc, k, "l0f_ln", k.X, k.XN, k.XNT)
    with ExitStack() as ctx:
        gates = ctx.enter_context(nc.sbuf_tensor("l0f_gates", [P, TILES, 16], F32))
        floor = ctx.enter_context(nc.sbuf_tensor("l0f_floor", [P, TILES], F32))
        router_stage(nc, k, "l0f_r", a, k.XNT, a["r0w"], a["r0b"], 16, 6, "probs", 4, gates, floor)
        linear_experts_stage(nc, k, "l0f_e", a["e0w"], gates, floor, 16)


def expert_layer_2(nc, k, a):
    layernorm_stage(nc, k, "l2f_ln", k.X, k.XN, k.XNT)
    with ExitStack() as ctx:
        plan = Plan(nc, ctx, "l2f", 8, GROUP, False)
        gates = ctx.enter_context(nc.sbuf_tensor("l2f_gates", [P, TILES, 8], F32))
        router_stage(nc, k, "l2f_r", a, k.XNT, a["r2w"], a["r2b"], 8, 2, "logits", 6, gates, pick=plan.pick)
        slots_stage(nc, k, "l2f_s", a, plan, gates)
        grouped_experts_stage(nc, k, "l2f_e", k.XN, plan, a["e2rows"], 8, True, (gates, a["e2b2"]))
        combine_stage(nc, k, "l2f_c", plan)


def qkv_stage(nc, k, name, w_dram, qkv, width):
    with Stage(nc, name) as st:
        w = st.sb("w", [P, DC, width])
        po = st.ps("po", [P, 4, 512])
        loaded, full, evac = st.sem("loaded"), st.sem("full"), st.sem("evac")
        with nc.Block() as block:
            @block.sync
            def _(sp):
                sp.dma_start(w[:], w_dram.rearrange("(c p) n -> p c n", p=P)).then_inc(loaded, DMA)

            @block.tensor
            def _(pe):
                pe.wait_ge(loaded, DMA)
                for t in range(TILES):
                    if t >= 4:
                        pe.wait_ge(evac, t - 3)
                    for c in range(DC):
                        mm = pe.matmul(po[:, t % 4, 0:width], k.XNT[:, c, t * P:(t + 1) * P], w[:, c, :], start=c == 0, stop=c == DC - 1)
                    mm.then_inc(full, 1)

            @block.scalar
            def _(act):
                for t in range(TILES):
                    act.wait_ge(full, t + 1)
                    act.copy(qkv[:, t, :], po[:, t % 4, 0:width]).then_inc(evac, 1)


def short_attention_stage(nc, k, name, qkv, ao):
    KV, QH = 4, 4
    W = (QH + 2) * HD
    NEG = -3.4028234663852886e38
    POOLS = [(0, 0), (1, 0), (2, 0), (3, 0), (2, 2), (3, 2)]
    OWN = [(1, 1), (2, 1), (3, 1), (3, 3)]
    NP_, NO_ = len(POOLS), len(OWN)
    ORDER = [("pool", 0), ("pool", 1), ("own", 0), ("pool", 2), ("own", 1), ("pool", 3), ("own", 2), ("pool", 4), ("own", 3), ("pool", 5)]
    FREE = 2
    with Stage(nc, name) as st:
        prod = st.sb("prod", [P, 2, KV, QH, HD])
        own = st.sb("own", [P, 2, KV, QH, HD])
        sc = st.sb("sc", [P, TPB, B, B, H])
        m, s, r = (st.sb(n, [P, TPB * B, H]) for n in ("m", "s", "r"))
        step, prod_full, prod_used, own_full, own_used, shifted, exp_done, p_ready, tick = (
            st.sem(n) for n in ("step", "prod_full", "prod_used", "own_full", "own_used", "shifted", "exp_done", "p_ready", "tick"))
        q5 = qkv[:].rearrange("p (s a) (g f) -> p s a g f", s=B, f=W)
        ao5 = ao.rearrange("p (s a) (g h d) -> p s a g h d", s=B, g=KV, h=QH)
        sc3 = sc[:].rearrange("p a s t h -> p (a s) t h")

        def heads(x):
            return x.unsqueeze(2).broadcast_to([P, KV, QH, HD])

        def query_key(a, sq, t):
            return (q5[:, sq, bass.ds(a, 1), :, 0:QH * HD].rearrange("p a g (h d) -> p (a g) h d", h=QH),
                    heads(q5[:, t, bass.ds(a, 1), :, QH * HD:(QH + 1) * HD].rearrange("p a g d -> p (a g) d")))

        def value_prob(a, sq, t):
            prob = sc[:, bass.ds(a, 1), sq, t, :].rearrange("p a (g h) -> p (a g) h", g=KV)
            return (heads(q5[:, t, bass.ds(a, 1), :, (QH + 1) * HD:W].rearrange("p a g d -> p (a g) d")),
                    prob.unsqueeze(3).broadcast_to([P, KV, QH, HD]))

        with nc.Block() as block:
            @block.gpsimd
            def _(pool):
                pool.sem_inc(prod_used, FREE)

                def products(before, factors):
                    with pool.Fori(0, TPB) as a:
                        for n, (sq, t) in enumerate(POOLS):
                            pool.wait_ge(prod_used, NP_ * a + before + n + 1)
                            pool.sem_inc(tick, 1)
                            pool.tensor_tensor(prod[:, n % 2], *factors(a, sq, t), ALU.mult).then_inc(prod_full, 1)

                products(0, query_key)
                pool.wait_ge(p_ready, 1)
                products(NP_ * TPB, value_prob)

            @block.scalar
            def _(act):
                act.wait_ge(shifted, 1)
                act.activation(sc3, sc3, ACT.Exp, scale=HD ** -0.5).then_inc(exp_done, 1)

            @block.vector
            def _(dve):
                dve.sem_inc(own_used, FREE)
                dve.memset(sc[:], NEG).then_inc(step, 1)
                dve.wait_ge(step, 1)

                def make_own(a, before, n, factors):
                    dve.wait_ge(own_used, NO_ * a + before + n + 1)
                    dve.tensor_tensor(own[:, n % 2], *factors(a, *OWN[n]), ALU.mult).then_inc(own_full, 1)

                def each_product(a, turn, factors, use):
                    make_own(a, NO_ * turn, 0, factors)
                    for who, n in ORDER:
                        if who == "pool":
                            dve.wait_ge(prod_full, NP_ * a + NP_ * turn + n + 1)
                            use(*POOLS[n], prod[:, n % 2], prod_used)
                        else:
                            dve.wait_ge(own_full, NO_ * a + NO_ * turn + n + 1)
                            if n + 1 < NO_:
                                make_own(a, NO_ * turn, n + 1, factors)
                            use(*OWN[n], own[:, n % 2], own_used)

                with dve.Fori(0, TPB) as a:
                    def score(sq, t, product, used):
                        dve.tensor_reduce(sc[:, bass.ds(a, 1), sq, t, :].rearrange("p a (g h) -> p (a g) h", g=KV),
                                          product, AX.X, ALU.add).then_inc(used, 1)
                    each_product(a, 0, query_key, score)
                dve.wait_ge(prod_used, NP_ * TPB + FREE)
                dve.wait_ge(own_used, NO_ * TPB + FREE)
                do = Chain(dve, step, 1)
                by_head = sc3.rearrange("p n t h -> p n h t")

                def over_keys(x):
                    return x.unsqueeze(2).broadcast_to([P, TPB * B, B, H])

                do(dve.tensor_reduce(m[:], by_head, AX.X, ALU.max))
                dve.tensor_tensor(sc3, sc3, over_keys(m[:]), ALU.subtract).then_inc(shifted, 1)
                dve.wait_ge(exp_done, 1)
                do(dve.tensor_reduce(s[:], by_head, AX.X, ALU.add))
                do(dve.reciprocal(r[:], s[:]))
                dve.tensor_tensor(sc3, sc3, over_keys(r[:]), ALU.mult).then_inc(p_ready, 1)
                dve.wait_ge(p_ready, 1)
                with dve.Fori(0, TPB) as a:
                    last = {}

                    def add(sq, t, product, used):
                        out = ao5[:, sq, bass.ds(a, 1)].rearrange("p a g h d -> p (a g h d)")
                        src = product.rearrange("p g h d -> p (g h d)")
                        if t == 0:
                            dve.tensor_scalar(out, src, 1.0, None, ALU.mult).then_inc(used, 1)
                        else:
                            sem, per, count = last[sq]
                            dve.wait_ge(sem, per * a + per * TPB + count + FREE)
                            dve.tensor_tensor(out, out, src, ALU.add).then_inc(used, 1)
                        pairs = POOLS if used is prod_used else OWN
                        last[sq] = (used, len(pairs), pairs.index((sq, t)) + 1)
                    each_product(a, TPB, value_prob, add)


def expert_layer_1(nc, k, a):
    E, GATE = 8, 5
    with ExitStack() as ctx:
        y = ctx.enter_context(nc.sbuf_tensor("l1f_y", [P, TILES, D], F32))
        layernorm_stage(nc, k, "l1f_ln", k.X, k.XN)
        layernorm_stage(nc, k, "l1f_ln1", k.XN, y, k.XNT, affine=(a["ln1w"], a["ln1b"]), have_stats=False)
        with ExitStack() as inner:
            qkv = inner.enter_context(nc.sbuf_tensor("l1f_qkv", [P, TILES, 384], F32))
            qkv_stage(nc, k, "l1f_qkv_s", a["qkvw"], qkv, 384)
            short_attention_stage(nc, k, "l1f_sa", qkv, y[:])
        transpose_stage(nc, k, "l1f_t", y, k.XNT)
        project_add_stage(nc, k, "l1f_pr", a["projw"], k.XN)
        layernorm_stage(nc, k, "l1f_ln2", k.XN, y, k.XNT, affine=(a["ln2w"], a["ln2b"]))
        gates = ctx.enter_context(nc.sbuf_tensor("l1f_gates", [P, TILES, E], F32))
        plan = Plan(nc, ctx, "l1f", E, CAPACITY, True)
        router_stage(nc, k, "l1f_r", a, k.XNT, a["r1w"], a["zero_rows"][:, 0:E], E, 2, "probs", GATE, gates, pick=plan.pick)
        slots_stage(nc, k, "l1f_s", a, plan, gates)
        grouped_experts_stage(nc, k, "l1f_e", y, plan, a["e1rows"], 4, False, add=(k.XN, GATE))
        combine_stage(nc, k, "l1f_c", plan)


def project_add_stage(nc, k, name, w_dram, acc):
    with Stage(nc, name) as st:
        w = st.sb("w", [P, DC, D])
        po = st.ps("po", [P, 4, 512])
        loaded, full, evac, stats_done = st.sem("loaded"), st.sem("full"), st.sem("evac"), st.sem("stats_done")
        with nc.Block() as block:
            @block.sync
            def _(sp):
                sp.dma_start(w[:], w_dram.rearrange("(c p) n -> p c n", p=P)).then_inc(loaded, DMA)

            @block.tensor
            def _(pe):
                pe.wait_ge(loaded, DMA)
                for t in range(TILES):
                    if t >= 4:
                        pe.wait_ge(evac, t - 3)
                    for c in range(DC):
                        mm = pe.matmul(po[:, t % 4, 0:D], k.XNT[:, c, t * P:(t + 1) * P], w[:, c, :], start=c == 0, stop=c == DC - 1)
                    mm.then_inc(full, 1)

            @block.vector
            def _(dve):
                for t in range(TILES):
                    dve.wait_ge(full, t + 1)
                    dve.tensor_tensor(acc[:, t, :], po[:, t % 4, 0:D], acc[:, t, :], ALU.add).then_inc(evac, 1)
                    if t:
                        row_stats(dve, k, acc, t - 1, evac, t, stats_done)
                row_stats(dve, k, acc, TILES - 1, evac, TILES, stats_done)


def single_head_stage(nc, k, name, qT, kT, v, scale, out, gate=None):
    with Stage(nc, name) as st:
        qb = [st.sb(f"qb{u}", [P, DC, S]) for u in range(2)]
        prob = st.sb("prob", [P, 2, S])
        pT = st.sb("pT", [P, 2, TPB, P])
        negm = st.sb("negm", [P, 2])
        nbias = st.sb("nbias", [P, 2])
        psum_row = st.sb("sum", [P, 2])
        rinv = st.sb("rinv", [P, 2])
        ps_s = st.ps("ps_s", [P, 2, S])
        ps_t = st.ps("ps_t", [P, 2, TPB, P])
        ps_o = st.ps("ps_o", [P, 2, 512])
        (qb_ready, s_full, negm_done, nbias_done, exp_done, t_full, t_evac, o_full, o_evac, r_step, tick) = (
            st.sem(n) for n in ("qb_ready", "s_full", "negm_done", "nbias_done", "exp_done", "t_full", "t_evac",
                                "o_full", "o_evac", "r_step", "tick"))
        PER = 2 * TPB
        with nc.Block() as block:
            @block.gpsimd
            def _(pool):
                with pool.Fori(0, B // 2) as it:
                    for u in range(2):
                        pool.wait_ge(s_full, PER * it + 1)
                        pool.sem_inc(tick, 1)
                        pool.tensor_copy(qb[u][:], qT[:, :, bass.ds((2 * it + u) * S, S)]).then_inc(qb_ready, 1)

            @block.tensor
            def _(pe):
                pe.sem_inc(s_full, 1)
                pe.sem_inc(t_full, 1)
                pe.sem_inc(o_full, 2)
                with pe.Fori(0, B // 2) as it:
                    def scores(n):
                        u, qt = divmod(n, TPB)
                        if qt == 0:
                            pe.wait_ge(qb_ready, 2 * it + u + 1)
                        pe.wait_ge(exp_done, PER * it + n + 1)
                        for c in range(DC):
                            mm = pe.matmul(ps_s[:, n % 2, :], qb[u][:, c, qt * P:(qt + 1) * P],
                                           kT[:, c, bass.ds((2 * it + u) * S, S)], start=c == 0, stop=c == DC - 1)
                        mm.then_inc(s_full, 1)

                    def transposes(n):
                        pe.wait_ge(exp_done, PER * it + n + 1 + 2)
                        pe.wait_ge(t_evac, PER * it + n + 1)
                        for kt in range(TPB):
                            mm = pe.transpose(ps_t[:, n % 2, kt, :], prob[:, n % 2, kt * P:(kt + 1) * P], k.ident[:])
                        mm.then_inc(t_full, 1)

                    def values(n):
                        pe.wait_ge(t_evac, PER * it + n + 1 + 2)
                        pe.wait_ge(o_evac, PER * it + n + 1)
                        for kt in range(TPB):
                            mm = pe.matmul(ps_o[:, n % 2, 0:D], pT[:, n % 2, kt, :],
                                           v[:, bass.ds((2 * it + n // TPB) * TPB + kt, 1), :], start=kt == 0, stop=kt == TPB - 1)
                        mm.then_inc(o_full, 1)

                    scores(0)
                    for n in range(PER):
                        if n + 1 < PER:
                            scores(n + 1)
                        if n:
                            values(n - 1)
                        transposes(n)
                    values(PER - 1)

            @block.scalar
            def _(act):
                act.sem_inc(exp_done, 2)
                with act.Fori(0, B // 2) as it:
                    for n in range(PER):
                        act.wait_ge(nbias_done, PER * it + n + 1 + 1)
                        act.wait_ge(t_full, PER * it + n + 1)
                        act.wait_ge(r_step, PER * it + n + 1)
                        act.activation(prob[:, n % 2, :], ps_s[:, n % 2, :], ACT.Exp, bias=nbias[:, n % 2:n % 2 + 1], scale=scale,
                                       accum_out=psum_row[:, n % 2:n % 2 + 1]).then_inc(exp_done, 1)

            @block.vector
            def _(dve):
                dve.sem_inc(t_evac, 2)
                dve.sem_inc(o_evac, 2)
                dve.sem_inc(r_step, 2)
                dve.sem_inc(nbias_done, 1)
                with dve.Fori(0, B // 2) as it:
                    def row_max(n):
                        dve.wait_ge(s_full, PER * it + n + 1 + 1)
                        dve.wait_ge(nbias_done, PER * it + n + 1)
                        dve.tensor_reduce(negm[:, n % 2:n % 2 + 1], ps_s[:, n % 2, :], AX.X, ALU.max, negate=True).then_inc(negm_done, 1)
                        dve.wait_ge(negm_done, PER * it + n + 1)
                        dve.wait_ge(exp_done, PER * it + n + 1)
                        dve.tensor_scalar(nbias[:, n % 2:n % 2 + 1], negm[:, n % 2:n % 2 + 1], scale, None, ALU.mult).then_inc(nbias_done, 1)

                    def finish(n):
                        dve.wait_ge(exp_done, PER * it + n + 1 + 2)
                        dve.wait_ge(o_evac, PER * it + n + 2)
                        dve.reciprocal(rinv[:, n % 2:n % 2 + 1], psum_row[:, n % 2:n % 2 + 1]).then_inc(r_step, 1)
                        dve.wait_ge(o_full, PER * it + n + 1 + 2)
                        dve.wait_ge(r_step, PER * it + n + 1 + 2)
                        tile = bass.ds(PER * it + n, 1)
                        o = out[:, tile, :].rearrange("p t d -> p (t d)")
                        if gate is None:
                            dve.tensor_scalar(o, ps_o[:, n % 2, 0:D], rinv[:, n % 2:n % 2 + 1], None, ALU.mult).then_inc(o_evac, 1)
                        else:
                            dve.scalar_tensor_tensor(out=o, in0=ps_o[:, n % 2, 0:D], scalar=rinv[:, n % 2:n % 2 + 1], in1=o,
                                                     op0=ALU.mult, op1=ALU.add).then_inc(o_evac, 1)

                    row_max(0)
                    for n in range(PER):
                        if n + 1 < PER:
                            row_max(n + 1)
                        if n:
                            finish(n - 1)
                        dve.wait_ge(t_full, PER * it + n + 1 + 1)
                        dve.wait_ge(o_full, PER * it + n + 1)
                        dve.tensor_copy(pT[:, n % 2], ps_t[:, n % 2]).then_inc(t_evac, 1)
                    finish(PER - 1)


def feature_major_stage(nc, k, name, w, bias, dst_T):
    with Stage(nc, name) as st:
        po = st.ps("po", [P, 4, 512])
        full, evac = st.sem("full"), st.sem("evac")
        with nc.Block() as block:
            @block.tensor
            def _(pe):
                for n in range(DC * B):
                    m, b = divmod(n, B)
                    if n >= 4:
                        pe.wait_ge(evac, n - 3)
                    for c in range(DC):
                        mm = pe.matmul(po[:, n % 4, :], w[:, c, m * P:(m + 1) * P], k.XNT[:, c, b * S:(b + 1) * S], start=c == 0, stop=c == DC - 1)
                    mm.then_inc(full, 1)

            @block.scalar
            def _(act):
                for n in range(DC * B):
                    m, b = divmod(n, B)
                    act.wait_ge(full, n + 1)
                    act.activation(dst_T[:, m, b * S:(b + 1) * S], po[:, n % 4, :], ACT.Identity, bias=bias[:, m:m + 1]).then_inc(evac, 1)


def fuse_stage(nc, k, name, w, bias, oT, gate):
    with Stage(nc, name) as st:
        po = st.ps("po", [P, 4, 512])
        full, evac, step, stats_done = st.sem("full"), st.sem("evac"), st.sem("step"), st.sem("stats_done")
        with nc.Block() as block:
            @block.tensor
            def _(pe):
                for t in range(TILES):
                    if t >= 4:
                        pe.wait_ge(evac, t - 3)
                    for c in range(2 * DC):
                        src = k.XNT if c < DC else oT
                        mm = pe.matmul(po[:, t % 4, 0:D], src[:, c % DC, t * P:(t + 1) * P], w[:, c, :], start=c == 0, stop=c == 2 * DC - 1)
                    mm.then_inc(full, 1)

            @block.vector
            def _(dve):
                do = Chain(dve, step)
                do(dve.tensor_scalar(bias[:], bias[:], k.tg[:, gate:gate + 1], None, ALU.mult))
                do(dve.tensor_tensor(k.X[:], k.X[:], bias[:].unsqueeze(1).broadcast_to([P, TILES, D]), ALU.add))
                for t in range(TILES):
                    dve.wait_ge(full, t + 1)
                    dve.scalar_tensor_tensor(out=k.X[:, t, :], in0=po[:, t % 4, 0:D], scalar=k.tg[:, gate:gate + 1],
                                             in1=k.X[:, t, :], op0=ALU.mult, op1=ALU.add).then_inc(evac, 1)
                    if t:
                        row_stats(dve, k, k.X, t - 1, evac, t, stats_done)
                row_stats(dve, k, k.X, TILES - 1, evac, TILES, stats_done)


def knowledge_layer(nc, k, a):
    with ExitStack() as ctx:
        def sb(name, shape=(P, DC, B * S)):
            return ctx.enter_context(nc.sbuf_tensor("l2x_" + name, list(shape), F32))
        qT, ctxT, v = sb("qT"), sb("ctxT"), sb("v", [P, TILES, D])
        wq, bq, wf, bf = sb("wq", [P, DC, D]), sb("bq", [P, DC]), sb("wf", [P, 2 * DC, D]), sb("bf", [P, D])
        layernorm_stage(nc, k, "l2x_ln", k.X, k.XN, k.XNT, prefetch=[
            (wq[:], a["w2x1"].rearrange("(c p) n -> p c n", p=P)), (bq[:], a["b2x1"]),
            (ctxT[:], a["ctxT"].rearrange("(c p) n -> p c n", p=P)), (v[:], a["ctx"].rearrange("(t p) d -> p t d", p=P)),
            (wf[:], a["w2x2"].rearrange("(c p) n -> p c n", p=P)), (bf[:], a["b2x2"])])
        feature_major_stage(nc, k, "l2x_q", wq, bq, qT)
        single_head_stage(nc, k, "l2x_a", qT, ctxT, v, D ** -0.5, k.XN)
        transpose_stage(nc, k, "l2x_t", k.XN, qT)
        fuse_stage(nc, k, "l2x_f", wf, bf, qT, 2)


TREES, LEAVES, LEVELS = 3, 16, 4
HIDDEN = 64
NODES = LEAVES - 1


class LeafWeights:

    def __init__(self, nc, ctx, name, w1, w2):
        self.w1, self.w2 = w1, w2
        self.b1 = ctx.enter_context(nc.sbuf_tensor(f"{name}_b1", [P, LEAVES * HIDDEN // P], F32))
        self.b2 = ctx.enter_context(nc.sbuf_tensor(f"{name}_b2", [LEAVES, D], F32))

    LOADS = DC + 3

    def load(self, sp, a, x, loaded):
        w1, w2 = a[f"t{x}w1"], a[f"t{x}w2"]
        for c in range(DC):
            sp.dma_start(self.w1[:, c, :].rearrange("p (l h) -> p l h", l=LEAVES),
                         w1[:, c * P:(c + 1) * P, :].rearrange("l p h -> p l h")).then_inc(loaded, DMA)
        sp.dma_start(self.w2[:], w2.rearrange("(j two) h n -> (two h) j n", two=2)).then_inc(loaded, DMA)
        sp.dma_start(self.b1[:], a[f"t{x}b1"]).then_inc(loaded, DMA)
        sp.dma_start(self.b2[:], a[f"t{x}b2"]).then_inc(loaded, DMA)


def trees_stage(nc, k, name, a, sel_T, x_high, x_low, leaf_weights):
    HALF = TILES // 2
    with Stage(nc, name) as st:
        w = st.sb("w", [P, DC, TREES * NODES])
        nb = st.sb("nb", [P, TREES * NODES])
        bit = st.sb("bit", [P, TILES * TREES, NODES])
        ind = [st.sb(f"ind{lv}", [P, TILES * TREES, 2 ** (lv + 1)]) for lv in range(LEVELS)]
        ps = st.ps("ps_n", [P, 2, HALF, 64])
        tp = st.ps("tp", [LEAVES, TILES, P])
        loaded, full, step, sel_done, t_full, act_evac, dve_evac, leaves_loaded = (
            st.sem(n) for n in ("loaded", "full", "step", "sel_done", "t_full", "act_evac", "dve_evac", "leaves_loaded"))

        def bank(n):
            r, q = divmod(n, TPB)
            return sel_T[r][:, q * S:(q + 1) * S], tp[:, TPB * q:TPB * (q + 1), :].rearrange("l t p -> l (t p)")

        high_done, low_done = st.sem("high_done"), st.sem("low_done")
        with nc.Block() as block:
            @block.sync
            def _(sp):
                sp.dma_start(w[:], a["tnw"].rearrange("(c p) e -> p c e", p=P)).then_inc(loaded, DMA)
                sp.dma_start(nb[:], a["tnb"]).then_inc(loaded, DMA)
                leaf_weights.load(sp, a, "q", leaves_loaded)
                sp.wait_ge(leaves_loaded, LeafWeights.LOADS * DMA)

            @block.tensor
            def _(pe):
                pe.wait_ge(loaded, 2 * DMA)
                for t in range(TILES):
                    for c in range(DC):
                        mm = pe.matmul(ps[:, t // HALF, t % HALF, 0:TREES * NODES], k.XNT[:, c, t * P:(t + 1) * P], w[:, c, :],
                                       start=c == 0, stop=c == DC - 1)
                mm.then_inc(full, 1)
                pe.wait_ge(sel_done, 1)
                for n in range(TREES * TPB):
                    r, q = divmod(n, TPB)
                    if n >= TPB:
                        pe.wait_ge(act_evac if n % 2 == 0 else dve_evac, (n - TPB) // 2 + 1)
                    for t in range(TPB * q, TPB * (q + 1)):
                        mm = pe.transpose(tp[:, t, :], ind[-1][:, TREES * t + r, :], k.ident[:])
                    mm.then_inc(t_full, 1)

            @block.scalar
            def _(act):
                act.wait_ge(full, 1)
                for b in range(B):
                    act.copy(x_high[:, :, b * S:(b + 1) * S], k.XNT[:, :, b * S:(b + 1) * S]).then_inc(high_done, 1)
                for n in range(0, TREES * TPB, 2):
                    act.wait_ge(t_full, n + 1)
                    act.copy(*bank(n)).then_inc(act_evac, 1)

            @block.vector
            def _(dve):
                do = Chain(dve, step)
                dve.wait_ge(loaded, 2 * DMA)
                dve.wait_ge(full, 1)
                do(dve.tensor_tensor(bit[:].rearrange("p (u t r) n -> p u t (r n)", u=2, r=TREES), ps[:, :, :, 0:TREES * NODES],
                                     nb[:].unsqueeze(1).unsqueeze(1).broadcast_to([P, 2, HALF, TREES * NODES]), ALU.add))
                do(dve.tensor_scalar(bit[:], bit[:], 0.0, None, ALU.is_ge))
                do(dve.tensor_copy(ind[0][:, :, 1:2], bit[:, :, 0:1]))
                do(dve.tensor_scalar(ind[0][:, :, 0:1], bit[:, :, 0:1], -1.0, 1.0, ALU.mult, ALU.add))
                for lv in range(1, LEVELS):
                    n = 2 ** lv
                    kids = ind[lv][:].rearrange("p t (n two) -> p t n two", two=2)
                    do(dve.tensor_tensor(kids[:, :, :, 1], ind[lv - 1][:], bit[:, :, n - 1:2 * n - 1], ALU.mult))
                    do(dve.tensor_tensor(kids[:, :, :, 0], ind[lv - 1][:], kids[:, :, :, 1], ALU.subtract))
                dve.sem_inc(sel_done, 1)
                for n in range(1, TREES * TPB, 2):
                    dve.wait_ge(t_full, n + 1)
                    dve.tensor_copy(*bank(n)).then_inc(dve_evac, 1)
                for b in range(B):
                    row = slice(b * S, (b + 1) * S)
                    dve.wait_ge(high_done, b + 1)
                    dve.tensor_tensor(x_low[:, :, row], k.XNT[:, :, row], x_high[:, :, row].bitcast(F32), ALU.subtract).then_inc(low_done, 1)


def leaves_stage(nc, k, name, weights, x_parts, sel_T, spread, dst, gate=None, then_load=None):
    feature_major = gate is None
    FC = LEAVES * HIDDEN // P
    CH = 2 * P
    PIECES = FC // 2
    NO = 2
    HB = 4
    LAST = len(PARTS) - 1
    with Stage(nc, name) as st:
        w1s, w2s, b1s, b2s = weights.w1, weights.w2, weights.b1, weights.b2
        w1p = st.sb("w1p", [P, 2, DC, FC * P], F32R)
        w2p = st.sb("w2p", [P, 2, FC, D], F32R)
        selb = st.sb("selb", [LEAVES, CH])
        relu = st.sb("relu", [P, 2, CH])
        hidden = st.sb("hidden", [P, 2, CH])
        ht = st.sb("ht", [P, 2, FC, CH], F32R)
        banks = st.ps("banks", [P, HB, 2, CH])
        ph, pm = banks[:, :, 0, :], banks[:, :, 1, :]
        po = st.ps("po", [P, NO, 512])
        (next_loaded, w_high, w_low, selb_ready, h_full, relu_done, h_ready, ht_high, ht_low, o_full, o_evac, tick) = (
            st.sem(n) for n in ("next_loaded", "w_high", "w_low", "selb_ready", "h_full", "relu_done", "h_ready", "ht_high",
                                "ht_low", "o_full", "o_evac", "tick"))

        def piece(n):
            if n < PIECES:
                cols = slice(2 * n * P, (2 * n + 2) * P)
                return w1s[:, :, cols], [w1p[:, i, :, cols] for i in range(2)]
            rows = slice(2 * (n - PIECES), 2 * (n - PIECES) + 2)
            return w2s[:, rows, :], [w2p[:, i, rows, :] for i in range(2)]

        with nc.Block() as block:
            if then_load:
                @block.sync
                def _(sp):
                    sp.wait_ge(w_low, 2 * PIECES)
                    then_load(sp, next_loaded)
                    sp.wait_ge(next_loaded, LeafWeights.LOADS * DMA)

            @block.gpsimd
            def _(pool):
                with pool.Fori(0, B * S // CH) as b:
                    pool.wait_ge(o_full, NO * b + 1)
                    pool.sem_inc(tick, 1)
                    pool.tensor_copy(selb[:], sel_T[:, bass.ds(b * CH, CH)]).then_inc(selb_ready, 1)

            @block.tensor
            def _(pe):
                pe.sem_inc(o_full, 1)
                with pe.Fori(0, B * S // CH) as b:
                    row = bass.ds(b * CH, CH)
                    for j in range(FC):
                        pe.wait_ge(h_ready, FC * b + j + 1)
                        pe.wait_ge(w_low, j // 2 + 1)
                        for i, (wp, xp) in enumerate(PARTS):
                            for c in range(DC):
                                pe.matmul(ph[:, j % HB, :], w1p[:, wp, c, j * P:(j + 1) * P], x_parts[xp][:, c, row],
                                          start=i == 0 and c == 0, stop=i == LAST and c == DC - 1)
                        pe.matmul(pm[:, j % HB, :], spread[:, j * P:(j + 1) * P], sel_T[:, row], start=True, stop=True).then_inc(h_full, 1)
                    pe.wait_ge(selb_ready, b + 1)
                    pe.wait_ge(w_low, 2 * PIECES)
                    for n in range(NO):
                        cols = slice(n * P, (n + 1) * P)
                        pe.wait_ge(o_evac, NO * b + n + 1)
                        for j in range(FC):
                            if n == 0:
                                pe.wait_ge(ht_low, FC * b + j + 1 + 1)
                            for i, (wp, hp) in enumerate(PARTS):
                                if feature_major:
                                    pe.matmul(po[:, n, 0:CH], w2p[:, wp, j, cols], ht[:, hp, j, :], start=i == 0 and j == 0, stop=False)
                                else:
                                    pe.matmul(po[:, n, 0:D], ht[:, hp, j, cols], w2p[:, wp, j, :], start=i == 0 and j == 0, stop=False)
                        if feature_major:
                            mm = pe.matmul(po[:, n, 0:CH], b2s[:, cols], selb[:], start=False, stop=True)
                        else:
                            mm = pe.matmul(po[:, n, 0:D], selb[:, cols], b2s[:], start=False, stop=True)
                        mm.then_inc(o_full, 1)

            @block.scalar
            def _(act):
                act.sem_inc(o_evac, NO)
                for n in range(2 * PIECES):
                    raw, parts = piece(n)
                    act.copy(parts[0], raw).then_inc(w_high, 1)
                with act.Fori(0, B * S // CH) as b:
                    def high(j):
                        act.wait_ge(h_ready, FC * b + j + 1 + HB)
                        act.copy(ht[:, 0, j, :], hidden[:, j % 2, :]).then_inc(ht_high, 1)

                    for j in range(FC):
                        act.wait_ge(h_full, FC * b + j + 1)
                        act.wait_ge(h_ready, FC * b + j - 1 + HB)
                        act.activation(relu[:, j % 2, :], ph[:, j % HB, :], ACT.Relu, bias=b1s[:, j:j + 1]).then_inc(relu_done, 1)
                        if j:
                            high(j - 1)
                    high(FC - 1)
                    for n in range(NO):
                        act.wait_ge(o_full, NO * b + n + 1 + 1)
                        act.sem_inc(tick, 1)
                        if feature_major:
                            act.copy(dst[:, n, bass.ds(b * CH, CH)], po[:, n, 0:CH]).then_inc(o_evac, 1)
                        else:
                            act.activation(dst[:, bass.ds(NO * b + n, 1), :].rearrange("p t d -> p (t d)"), po[:, n, 0:D],
                                           ACT.Identity, scale=k.tg[:, gate:gate + 1]).then_inc(o_evac, 1)

            @block.vector
            def _(dve):
                dve.sem_inc(h_ready, HB)
                dve.sem_inc(ht_low, 1)
                for n in range(2 * PIECES):
                    raw, parts = piece(n)
                    dve.wait_ge(w_high, n + 1)
                    dve.tensor_tensor(parts[1], raw, parts[0].bitcast(F32), ALU.subtract).then_inc(w_low, 1)
                with dve.Fori(0, B * S // CH) as b:
                    def low(j):
                        dve.wait_ge(ht_high, FC * b + j + 1)
                        dve.tensor_tensor(ht[:, 1, j, :], hidden[:, j % 2, :], ht[:, 0, j, :].bitcast(F32), ALU.subtract).then_inc(ht_low, 1)

                    for j in range(FC):
                        if j >= 2:
                            low(j - 2)
                        dve.wait_ge(relu_done, FC * b + j + 1)
                        dve.wait_ge(ht_low, FC * b + (j - 1 if j else 0) + 1)
                        dve.tensor_tensor(hidden[:, j % 2, :], pm[:, j % HB, :], relu[:, j % 2, :], ALU.mult).then_inc(h_ready, 1)
                    low(FC - 2)
                    low(FC - 1)


def tree_layer(nc, k, a):
    layernorm_stage(nc, k, "l3f_ln", k.X, k.XN, k.XNT)
    with ExitStack() as ctx:
        qT, kT, v = ctx.enter_context(nc.sbuf_tensor("l3f_qT", [P, DC, B * S], F32)), k.XNT, k.XN
        with ExitStack() as inner:
            sel_T = [inner.enter_context(nc.sbuf_tensor(f"l3f_selT{r}", [LEAVES, B * S], BF16)) for r in range(TREES)]
            spread = inner.enter_context(nc.sbuf_tensor("l3f_spread", [LEAVES, LEAVES * HIDDEN], BF16))
            spread_stage(nc, k, "l3f_s", a["spread"], spread)
            w1 = inner.enter_context(nc.sbuf_tensor("l3f_leaves_w1", [P, DC, LEAVES * HIDDEN], F32))
            w2 = inner.enter_context(nc.sbuf_tensor("l3f_leaves_w2", [P, LEAVES * HIDDEN // P, D], F32))
            leaves = [LeafWeights(nc, inner, f"l3f_leaves{r}", w1, w2) for r in range(TREES)]
            x_high, x_low = (inner.enter_context(nc.sbuf_tensor(f"l3f_x_{part}", [P, DC, B * S], F32R)) for part in ("high", "low"))
            trees_stage(nc, k, "l3f_t", a, sel_T, x_high[:], x_low[:], leaves[0])
            for r, (x, dst) in enumerate((("q", qT), ("k", kT), ("v", v))):
                then_load = (lambda sp, sem: leaves[r + 1].load(sp, a, "qkv"[r + 1], sem)) if r + 1 < TREES else None
                leaves_stage(nc, k, f"l3f_{x}l", leaves[r], (x_high[:], x_low[:]), sel_T[r], spread, dst,
                             7 if x == "v" else None, then_load)
        single_head_stage(nc, k, "l3f_a", qT, kT, v, D ** -0.5, k.X, gate=7)


def spread_stage(nc, k, name, spread_dram, spread):
    with Stage(nc, name) as st:
        raw = st.sb("raw", [LEAVES, LEAVES * HIDDEN])
        loaded, done = st.sem("loaded"), st.sem("done")
        with nc.Block() as block:
            @block.sync
            def _(sp):
                sp.dma_start(raw[:], spread_dram).then_inc(loaded, DMA)

            @block.vector
            def _(dve):
                dve.wait_ge(loaded, DMA)
                dve.tensor_copy(spread[:], raw[:]).then_inc(done, 1)
                dve.wait_ge(done, 1)


def more_stages(nc, k, a):
    return [
        lambda: expert_layer_0(nc, k, a),
        lambda: attention_layer(nc, k, "l1x", a, a["w1q"], a["w1k"], a["w1v"], a["zero_col"], a["zero_col"], a["zero_rows"],
                                a["w1o"], a["b1o"], D ** -0.5, 1, mask=(a["m1"], a["m1T"], True)),
        lambda: expert_layer_1(nc, k, a),
        lambda: knowledge_layer(nc, k, a),
        lambda: expert_layer_2(nc, k, a),
        lambda: attention_layer(nc, k, "l3x", a, a["w3q"], a["w3k"], a["w3v"], a["b3q"], a["b3k"], a["b3v"], a["w3o"],
                                a["b3o"], HD ** -0.5, 3, tril2=a["tril2"]),
        lambda: tree_layer(nc, k, a),
    ]


def more_layout(n, all_rows, columns, T):
    import numpy as np
    f32 = np.float32

    def expert_rows(w1, w2, b1=None):
        E = w1.shape[0]
        parts = [w1.reshape(E, DC, P, -1).transpose(0, 2, 1, 3), w2.reshape(E, -1, P, D).transpose(0, 2, 1, 3)]
        if b1 is not None:
            parts.append(b1.reshape(E, -1, P).transpose(0, 2, 1))
        return np.concatenate([x.reshape(E * P, -1) for x in parts], 1)

    a = {f"ranks{E}": all_rows(np.arange(E, 0, -1).astype(f32)) for E in (8, 16)}
    a["before"] = np.triu(np.ones((P, P), f32), 1)
    a |= {"r0w": T(n["L0_ffn_router_w"]), "r0b": all_rows(n["L0_ffn_router_b"]), "e0w": n["L0_ffn_expert_w"]}
    a |= {"r2w": T(n["L2_ffn_router_w"]), "r2b": all_rows(n["L2_ffn_router_b"]), "e2b2": n["L2_ffn_b2"],
          "e2rows": expert_rows(T(n["L2_ffn_w1"]), T(n["L2_ffn_w2"]), n["L2_ffn_b1"])}
    p = "L1_ffn_"
    for x in ("ln1", "ln2"):
        a |= {x + "w": all_rows(n[p + x + "_weight"]), x + "b": all_rows(n[p + x + "_bias"])}
    a |= {"qkvw": T(n[p + "qkv_weight"]), "projw": T(n[p + "proj_weight"]), "r1w": n[p + "router_weight"],
          "e1rows": expert_rows(n[p + "moe_w1"], n[p + "moe_w2"])}
    a["first_slots"] = all_rows((CAPACITY * np.arange(8)).astype(f32))
    a["spare_slots"] = (8 * CAPACITY + np.arange(2 * B * S)).reshape(2, TILES, P).transpose(2, 0, 1).astype(f32)
    a["index"] = all_rows(np.arange(2 * TILES).astype(f32))
    a["lane"] = np.arange(P).astype(f32).reshape(P, 1)
    p = "L2_xattn_"
    a |= {"w2x1": T(n[p + "w1_w"]), "b2x1": columns(n[p + "w1_b"]), "w2x2": T(n[p + "w2_w"]), "b2x2": all_rows(n[p + "w2_b"])}
    for x in "qkv":
        p = f"L3_ffn_{x}_"
        a |= {f"t{x}w1": n[p + "w1"], f"t{x}b1": columns(n[p + "b1"].reshape(-1)), f"t{x}w2": n[p + "w2"], f"t{x}b2": n[p + "b2"]}
    a["tnw"] = np.concatenate([T(n[f"L3_ffn_{x}_node_w"]) for x in "qkv"], 1)
    a["tnb"] = all_rows(np.concatenate([n[f"L3_ffn_{x}_node_b"] for x in "qkv"]))
    a["spread"] = np.kron(np.eye(LEAVES, dtype=f32), np.ones((1, HIDDEN), f32))
    return a


_OUT = (B, S, D)


def build(nc, a, out, stop=99):
    k = Held()
    with ExitStack() as ctx:
        k.X = ctx.enter_context(nc.sbuf_tensor("X", [P, TILES, D], F32))
        norm = ctx.enter_context(nc.sbuf_tensor("norm", [P, 2 * TILES * D], F32))
        k.XN = norm[:, 0:TILES * D].rearrange("p (t d) -> p t d", t=TILES)
        k.XNT = norm[:, TILES * D:].rearrange("p (c n) -> p c n", c=DC)
        k.ATN = norm[:].rearrange("p (g n) -> p g n", g=B * GROUPS)
        k.tg = ctx.enter_context(nc.sbuf_tensor("tg", [P, 8], F32))
        k.stats = ctx.enter_context(nc.sbuf_tensor("stats", [P, TILES, 6], F32))
        k.ident = ctx.enter_context(nc.sbuf_tensor("ident_f32", [P, P], F32))
        k.ident_bf = ctx.enter_context(nc.sbuf_tensor("ident_bf", [P, P], BF16))
        k.qk_dram = nc.dram_tensor("qk_parts", [2, 3, B * GROUPS, GH, HD, S], BF16, kind="Internal").ap()
        k.slot_x = nc.dram_tensor("slot_x", [8 * CAPACITY + 2 * B * S, D], F32, kind="Internal").ap()
        k.slot_y = nc.dram_tensor("slot_y", [FILL_ROWS, D], F32, kind="Internal").ap()
        load_stage(nc, k, a)
        stages = [
            lambda: attention_layer(nc, k, "l0x", a, a["w0q"], a["w0k"], a["w0v"], a["b0q"], a["b0k"], a["b0v"], a["w0o"],
                                    a["b0o"], HD ** -0.5, 0, mask=(a["m0"], a["m0T"], False)),
        ] + more_stages(nc, k, a)
        for n, stage in enumerate(stages):
            if n in range(*(stop if isinstance(stop, tuple) else (0, stop))):
                stage()
        store_stage(nc, k, out)


def store_stage(nc, k, out):
    with Stage(nc, "store") as st:
        stored = st.sem("stored")
        with nc.Block() as block:
            @block.sync
            def _(sp):
                sp.dma_start(out.rearrange("b (t p) d -> p (b t) d", p=P), k.X[:]).then_inc(stored, DMA)
                sp.wait_ge(stored, DMA)


def lay_out(v):
    import numpy as np
    n = {name: np.asarray(x) for name, x in v.items()}
    f32 = np.float32

    def all_rows(x):
        return np.ascontiguousarray(np.broadcast_to(x.reshape(1, -1), (P, x.size)))

    def columns(x):
        return np.ascontiguousarray(x.reshape(-1, P).T)

    def heads(w):
        full = np.zeros((H, HD, H, HD), w.dtype)
        for h in range(H):
            full[h, :, h, :] = w.T
        return full.reshape(D, D)

    def strips(w):
        full = np.zeros((GH, STRIP, GROUPS, w.shape[1]), w.dtype)
        full[:, :HD] = w.reshape(GROUPS, GH, HD, -1).transpose(1, 2, 0, 3)
        return full.reshape(P, GROUPS, -1)

    def T(x):
        return np.ascontiguousarray(np.swapaxes(x, -1, -2))

    selsum = np.zeros((P, GH), f32)
    for i in range(GH):
        selsum[STRIP * i + HD, i] = 1.0
    zero = np.zeros(D, f32)
    m0 = n["mask_SxS2_bk1"]
    m1 = n["mask_Bx1xSxS2_ik1"].reshape(B, S, S)
    a = {
        "x": n["x"].reshape(B * S, D),
        "ctx": n["ctx_1024"].reshape(B * S, D),
        "ctxT": T(n["ctx_1024"].reshape(B * S, D)),
        "gates": all_rows(np.concatenate([n["g_xattn"], n["g_ffn"]])),
        "ident": np.eye(P, dtype=f32),
        "selsum": selsum,
        "tril2": (1.0 + np.triu(np.ones((P, P)))).astype(f32),
        "m0": m0, "m0T": T(m0),
        "m1": m1.reshape(B * S, S), "m1T": T(m1).reshape(B * S, S),
    }
    for layer in (0, 3):
        p = f"L{layer}_xattn_"
        a |= {f"w{layer}q": n[p + "Wq"], f"w{layer}k": n[p + "Wk"], f"w{layer}v": n[p + "Wv"],
              f"b{layer}q": columns(n[p + "bq"]), f"b{layer}k": columns(n[p + "bk"]), f"b{layer}v": all_rows(n[p + "bv"]),
              f"w{layer}o": strips(n[p + "Wo"]), f"b{layer}o": all_rows(n[p + "bo"])}
    p = "L1_xattn_"
    a |= {"w1q": heads(n[p + "Wq"]), "w1k": heads(n[p + "Wk"]), "w1v": heads(n[p + "Wv"]), "zero_col": columns(zero),
          "zero_rows": all_rows(zero), "w1o": strips(T(n[p + "Wo"])), "b1o": all_rows(n[p + "bo"])}
    a |= more_layout(n, all_rows, columns, T)
    return {name: np.ascontiguousarray(x) for name, x in a.items()}


def kernel(**inputs):
    import concourse.bacc as bacc
    from concourse.bass_utils import run_bass_kernel_spmd

    nc = bacc.Bacc("TRN2", target_bir_lowering=False, num_devices=1)
    arrays = lay_out(inputs)
    args = {name: nc.dram_tensor(name, x.shape, mybir.dt.from_np(x.dtype), kind="ExternalInput").ap()
            for name, x in arrays.items()}
    out = nc.dram_tensor("out", _OUT, F32, kind="ExternalOutput").ap()
    build(nc, args, out)
    return run_bass_kernel_spmd(nc, [arrays], core_ids=[0]).results[0]["out"]
```
